# Optimizing a Trainium2 kernel written in Bass

```python
import numpy as np
import jax
import jax.numpy as jnp

def _softmax(x, axis=-1):
    return jax.nn.softmax(x, axis=axis)

def _gelu(x):
    return jax.nn.gelu(x, approximate=True)

def _silu(x):
    return jax.nn.silu(x)

def _sigmoid(x):
    return jax.nn.sigmoid(x)

def _layernorm(x, axis=-1, eps=1e-05):
    m = jnp.mean(x, axis=axis, keepdims=True)
    v = jnp.var(x, axis=axis, keepdims=True)
    return (x - m) / jnp.sqrt(v + eps)

def _scatter_add(tgt, idx, src, axis=0):
    return tgt.at[idx].add(src)

def _segment_sum(src, seg, n):
    return jax.ops.segment_sum(src, seg, n)
kernel_name = 'mk_conv_attn_hybrid_d2_conv_nchw512_r4_2ff3ba'

def setup_inputs(seed: int=0):
    np.random.seed(seed)
    _w = jnp.asarray

    def _rec_inputs():
        import jax
        import jax.numpy as jnp
        _gk = jax.random.key(seed)
        x = 0.0002103 + 1 * jax.random.normal(jax.random.fold_in(_gk, 1), (16, 128, 32, 32), jnp.float32)
        return x
    x = _rec_inputs()

    def _L0_conv_setup():
        import jax, jax.numpy as jnp
        import numpy as np
        SCOPE = 63
        IN_CHANNELS = 128
        SELF_CONNECT = False

        def ricker_filter(width, damp):
            x = jnp.arange(SCOPE, dtype=jnp.float32) - SCOPE // 2
            a = 2.0 / (jnp.sqrt(3.0 * width) * np.pi ** 0.25)
            r = damp * a * (1.0 - (x / width) ** 2) * jnp.exp(-x ** 2 / (2.0 * width ** 2))
            if not SELF_CONNECT:
                r = r.at[SCOPE // 2].set(0.0)
            return r

        def circulant_from_filter(f, n):
            center = SCOPE // 2
            row0 = jnp.zeros(n, dtype=f.dtype).at[(jnp.arange(SCOPE) - center) % n].add(f)
            i = jnp.arange(n)
            return row0[(i[None, :] - i[:, None]) % n]
        key = jax.random.key(seed)
        activations = jax.random.normal(key, (16, IN_CHANNELS, 32, 32), dtype=jnp.float32)
        width = jnp.float32(4.0)
        damp = jnp.float32(0.12)
        return {'activations': activations, 'width': width, 'damp': damp}
    _L0_conv_all = _L0_conv_setup()
    _L0_conv_in = {k: v for k, v in _L0_conv_all.items() if k in ('width', 'damp')}
    del _L0_conv_all

    def _L1_attn_setup():
        import jax, jax.numpy as jnp
        import numpy as np
        D_MODEL, N_HEADS, D_VALUE = (128, 8, 16)
        D_HEAD = D_MODEL // N_HEADS

        def _elu_feature_map(t):
            return jax.nn.elu(t) + 1.0
        key = jax.random.key(seed)
        ks = jax.random.split(key, 5)
        B, T = (2, 512)
        x = jax.random.normal(ks[0], (B, T, D_MODEL), dtype=jnp.float32)
        scale = 0.02
        W_q = jax.random.normal(ks[1], (N_HEADS * D_HEAD, D_MODEL), dtype=jnp.float32) * scale
        W_k = jax.random.normal(ks[2], (N_HEADS * D_HEAD, D_MODEL), dtype=jnp.float32) * scale
        W_v = jax.random.normal(ks[3], (N_HEADS * D_VALUE, D_MODEL), dtype=jnp.float32) * scale
        W_out = jax.random.normal(ks[4], (D_MODEL, N_HEADS * D_VALUE), dtype=jnp.float32) * scale
        return {'x': x, 'W_q': W_q, 'W_k': W_k, 'W_v': W_v, 'W_out': W_out}
    _L1_attn_all = _L1_attn_setup()
    _L1_attn_in = {k: v for k, v in _L1_attn_all.items() if k in ('W_q', 'W_k', 'W_v', 'W_out')}
    del _L1_attn_all

    def _L1_ffn_setup():
        import jax, jax.numpy as jnp
        import numpy as np
        B, S, D, F, E = (8, 1024, 128, 512, 8)
        INIT_LAMBDA = 0.2
        LN_EPS = 1e-05
        LN_MERGE = 0.03
        key = jax.random.key(seed)
        ks = jax.random.split(key, 12)
        n = lambda k, shp, s=1.0: jax.random.normal(k, shp, dtype=jnp.float32) * s
        return {'hidden_states': n(ks[0], (B, S, D)), 'gfc1_w': n(ks[1], (D, D), 0.01), 'gfc1_b': jnp.zeros((D,), jnp.float32), 'gfc2_w': n(ks[2], (E, D), 0.01), 'gfc2_b': jnp.full((E,), INIT_LAMBDA, dtype=jnp.float32), 'W1': n(ks[3], (F, D), 0.02), 'b1': jnp.zeros((F,), jnp.float32), 'W2': n(ks[4], (D, F), 0.02), 'b2': jnp.zeros((D,), jnp.float32), 'ln_g': jnp.ones((D,), jnp.float32), 'ln_b': jnp.zeros((D,), jnp.float32), 'tv_W1': n(ks[5], (E, F, D), 0.02), 'tv_b1': n(ks[6], (E, F), 0.02), 'tv_W2': n(ks[7], (E, D, F), 0.02), 'tv_b2': n(ks[8], (E, D), 0.02), 'tv_ln_g': n(ks[9], (E, D), 0.02), 'tv_ln_b': n(ks[10], (E, D), 0.02)}
    _L1_ffn_all = _L1_ffn_setup()
    _L1_ffn_in = {k: v for k, v in _L1_ffn_all.items() if k in ('gfc1_w', 'gfc1_b', 'gfc2_w', 'gfc2_b', 'W1', 'b1', 'W2', 'b2', 'ln_g', 'ln_b', 'tv_W1', 'tv_b1', 'tv_W2', 'tv_b2', 'tv_ln_g', 'tv_ln_b')}
    del _L1_ffn_all
    return {'x': x, 'L0_conv_width': _L0_conv_in['width'], 'L0_conv_damp': _L0_conv_in['damp'], 'L1_attn_W_q': _L1_attn_in['W_q'], 'L1_attn_W_k': _L1_attn_in['W_k'], 'L1_attn_W_v': _L1_attn_in['W_v'], 'L1_attn_W_out': _L1_attn_in['W_out'], 'L1_ffn_gfc1_w': _L1_ffn_in['gfc1_w'], 'L1_ffn_gfc1_b': _L1_ffn_in['gfc1_b'], 'L1_ffn_gfc2_w': _L1_ffn_in['gfc2_w'], 'L1_ffn_gfc2_b': _L1_ffn_in['gfc2_b'], 'L1_ffn_W1': _L1_ffn_in['W1'], 'L1_ffn_b1': _L1_ffn_in['b1'], 'L1_ffn_W2': _L1_ffn_in['W2'], 'L1_ffn_b2': _L1_ffn_in['b2'], 'L1_ffn_ln_g': _L1_ffn_in['ln_g'], 'L1_ffn_ln_b': _L1_ffn_in['ln_b'], 'L1_ffn_tv_W1': _L1_ffn_in['tv_W1'], 'L1_ffn_tv_b1': _L1_ffn_in['tv_b1'], 'L1_ffn_tv_W2': _L1_ffn_in['tv_W2'], 'L1_ffn_tv_b2': _L1_ffn_in['tv_b2'], 'L1_ffn_tv_ln_g': _L1_ffn_in['tv_ln_g'], 'L1_ffn_tv_ln_b': _L1_ffn_in['tv_ln_b']}

def reference(x, L0_conv_width, L0_conv_damp, L1_attn_W_q, L1_attn_W_k, L1_attn_W_v, L1_attn_W_out, L1_ffn_gfc1_w, L1_ffn_gfc1_b, L1_ffn_gfc2_w, L1_ffn_gfc2_b, L1_ffn_W1, L1_ffn_b1, L1_ffn_W2, L1_ffn_b2, L1_ffn_ln_g, L1_ffn_ln_b, L1_ffn_tv_W1, L1_ffn_tv_b1, L1_ffn_tv_W2, L1_ffn_tv_b2, L1_ffn_tv_ln_g, L1_ffn_tv_ln_b):
    import jax
    import jax.numpy as jnp

    def _L0_conv_ref(activations, width, damp):
        import jax, jax.numpy as jnp
        import numpy as np
        SCOPE = 63
        IN_CHANNELS = 128
        SELF_CONNECT = False

        def ricker_filter(width, damp):
            x = jnp.arange(SCOPE, dtype=jnp.float32) - SCOPE // 2
            a = 2.0 / (jnp.sqrt(3.0 * width) * np.pi ** 0.25)
            r = damp * a * (1.0 - (x / width) ** 2) * jnp.exp(-x ** 2 / (2.0 * width ** 2))
            if not SELF_CONNECT:
                r = r.at[SCOPE // 2].set(0.0)
            return r

        def circulant_from_filter(f, n):
            center = SCOPE // 2
            row0 = jnp.zeros(n, dtype=f.dtype).at[(jnp.arange(SCOPE) - center) % n].add(f)
            i = jnp.arange(n)
            return row0[(i[None, :] - i[:, None]) % n]
        f = ricker_filter(width, damp)
        tpl = circulant_from_filter(f, IN_CHANNELS)
        tpl_inv = jnp.linalg.inv(jnp.eye(IN_CHANNELS, dtype=tpl.dtype) - tpl)
        return jnp.einsum('oc,bchw->bohw', tpl_inv, activations)

    def _L1_attn_ref(x, W_q, W_k, W_v, W_out):
        import jax, jax.numpy as jnp
        import numpy as np
        D_MODEL, N_HEADS, D_VALUE = (128, 8, 16)
        D_HEAD = D_MODEL // N_HEADS

        def _elu_feature_map(t):
            return jax.nn.elu(t) + 1.0
        B, T, D = x.shape
        H, dh, dv = (N_HEADS, D_HEAD, D_VALUE)
        Q = _elu_feature_map((x @ W_q.T).reshape(B, T, H, dh)).transpose(0, 2, 1, 3)
        K = _elu_feature_map((x @ W_k.T).reshape(B, T, H, dh)).transpose(0, 2, 1, 3)
        V = (x @ W_v.T).reshape(B, T, H, dv).transpose(0, 2, 1, 3)
        KV = jnp.einsum('bhti,bhtj->bhtij', K, V)
        S = jnp.cumsum(KV, axis=2)
        z = jnp.cumsum(K, axis=2)
        num = jnp.einsum('bhti,bhtij->bhtj', Q, S)
        den = jnp.maximum(jnp.einsum('bhti,bhti->bht', Q, z), 1e-06)[..., None]
        out = (num / den).transpose(0, 2, 1, 3).reshape(B, T, H * dv)
        return out @ W_out.T

    def _L1_ffn_ref(hidden_states, gfc1_w, gfc1_b, gfc2_w, gfc2_b, W1, b1, W2, b2, ln_g, ln_b, tv_W1, tv_b1, tv_W2, tv_b2, tv_ln_g, tv_ln_b):
        import jax, jax.numpy as jnp
        import numpy as np
        B, S, D, F, E = (8, 1024, 128, 512, 8)
        INIT_LAMBDA = 0.2
        LN_EPS = 1e-05
        LN_MERGE = 0.03
        x = hidden_states
        gh = jax.nn.relu(jnp.einsum('bsd,hd->bsh', x, gfc1_w) + gfc1_b)
        g = (jnp.einsum('bsh,eh->bse', gh, gfc2_w) + gfc2_b).mean(axis=1)
        W1m = W1 + jnp.einsum('be,efd->bfd', g, tv_W1)
        b1m = b1 + g @ tv_b1
        W2m = W2 + jnp.einsum('be,edf->bdf', g, tv_W2)
        b2m = b2 + g @ tv_b2
        lng = ln_g + LN_MERGE * (tv_ln_g - ln_g).sum(axis=0)
        lnb = ln_b + LN_MERGE * (tv_ln_b - ln_b).sum(axis=0)
        h = jax.nn.relu(jnp.einsum('bsd,bfd->bsf', x, W1m) + b1m[:, None, :])
        out = jnp.einsum('bsf,bdf->bsd', h, W2m) + b2m[:, None, :]
        res = x + out
        mu = res.mean(axis=-1, keepdims=True)
        var = res.var(axis=-1, keepdims=True)
        return (res - mu) * jax.lax.rsqrt(var + LN_EPS) * lng + lnb

    def _gn(v, G=32, eps=1e-05):
        B_, C_, H_, W_ = v.shape
        g = v.reshape(B_, G, C_ // G, H_, W_)
        m = jnp.mean(g, axis=(2, 3, 4), keepdims=True)
        s = jnp.var(g, axis=(2, 3, 4), keepdims=True)
        return ((g - m) / jnp.sqrt(s + eps)).reshape(v.shape)

    def _ln_c(v, eps=1e-06):
        m = jnp.mean(v, axis=1, keepdims=True)
        s = jnp.var(v, axis=1, keepdims=True)
        return (v - m) / jnp.sqrt(s + eps)

    def _ln_t(v, eps=1e-05):
        m = jnp.mean(v, axis=-1, keepdims=True)
        s = jnp.var(v, axis=-1, keepdims=True)
        return (v - m) / jnp.sqrt(s + eps)

    def _to_tokens(v):
        B_, C_, H_, W_ = v.shape
        return v.reshape(B_, C_, H_ * W_).transpose(0, 2, 1)

    def _from_tokens(t, like):
        B_, C_, H_, W_ = like.shape
        return t.transpose(0, 2, 1).reshape(B_, C_, H_, W_)
    x = _L0_conv_ref(x, L0_conv_width, L0_conv_damp)
    t = _to_tokens(x)
    t = t + _L1_attn_ref(_ln_t(t), L1_attn_W_q, L1_attn_W_k, L1_attn_W_v, L1_attn_W_out)
    t = t + _L1_ffn_ref(_ln_t(t), L1_ffn_gfc1_w, L1_ffn_gfc1_b, L1_ffn_gfc2_w, L1_ffn_gfc2_b, L1_ffn_W1, L1_ffn_b1, L1_ffn_W2, L1_ffn_b2, L1_ffn_ln_g, L1_ffn_ln_b, L1_ffn_tv_W1, L1_ffn_tv_b1, L1_ffn_tv_W2, L1_ffn_tv_b2, L1_ffn_tv_ln_g, L1_ffn_tv_ln_b)
    x = _from_tokens(t, x)
    return x

_drawn_inputs = setup_inputs


def setup_inputs(seed=0):
    import zlib

    import numpy as np

    out = dict(_drawn_inputs(seed))
    spreads = {'L1_ffn_gfc1_b': (0.0, 0.8),
     'L1_ffn_gfc2_b': (0.20000000298023224, 0.6),
     'L1_ffn_b1': (0.0, 0.528),
     'L1_ffn_b2': (0.0, 0.1),
     'L1_ffn_ln_g': (1.0, 0.2),
     'L1_ffn_ln_b': (0.0, 0.1)}
    factors = {'L1_attn_W_q': 8.0,
     'L1_attn_W_k': 8.0,
     'L1_attn_W_v': 8.0,
     'L1_attn_W_out': 8.0,
     'L1_ffn_gfc1_w': 8.0,
     'L1_ffn_gfc2_w': 8.0,
     'L1_ffn_tv_W1': 2.686,
     'L1_ffn_tv_b1': 8.0,
     'L1_ffn_tv_b2': 8.0,
     'L1_ffn_tv_ln_g': 59.642,
     'L1_ffn_tv_ln_b': 62.715}
    for name, (base, spread) in spreads.items():
        noise = np.random.default_rng([zlib.crc32(name.encode()), seed]).standard_normal(out[name].shape)
        drawn = base * np.exp(spread * noise) if base else spread * noise
        out[name] = jnp.asarray(drawn.astype(out[name].dtype))
    for name, factor in factors.items():
        out[name] = (out[name] * factor).astype(out[name].dtype)
    return out
```

```python
from contextlib import ExitStack

import numpy as np

import concourse.bass as bass
from concourse import mybir

F32 = mybir.dt.float32
F16 = mybir.dt.float16
BF16 = mybir.dt.bfloat16
ALU = mybir.AluOpType
ACT = mybir.ActivationFunctionType
AX = mybir.AxisListType

B, C, T = 16, 128, 1024
P = 128
TILES = T // P
NT = B * TILES
HALF = 4
NHALF = NT // HALF
NH, DH = 8, 16
VW = DH + 1
NP = NH // 2
F, E = 512, 8
FC = F // P
SCOPE = 63
WS = 32.0
WSI = 256.0
VS = 0.125
GB = 8
NG = B // GB
FI = P // E
FO = F // FI
DO = C // FI
EPS = 1e-5
BIG = -1.0e30

TENSOR_ORDER = [("turn_z", 8), ("out_project", 6), ("scores", 4), ("values", 5), ("gate", 8), ("turn", 2),
                ("state", 2), ("turn_out", 5), ("project", 0)]
SCALAR_ORDER = [("split_x", 0), ("copy_qk", 3), ("z_hi", 8), ("scores_hi", 4), ("relu_qk", 1), ("v_hi", 1),
                ("read_conv", 1), ("exp_qk", 1), ("copy_out", 5), ("gate_relu", 8)]
VECTOR_ORDER = [("read_state", 3), ("qk_hi", 2), ("residual", 6), ("stats2", 6), ("z_lo", 8),
                ("normalise", 7), ("denominator", 5), ("invert", 5), ("mean_var2", 6), ("divide", 5),
                ("v_lo", 1), ("scores_lo", 4), ("stats1", 0), ("make_qk", 1), ("mean_var1", 0)]
GPSIMD_ORDER = [("eps1", 1), ("rsqrt2", 7), ("state_lo", 4), ("rsqrt1", 1), ("qk_lo", 2), ("split_x", 0),
                ("state_hi", 3), ("eps2", 6)]


def before(stage, other):
    names = [name for name, _ in TENSOR_ORDER]
    skew = dict(TENSOR_ORDER)
    return skew[other] - skew[stage] + (0 if names.index(other) < names.index(stage) else 1)


_COLS = [("cas", P), ("ident", P), ("maskneg", P), ("blk", 2 * VW), ("delta", FI), ("delta2", FI),
         ("onehot", B), ("pos", 1), ("fmask", 1), ("nodc", 1), ("lncoef", P), ("mhalf", HALF), ("eps", 2)]
COL = {}
_at = 0
for _name, _n in _COLS:
    COL[_name] = (_at, _at + _n)
    _at += _n
NCONST = _at


def shape_constants():
    k = np.zeros((P, NCONST), np.float32)

    def put(name, a):
        k[:a.shape[0], COL[name][0]:COL[name][1]] = a

    j = np.arange(P)
    ang = 2 * np.pi * ((j[:, None] * j[None, :]) % P) / P
    put("cas", np.cos(ang) + np.sin(ang))
    put("ident", np.eye(P))
    put("maskneg", np.where(j[:, None] > j[None, :], BIG, 0.0))
    put("blk", (j[:, None] // 64 == np.arange(2 * VW)[None, :] // VW).astype(np.float32))
    put("delta", (j[:, None] % FI == np.arange(FI)[None, :]).astype(np.float32))
    d2 = np.zeros((P, FI), np.float32)
    d2[:FI] = np.eye(FI)
    d2[32:32 + FI] = np.eye(FI)
    put("delta2", d2)
    oh = np.zeros((P, B), np.float32)
    oh[:B] = np.eye(B)
    oh[32:32 + B] = np.eye(B)
    put("onehot", oh)
    pos = np.where(j <= P // 2, j, j - P).astype(np.float32)
    put("pos", pos[:, None])
    put("fmask", ((np.abs(pos) <= SCOPE // 2) & (pos != 0)).astype(np.float32)[:, None])
    put("nodc", (j != 0).astype(np.float32)[:, None])
    merge = 0.03
    co = np.zeros((P, P), np.float32)
    co[:E] = merge
    co[E] = 1 - E * merge
    put("lncoef", co)
    put("mhalf", np.full((P, HALF), -0.5))
    put("eps", np.full((P, 2), [EPS * WSI * WSI, EPS]))
    return k


def build(nc, d):
    top = ExitStack()
    with top:
        def sb(ctx, name, shape, dt=F32):
            return ctx.enter_context(nc.sbuf_tensor(name, shape, dt))

        def sem(name):
            return top.enter_context(nc.semaphore(name))

        kc = sb(top, "consts", [P, NCONST])
        identb = sb(top, "ident_bf16", [P, P], BF16)
        identh = sb(top, "ident_f16", [P, P], F16)
        ident_ws = sb(top, "ident_f16_scaled", [P, P], F16)
        maskb = sb(top, "mask_bf16", [P, P], BF16)
        onehoth = sb(top, "onehot_f16", [64, B], F16)
        delta2h = sb(top, "delta2_f16", [64, GB, FI], F16)
        wh = sb(top, "w_in_hi", [P, 4 * C], F16)
        wl = sb(top, "w_in_lo", [P, 4 * C], F16)
        woT = sb(top, "w_outT", [P, C])
        gfh = sb(top, "gate1_hi", [P, C], F16)
        gfl = sb(top, "gate1_lo", [P, C], F16)
        gf1b = sb(top, "gate1_b", [P, 1])
        gf2T = sb(top, "gate2T", [P, E])
        gf2rep = sb(top, "gate2T_rep", [P, E, FI])
        gf2b = sb(top, "gate2_b", [E, 1])
        gf2brep = sb(top, "gate2_b_rep", [P, 1])
        t9b1 = sb(top, "tv_b1_and_b1", [E + 1, F])
        t9b2 = sb(top, "tv_b2_and_b2", [E + 1, C])
        lng = sb(top, "ln_gain_rows", [P, C])
        lnb = sb(top, "ln_bias_col", [P, 1])
        tv1 = [sb(top, f"tv_W1_{s}", [P, FO * C], F16) for s in ("hi", "lo")]
        tv2 = [sb(top, f"tv_W2_{s}", [P, DO * F], F16) for s in ("hi", "lo")]
        w1s = sb(top, "W1_hi_lo_rows", [64, FO * C], F16)
        w2s = sb(top, "W2_hi_lo_rows", [64, DO * F], F16)
        zh = sb(top, "zT_hi", [P, NT * P], F16)
        zl = sb(top, "zT_lo", [P, NT * P], F16)
        ghs = sb(top, "gate_hidden_sums", [P, NT])

        cas = kc[:, COL["cas"][0]:COL["cas"][1]]
        ident = kc[:, COL["ident"][0]:COL["ident"][1]]

        def kcol(name, rows=P):
            return kc[0:rows, COL[name][0]:COL[name][1]]

        s_const = sem("const_loaded")
        s_scal = sem("scalars_loaded")
        s_wts = sem("square_weights_loaded")
        s_small = sem("small_weights_loaded")
        s_tvl = [sem(f"tv_staged_{i}") for i in range(4)]
        s_tvf = sem("tv_stage_freed")
        s_dch = sem("setup_vector_chain")
        s_ach = sem("setup_scalar_chain")
        s_pch = sem("setup_tensor_chain")
        s_gch = sem("setup_gpsimd_chain")
        with ExitStack() as su:
            wid = sb(su, "width", [P, 1])
            dmp = sb(su, "damp", [P, 1])
            wsq = sb(su, "square_weights", [P, 5, C])
            wsqT = sb(su, "square_weights_T", [P, 5, C])
            g2n = sb(su, "gate2_rows", [E, C])
            l9g = sb(su, "ln_g_rows", [E + 1, C])
            l9b = sb(su, "ln_b_rows", [E + 1, C])
            v = sb(su, "filter_steps", [P, 16])
            casd = sb(su, "cas_scaled", [P, 2, C])
            wbig = sb(su, "w_in", [P, 4 * C])
            cw = sb(su, "centred_inverse", [P, C])
            stage = sb(su, "tv_stage", [P, 2, 4096])
            pa = su.enter_context(nc.psum_tensor("setup_psum", [P, 8, 512], F32))

            SQ = ["L1_attn_W_q", "L1_attn_W_k", "L1_attn_W_v", "L1_attn_W_out", "L1_ffn_gfc1_w"]
            tvsrc = [d["L1_ffn_tv_W1"].rearrange("e (i o) d -> (e i) (o d)", i=FI),
                     d["L1_ffn_tv_W2"].rearrange("e (i o) f -> (e i) (o f)", i=FI),
                     d["L1_ffn_W1"].rearrange("(i o) d -> i (o d)", i=FI),
                     d["L1_ffn_W2"].rearrange("(i o) f -> i (o f)", i=FI)]
            tvrows = [P, P, FI, FI]
            with nc.Block() as block:
                @block.sync
                def _(sp):
                    sp.dma_start(kc[:, :], d["consts"]).then_inc(s_const, 16)
                    sp.dma_start(wid[:, :], d["L0_conv_width"].partition_broadcast(P)).then_inc(s_scal, 16)
                    sp.dma_start(dmp[:, :], d["L0_conv_damp"].partition_broadcast(P)).then_inc(s_scal, 16)
                    for i, name in enumerate(SQ):
                        sp.dma_start(wsq[:, i, :], d[name]).then_inc(s_wts, 16)
                    sp.dma_start(g2n[:, :], d["L1_ffn_gfc2_w"]).then_inc(s_small, 16)
                    for dst, tv, base in ((l9g, "tv_ln_g", "ln_g"), (l9b, "tv_ln_b", "ln_b"),
                                          (t9b1, "tv_b1", "b1"), (t9b2, "tv_b2", "b2")):
                        sp.dma_start(dst[0:E, :], d["L1_ffn_" + tv]).then_inc(s_small, 16)
                        sp.dma_start(dst[E:E + 1, :], d["L1_ffn_" + base].unsqueeze(0)).then_inc(s_small, 16)
                    sp.dma_start(gf1b[:, :], d["L1_ffn_gfc1_b"].unsqueeze(1)).then_inc(s_small, 16)
                    sp.dma_start(gf2b[:, :], d["L1_ffn_gfc2_b"].unsqueeze(1)).then_inc(s_small, 16)
                    for e in range(E):
                        sp.dma_start(gf2brep[e * FI:(e + 1) * FI, :],
                                     d["L1_ffn_gfc2_b"][e:e + 1].partition_broadcast(FI)).then_inc(s_small, 16)
                    for i in range(4):
                        if i >= 2:
                            sp.wait_ge(s_tvf, i - 1)
                        sp.dma_start(stage[0:tvrows[i], i % 2, :], tvsrc[i]).then_inc(s_tvl[i], 16)
                NSMALL = 16 * (1 + 8 + 2 + E)

                @block.vector
                def _(dve):
                    n = [0]

                    def link(ins):
                        n[0] += 1
                        ins.then_inc(s_dch, 1)
                        dve.wait_ge(s_dch, n[0])

                    dve.wait_ge(s_const, 16)
                    dve.wait_ge(s_scal, 32)
                    pos, fmask, nodc = kcol("pos"), kcol("fmask"), kcol("nodc")
                    link(nc.vector.reciprocal(v[:, 0:1], wid[:, :]))
                    link(nc.vector.tensor_tensor(v[:, 1:2], pos, v[:, 0:1], ALU.mult))
                    link(nc.vector.tensor_tensor(v[:, 2:3], v[:, 1:2], v[:, 1:2], ALU.mult))
                    link(nc.vector.tensor_scalar(v[:, 3:4], v[:, 2:3], -1.0, 1.0, ALU.mult, ALU.add))
                    link(nc.vector.tensor_scalar(v[:, 14:15], wid[:, :], 3.0, None, ALU.mult))
                    dve.wait_ge(s_gch, 2)
                    link(nc.vector.tensor_scalar(v[:, 5:6], v[:, 4:5], float(2.0 / np.pi ** 0.25), dmp[:, 0:1],
                                                 ALU.mult, ALU.mult))
                    link(nc.vector.tensor_tensor(v[:, 6:7], v[:, 5:6], v[:, 3:4], ALU.mult))
                    link(nc.vector.tensor_tensor(v[:, 7:8], v[:, 6:7], fmask, ALU.mult))
                    dve.wait_ge(s_ach, 1)
                    link(nc.vector.tensor_tensor(v[:, 8:9], v[:, 7:8], v[:, 9:10], ALU.mult))
                    nc.vector.tensor_copy(identb[:, :], ident)
                    nc.vector.tensor_copy(identh[:, :], ident)
                    nc.vector.tensor_scalar(ident_ws[:, :], ident, WS, None, ALU.mult)
                    nc.vector.tensor_copy(maskb[:, :], kcol("maskneg"))
                    nc.vector.tensor_copy(onehoth[:, :], kcol("onehot", 64))
                    nc.vector.tensor_copy(delta2h[:, :, :],
                                          kcol("delta2", 64).unsqueeze(1).broadcast_to([64, GB, FI]))
                    dve.wait_ge(s_pch, 1)
                    link(nc.vector.tensor_scalar(v[:, 10:11], pa[:, 0, 0:1], -1.0, 1.0, ALU.mult, ALU.add))
                    link(nc.vector.reciprocal(v[:, 11:12], v[:, 10:11]))
                    link(nc.vector.tensor_scalar(v[:, 12:13], v[:, 11:12], 1.0 / P, None, ALU.mult))
                    link(nc.vector.tensor_tensor(v[:, 13:14], v[:, 12:13], nodc, ALU.mult))
                    link(nc.vector.tensor_scalar(casd[:, 0, :], cas, v[:, 12:13], None, ALU.mult))
                    link(nc.vector.tensor_scalar(casd[:, 1, :], cas, v[:, 13:14], None, ALU.mult))
                    dve.wait_ge(s_pch, 2)
                    nc.vector.tensor_copy(cw[:, :], pa[:, 1, 128:256])
                    nc.vector.tensor_scalar(wbig[:, 0:C], pa[:, 1, 0:128], WSI, None, ALU.mult)
                    link(nc.vector.tensor_copy(wsqT[:, 0:4, :], pa[:, 2, :].rearrange("p (a c) -> p a c", a=4)))
                    link(nc.vector.tensor_scalar(wsqT[:, 4, :], pa[:, 3, 0:128], WS, None, ALU.mult))
                    link(nc.vector.tensor_copy(woT[:, :], wsqT[:, 3, :]))
                    link(nc.vector.tensor_copy(gf2T[:, :], pa[:, 3, 128:128 + E]))
                    link(nc.vector.tensor_copy(gf2rep[:, :, :],
                                               gf2T[:, :].unsqueeze(2).broadcast_to([P, E, FI])))
                    link(nc.vector.tensor_copy(gfh[:, :], wsqT[:, 4, :]))
                    link(nc.vector.tensor_tensor(gfl[:, :], wsqT[:, 4, :], gfh[:, :], ALU.subtract))
                    dve.wait_ge(s_pch, 3)
                    nc.vector.tensor_scalar(wbig[:, C:3 * C], pa[:, 4, 0:2 * C], WSI, None, ALU.mult)
                    link(nc.vector.tensor_scalar(wbig[:, 3 * C:4 * C], pa[:, 4, 2 * C:3 * C], WSI * VS, None, ALU.mult))
                    link(nc.vector.tensor_copy(wh[:, :], wbig[:, :]))
                    link(nc.vector.tensor_tensor(wl[:, :], wbig[:, :], wh[:, :], ALU.subtract))
                    dve.wait_ge(s_pch, 4)
                    nc.vector.tensor_copy(lng[:, :], pa[:, 5, 0:C])
                    nc.vector.tensor_copy(lnb[:, :], pa[:, 5, C:C + 1])
                    dve.wait_ge(s_gch, 1)
                    los = [tv1[1], tv2[1]]
                    his = [tv1[0], tv2[0]]
                    for i in range(4):
                        dve.wait_ge(s_ach, i + 2)
                        if i < 2:
                            lo, hi, src = los[i][:, :], his[i][:, :], stage[:, i % 2, :]
                        else:
                            w = (w1s, w2s)[i - 2]
                            lo, hi, src = w[32:32 + FI, :], w[0:FI, :], stage[0:FI, i % 2, :]
                        nc.vector.scalar_tensor_tensor(lo, src, WS, hi, ALU.mult, ALU.subtract).then_inc(s_tvf, 1)

                @block.gpsimd
                def _(pool):
                    nc.gpsimd.memset(w1s[:, :], 0.0)
                    nc.gpsimd.memset(w2s[:, :], 0.0).then_inc(s_gch, 1)
                    pool.wait_ge(s_dch, 5)
                    nc.gpsimd.tensor_tensor(v[:, 4:5], v[:, 14:15], kc[:, COL["mhalf"][0]:COL["mhalf"][0] + 1], ALU.pow)\
                        .then_inc(s_gch, 1)

                @block.scalar
                def _(act):
                    act.wait_ge(s_dch, 3)
                    nc.scalar.activation(v[:, 9:10], v[:, 2:3], ACT.Exp, scale=-0.5).then_inc(s_ach, 1)
                    act.wait_ge(s_gch, 1)
                    for i in range(4):
                        act.wait_ge(s_tvl[i], 16)
                        hi = (tv1[0][:, :], tv2[0][:, :], w1s[0:FI, :], w2s[0:FI, :])[i]
                        nc.scalar.activation(hi, stage[0:tvrows[i], i % 2, :], ACT.Copy, scale=WS).then_inc(s_ach, 1)

                @block.tensor
                def _(pe):
                    mm = nc.tensor.matmul
                    pe.wait_ge(s_dch, 9)
                    mm(pa[:, 0, 0:1], cas, v[:, 8:9], start=True, stop=True).then_inc(s_pch, 1)
                    pe.wait_ge(s_wts, 16 * 5)
                    pe.wait_ge(s_small, NSMALL)
                    for i in range(5):
                        nc.tensor.transpose(pa[:, 2 + i // 4, (i % 4) * 128:(i % 4) * 128 + 128], wsq[:, i, :], ident)
                    nc.tensor.transpose(pa[:, 3, 128:128 + E], g2n[:, :], kc[0:E, COL["ident"][0]:COL["ident"][0] + E])
                    pe.wait_ge(s_dch, 15)
                    mm(pa[:, 1, 0:128], casd[:, 0, :], cas, start=True, stop=True)
                    mm(pa[:, 1, 128:256], casd[:, 1, :], cas, start=True, stop=True).then_inc(s_pch, 1)
                    pe.wait_ge(s_dch, 16)
                    mm(pa[:, 4, 0:3 * C], cw[:, :], wsqT[:, 0:3, :].rearrange("p a c -> p (a c)"),
                       start=True, stop=True).then_inc(s_pch, 1)
                    mm(pa[:, 5, 0:C], kcol("lncoef", E + 1), l9g[:, :], start=True, stop=True)
                    mm(pa[:, 5, C:C + 1], l9b[:, :], kc[0:E + 1, COL["lncoef"][0]:COL["lncoef"][0] + 1],
                       start=True, stop=True).then_inc(s_pch, 1)

        with ExitStack() as pa_:
            xf = sb(pa_, "x_f32", [P, 2, HALF * P])
            xh = sb(pa_, "x_hi", [P, 2, HALF * P], F16)
            xl = sb(pa_, "x_lo", [P, 2, HALF * P], F16)
            yt = sb(pa_, "y_then_t1", [P, TILES, C])
            eq = sb(pa_, "exp_qk", [P, 4, 2 * C])
            rq = sb(pa_, "relu_qk", [P, 4, 2 * C])
            qk = sb(pa_, "qk_f32", [P, 4, 2 * C])
            pk = sb(pa_, "qk_parts", [P, 4, 2, NH, 4 * DH], F16)
            vp = sb(pa_, "v_parts", [P, 8, NH, 2 * DH + 1], F16)
            qkT = sb(pa_, "qkT_parts", [P, 4, 2, NP, P], F16)
            ah = sb(pa_, "scores_hi", [P, 2, NH * P], F16)
            al = sb(pa_, "scores_lo", [P, 2, NH * P], F16)
            sm = sb(pa_, "state_f32", [P, 2, NP, 2 * VW])
            sone = sb(pa_, "state_ones", [P, NP, 2 * VW])
            sp2 = sb(pa_, "state_parts", [P, 4, 2, NP, 2 * VW], F16)
            o_ = sb(pa_, "attn_out", [P, 2, C])
            oT = sb(pa_, "attn_outT", [P, 2, C])
            z_ = sb(pa_, "z", [P, 2, C])
            st = sb(pa_, "stats1", [P, 4, 16])
            st2 = sb(pa_, "stats2", [P, 4, 16])
            dn = sb(pa_, "denominators", [P, 2, 2, NH])
            gjunk = sb(pa_, "gate_hidden", [P, P])

            p_in = pa_.enter_context(nc.psum_tensor("p_in", [P, 512], F32))
            p_m1 = pa_.enter_context(nc.psum_tensor("p_m1", [P, 512], F32))
            p_tr = pa_.enter_context(nc.psum_tensor("p_tr", [P, 2, NP, P], F16))
            p_a = pa_.enter_context(nc.psum_tensor("p_a", [P, NH * P], F32))
            p_o = pa_.enter_context(nc.psum_tensor("p_o", [P, 512], F32))
            p_s = pa_.enter_context(nc.psum_tensor("p_s", [P, 512], F32))
            p_m2 = pa_.enter_context(nc.psum_tensor("p_m2", [P, 512], F32))
            num = p_o[:, 0:NH * VW].rearrange("p (h w) -> p h w", w=VW)
            sbank = p_s[:, 0:NP * 2 * VW].rearrange("p (a w) -> p a w", w=2 * VW)

            x_loaded = [sem(f"x_loaded_{i}") for i in range(2)]
            t1_stored = [sem(f"t1_stored_{i}") for i in range(TILES // 2)]
            (xh_ready, xl_ready, in_done, bn1, mv1, ve1, rstd1, y_ready, vhi_ready, exp_ready, relu_ready, vlo_ready,
             qk_ready, hi_ready, lo_ready, tr_done, qkT_ready, su_done, sm_ready, sh_ready, sp_ready,
             sc_done, ahi_ready, alo_ready, av_done, den1, den2, o_ready, ot_done, oT_ready, wo_done,
             t1_ready, bn2, mv2, ve2, rstd2, z_ready, zt_done, zhi_ready, zlo_ready, gt_done, gate_ready) = [
                sem(s) for s in (
                    "xh_ready xl_ready in_done bn1 mv1 ve1 rstd1 y_ready vhi_ready exp_ready relu_ready vlo_ready "
                    "qk_ready hi_ready lo_ready tr_done qkT_ready su_done sm_ready sh_ready sp_ready "
                    "sc_done ahi_ready alo_ready av_done den1 den2 o_ready ot_done oT_ready wo_done "
                    "t1_ready bn2 mv2 ve2 rstd2 z_ready zt_done zhi_ready zlo_ready gt_done gate_ready").split()]
            ones_set = sem("ones_set")

            def at_least(eng, s, value):
                if not isinstance(value, int) or value > 0:
                    eng.wait_ge(s, value)

            def batch(stages, b, old=True, new=True):
                for slot in range(TILES):
                    for k, stage_ in stages:
                        t = slot - k
                        if t >= 0 and new:
                            stage_(b, t)
                        elif t < 0 and old:
                            stage_(b - 1, t + TILES)

            def run(eng, order, stages):
                stages = [(skew, stages[name]) for name, skew in order]
                batch(stages, 0, old=False)
                with eng.Fori(1, B) as b:
                    batch(stages, b)
                batch(stages, B, new=False)

            def cap(n):
                return min(n, NT) if isinstance(n, int) else n

            with nc.Block() as block:
                @block.sync
                def _(sp):
                    def load(b, hf):
                        q = 2 * b + hf
                        at_least(sp, xh_ready, q - 1)
                        at_least(sp, xl_ready, q - 1)
                        sp.dma_start(xf[:, hf, :], d["x"][bass.ds(b * P, P), hf * HALF * P:(hf + 1) * HALF * P])\
                            .then_inc(x_loaded[hf], 16)

                    def store(b, pair):
                        hf, i = pair // 2, pair % 2
                        sp.wait_ge(t1_ready, TILES * b + 2 * (pair + 1))
                        sp.dma_start(d["t1"][bass.ds((2 * b + hf) * P, P), 2 * C * i:2 * C * (i + 1)],
                                     yt[:, 2 * pair:2 * pair + 2, :].rearrange("p a c -> p (a c)"))\
                            .then_inc(t1_stored[pair], 16)

                    load(0, 0)
                    load(0, 1)
                    with sp.Fori(1, B) as b:
                        load(b, 0)
                        store(b - 1, 0)
                        store(b - 1, 1)
                        load(b, 1)
                        store(b - 1, 2)
                        store(b - 1, 3)
                    for pair in range(TILES // 2):
                        store(B - 1, pair)
                    for pair in range(TILES // 2):
                        sp.wait_ge(t1_stored[pair], 16 * B)

                @block.tensor
                def _(pe):
                    mm = nc.tensor.matmul

                    def project(b, t):
                        n = TILES * b + t
                        hf, j = t // HALF, t % HALF
                        if j == 0:
                            pe.wait_ge(xh_ready, 2 * b + hf + 1)
                            pe.wait_ge(xl_ready, 2 * b + hf + 1)
                        at_least(pe, exp_ready, n)
                        at_least(pe, relu_ready, n)
                        at_least(pe, vlo_ready, n)
                        cols = slice(j * P, (j + 1) * P)
                        mm(p_in[:, :], xh[:, hf, cols], wh[:, :], start=True, stop=False)
                        mm(p_in[:, :], xh[:, hf, cols], wl[:, :], start=False, stop=False)
                        mm(p_in[:, :], xl[:, hf, cols], wh[:, :], start=False, stop=True).then_inc(in_done, 1)

                    def state(b, t):
                        if t == TILES - 1:
                            return
                        n = TILES * b + t
                        pe.wait_ge(lo_ready, n + 1)
                        pe.wait_ge(hi_ready, n + 1)
                        pe.wait_ge(vlo_ready, n + 1)
                        pe.wait_ge(vhi_ready, n + 1)
                        if n == 0 if isinstance(n, int) else False:
                            pe.wait_ge(ones_set, 1)
                        at_least(pe, sm_ready, (TILES - 1) * b + t)
                        for a in range(NP):
                            kk = pk[:, t % 4, 1, 2 * a:2 * a + 2, :].rearrange("p h c -> p (h c)")
                            mm(sbank[:, a, :], kk, vp[:, t, 2 * a:2 * a + 2, 0:VW],
                               start=(t == 0 and a == 0), stop=False, skip_group_check=True)
                            last = mm(sbank[:, a, :].rearrange("p (h w) -> p h w", w=VW)[:, :, 0:DH], kk,
                                      vp[:, t, 2 * a:2 * a + 2, VW:VW + DH],
                                      start=False, stop=True, skip_group_check=True)
                        last.then_inc(su_done, 1)

                    def turn(b, t):
                        n = TILES * b + t
                        pe.wait_ge(lo_ready, n + 1)
                        pe.wait_ge(hi_ready, n + 1)
                        at_least(pe, qkT_ready, n)
                        for w in range(2):
                            for a in range(NP):
                                last = nc.tensor.transpose(
                                    p_tr[:, w, a, :], pk[:, t % 4, w, 2 * a:2 * a + 2, :].rearrange("p h c -> p (h c)"),
                                    identh[:, :])
                        last.then_inc(tr_done, 1)

                    def scores(b, t):
                        n = TILES * b + t
                        pe.wait_ge(qkT_ready, n + 1)
                        at_least(pe, ahi_ready, n)
                        at_least(pe, alo_ready, n)
                        for eo in range(2):
                            mm(p_a[:, eo * 512:(eo + 1) * 512], identb[:, :],
                               maskb[:, :].unsqueeze(1).broadcast_to([P, NP, P]),
                               start=True, stop=False, skip_group_check=True)
                        for h in range(NH):
                            a, eo = h // 2, h % 2
                            r = 64 * eo
                            last = mm(p_a[:, eo * 512 + a * P:eo * 512 + (a + 1) * P],
                                      qkT[r:r + 64, t % 4, 1, a, :], qkT[r:r + 64, t % 4, 0, a, :],
                                      start=False, stop=True, skip_group_check=True)
                        last.then_inc(sc_done, 1)

                    def values(b, t):
                        n = TILES * b + t
                        pe.wait_ge(ahi_ready, n + 1)
                        pe.wait_ge(alo_ready, n + 1)
                        at_least(pe, o_ready, n)
                        if t:
                            pe.wait_ge(sp_ready, (TILES - 1) * b + t)
                        for h in range(NH):
                            c0 = (h % 2) * 512 + (h // 2) * P
                            hi, lo = ah[:, t % 2, c0:c0 + P], al[:, t % 2, c0:c0 + P]
                            mm(num[:, h, :], hi, vp[:, t, h, 0:VW], start=(h == 0), stop=False,
                               skip_group_check=True)
                            mm(num[:, h, 0:DH], hi, vp[:, t, h, VW:VW + DH], start=False, stop=False,
                               skip_group_check=True)
                            last = mm(num[:, h, :], lo, vp[:, t, h, 0:VW], start=False, stop=True,
                                      skip_group_check=True)
                        if t:
                            for a in range(NP):
                                for part in range(2):
                                    last = mm(p_o[:, 2 * VW * a:2 * VW * (a + 1)], qkT[:, t % 4, 0, a, :],
                                              sp2[:, (t - 1) % 4, part, a, :], start=False, stop=True,
                                              skip_group_check=True)
                        last.then_inc(av_done, 1)

                    def other_read(n, own, other, lag):
                        for s_ in other:
                            at_least(pe, s_, cap(n - lag + 1))
                        if isinstance(n, int) and (n - lag < 0 or n - lag >= NT):
                            for s_ in own:
                                at_least(pe, s_, n)

                    def turn_out(b, t):
                        n = TILES * b + t
                        pe.wait_ge(o_ready, n + 1)
                        other_read(n, (oT_ready,), (zhi_ready, zlo_ready), before("turn_out", "turn_z"))
                        nc.tensor.transpose(p_m2[:, 0:P], o_[:, t % 2, :], ident).then_inc(ot_done, 1)

                    def out_project(b, t):
                        n = TILES * b + t
                        pe.wait_ge(oT_ready, n + 1)
                        other_read(n, (t1_ready,), (gate_ready,), before("out_project", "gate"))
                        mm(p_m1[:, 0:P], oT[:, t % 2, :], woT[:, :], start=True, stop=True).then_inc(wo_done, 1)

                    def turn_z(b, t):
                        n = TILES * b + t
                        pe.wait_ge(z_ready, n + 1)
                        other_read(n, (zhi_ready, zlo_ready), (oT_ready,), before("turn_z", "turn_out"))
                        nc.tensor.transpose(p_m2[:, P:2 * P], z_[:, t % 2, :], ident).then_inc(zt_done, 1)

                    def gate(b, t):
                        n = TILES * b + t
                        pe.wait_ge(zhi_ready, n + 1)
                        pe.wait_ge(zlo_ready, n + 1)
                        other_read(n, (gate_ready,), (t1_ready,), before("gate", "out_project"))
                        g = p_m1[:, P:2 * P]
                        hi, lo = zh[:, bass.ds(n * P, P)], zl[:, bass.ds(n * P, P)]
                        mm(g, gfh[:, :], hi, start=True, stop=False)
                        mm(g, gfl[:, :], hi, start=False, stop=False)
                        mm(g, gfh[:, :], lo, start=False, stop=True).then_inc(gt_done, 1)

                    pe.wait_ge(ones_set, 1)
                    run(pe, TENSOR_ORDER, {"project": project, "state": state, "turn": turn, "scores": scores,
                        "values": values, "turn_out": turn_out, "out_project": out_project, "turn_z": turn_z,
                        "gate": gate})

                @block.scalar
                def _(act):
                    def split_x(b, t):
                        if t % HALF:
                            return
                        hf = t // HALF
                        q = 2 * b + hf
                        act.wait_ge(x_loaded[hf], 16 * (b + 1))
                        at_least(act, in_done, HALF * (q - 1))
                        nc.scalar.activation(xh[:, hf, :], xf[:, hf, :], ACT.Copy).then_inc(xh_ready, 1)

                    def read_conv(b, t):
                        n = TILES * b + t
                        act.wait_ge(bn1, n + 1)
                        if t % 2 == 0:
                            at_least(act, t1_stored[t // 2], 16 * b)
                        at_least(act, z_ready, n - TILES + 2)
                        nc.scalar.activation(yt[:, t, :], p_in[:, 0:C], ACT.Copy, scale=1.0 / WSI).then_inc(y_ready, 1)

                    def v_hi(b, t):
                        n = TILES * b + t
                        act.wait_ge(rstd1, n + 1)
                        at_least(act, av_done, n - TILES + 2)
                        nc.scalar.activation(vp[:, t, :, 0:DH],
                                             p_in[:, 3 * C:4 * C].rearrange("p (h i) -> p h i", i=DH),
                                             ACT.Copy, scale=st[:, t % 4, 8:9]).then_inc(vhi_ready, 1)

                    def exp_qk(b, t):
                        n = TILES * b + t
                        act.wait_ge(rstd1, n + 1)
                        at_least(act, qk_ready, n - 3)
                        nc.scalar.activation(eq[:, t % 4, :], p_in[:, C:3 * C], ACT.Exp, scale=st[:, t % 4, 8:9])\
                            .then_inc(exp_ready, 1)

                    def relu_qk(b, t):
                        n = TILES * b + t
                        act.wait_ge(rstd1, n + 1)
                        at_least(act, qk_ready, n - 3)
                        nc.scalar.activation(rq[:, t % 4, :], p_in[:, C:3 * C], ACT.Relu, scale=st[:, t % 4, 8:9])\
                            .then_inc(relu_ready, 1)

                    def copy_out(b, t):
                        n = TILES * b + t
                        act.wait_ge(ot_done, n + 1)
                        at_least(act, wo_done, n - 1)
                        nc.scalar.activation(oT[:, t % 2, :], p_m2[:, 0:P], ACT.Copy).then_inc(oT_ready, 1)

                    def copy_qk(b, t):
                        n = TILES * b + t
                        act.wait_ge(tr_done, n + 1)
                        at_least(act, av_done, n - 3)
                        nc.scalar.activation(qkT[:, t % 4, :, :, :].rearrange("p w a c -> p (w a c)"),
                                             p_tr[:, :, :, :].rearrange("p w a c -> p (w a c)"), ACT.Copy)\
                            .then_inc(qkT_ready, 1)

                    def scores_hi(b, t):
                        n = TILES * b + t
                        act.wait_ge(sc_done, n + 1)
                        at_least(act, av_done, n - 1)
                        nc.scalar.activation(ah[:, t % 2, :], p_a[:, :], ACT.Relu).then_inc(ahi_ready, 1)

                    def z_hi(b, t):
                        n = TILES * b + t
                        act.wait_ge(ones_set, 1)
                        act.wait_ge(zt_done, n + 1)
                        nc.scalar.activation(zh[:, bass.ds(n * P, P)], p_m2[:, P:2 * P], ACT.Copy).then_inc(zhi_ready, 1)

                    def gate_relu(b, t):
                        n = TILES * b + t
                        act.wait_ge(ones_set, 1)
                        act.wait_ge(gt_done, n + 1)
                        nc.scalar.activation(gjunk[:, :], p_m1[:, P:2 * P], ACT.Relu, bias=gf1b[:, 0:1], scale=1.0 / WS,
                                             accum_out=ghs[:, bass.ds(n, 1)]).then_inc(gate_ready, 1)

                    run(act, SCALAR_ORDER, {"split_x": split_x, "read_conv": read_conv, "v_hi": v_hi,
                        "exp_qk": exp_qk, "relu_qk": relu_qk, "copy_qk": copy_qk, "scores_hi": scores_hi,
                        "copy_out": copy_out, "z_hi": z_hi, "gate_relu": gate_relu})

                @block.vector
                def _(dve):
                    def stats1(b, t):
                        n = TILES * b + t
                        dve.wait_ge(in_done, n + 1)
                        nc.vector.bn_stats(st[:, t % 4, 0:6], p_in[:, 0:C]).then_inc(bn1, 1)

                    def mean_var1(b, t):
                        n = TILES * b + t
                        dve.wait_ge(ones_set, 1)
                        dve.wait_ge(bn1, n + 1)
                        nc.vector.bn_aggr(st[:, t % 4, 6:8], st[:, t % 4, 0:6]).then_inc(mv1, 1)

                    def v_lo(b, t):
                        n = TILES * b + t
                        dve.wait_ge(vhi_ready, n + 1)
                        dve.wait_ge(exp_ready, n + 1)
                        dve.wait_ge(relu_ready, n + 1)
                        nc.vector.scalar_tensor_tensor(
                            vp[:, t, :, VW:VW + DH], p_in[:, 3 * C:4 * C].rearrange("p (h i) -> p h i", i=DH),
                            st[:, t % 4, 8:9], vp[:, t, :, 0:DH], ALU.mult, ALU.subtract).then_inc(vlo_ready, 1)

                    def make_qk(b, t):
                        n = TILES * b + t
                        dve.wait_ge(exp_ready, n + 1)
                        dve.wait_ge(relu_ready, n + 1)
                        at_least(dve, lo_ready, n - 3)
                        nc.vector.scalar_tensor_tensor(qk[:, t % 4, :], eq[:, t % 4, :], 1.0, rq[:, t % 4, :],
                                                       ALU.min, ALU.add).then_inc(qk_ready, 1)

                    def qk_hi(b, t):
                        n = TILES * b + t
                        dve.wait_ge(qk_ready, n + 1)
                        at_least(dve, tr_done, n - 3)
                        for w in range(2):
                            src = qk[:, t % 4, w * C:(w + 1) * C].rearrange("p (h i) -> p h i", i=DH)
                            dst = pk[:, t % 4, w, :, :].rearrange("p h (a b i) -> p h a b i", a=2, b=2)
                            dst = dst[:, :, :, 0, :] if w == 0 else dst[:, :, 0, :, :]
                            last = nc.vector.tensor_copy(dst, src.unsqueeze(2).broadcast_to([P, NH, 2, DH]))
                        last.then_inc(hi_ready, 1)

                    def read_state(b, t):
                        if t == TILES - 1:
                            return
                        m = (TILES - 1) * b + t
                        dve.wait_ge(su_done, m + 1)
                        at_least(dve, sp_ready, m if t == 0 else m - 1)
                        nc.vector.tensor_tensor(sm[:, t % 2, :, :], sbank,
                                                kcol("blk").unsqueeze(1).broadcast_to([P, NP, 2 * VW]), ALU.mult)\
                            .then_inc(sm_ready, 1)

                    def scores_lo(b, t):
                        n = TILES * b + t
                        dve.wait_ge(ahi_ready, n + 1)
                        at_least(dve, av_done, n - 1)
                        nc.vector.scalar_tensor_tensor(al[:, t % 2, :], p_a[:, :], 0.0, ah[:, t % 2, :],
                                                       ALU.max, ALU.subtract).then_inc(alo_ready, 1)

                    def denominator(b, t):
                        n = TILES * b + t
                        dve.wait_ge(av_done, n + 1)
                        nc.vector.tensor_scalar(dn[:, t % 2, 0, :], num[:, :, DH], 1e-6 * VS, None, ALU.max)\
                            .then_inc(den1, 1)

                    def invert(b, t):
                        n = TILES * b + t
                        dve.wait_ge(den1, n + 1)
                        nc.vector.reciprocal(dn[:, t % 2, 1, :], dn[:, t % 2, 0, :]).then_inc(den2, 1)

                    def divide(b, t):
                        n = TILES * b + t
                        dve.wait_ge(den2, n + 1)
                        at_least(dve, ot_done, n - 1)
                        nc.vector.tensor_tensor(o_[:, t % 2, :].rearrange("p (h i) -> p h i", i=DH), num[:, :, 0:DH],
                                                dn[:, t % 2, 1, :].unsqueeze(2).broadcast_to([P, NH, DH]), ALU.mult)\
                            .then_inc(o_ready, 1)

                    def residual(b, t):
                        n = TILES * b + t
                        dve.wait_ge(wo_done, n + 1)
                        dve.wait_ge(y_ready, n + 1)
                        nc.vector.tensor_tensor(yt[:, t, :], p_m1[:, 0:P], yt[:, t, :], ALU.add).then_inc(t1_ready, 1)

                    def stats2(b, t):
                        n = TILES * b + t
                        dve.wait_ge(t1_ready, n + 1)
                        nc.vector.bn_stats(st2[:, t % 4, 0:6], yt[:, t, :]).then_inc(bn2, 1)

                    def mean_var2(b, t):
                        n = TILES * b + t
                        dve.wait_ge(ones_set, 1)
                        dve.wait_ge(bn2, n + 1)
                        nc.vector.bn_aggr(st2[:, t % 4, 6:8], st2[:, t % 4, 0:6]).then_inc(mv2, 1)

                    def normalise(b, t):
                        n = TILES * b + t
                        s = st2[:, t % 4, :]
                        dve.wait_ge(rstd2, n + 1)
                        at_least(dve, zt_done, n)
                        nc.vector.tensor_scalar(z_[:, t % 2, :], yt[:, t, :], s[:, 6:7], s[:, 8:9],
                                                ALU.subtract, ALU.mult).then_inc(z_ready, 1)

                    def z_lo(b, t):
                        n = TILES * b + t
                        dve.wait_ge(zhi_ready, n + 1)
                        cols = bass.ds(n * P, P)
                        nc.vector.tensor_tensor(zl[:, cols], p_m2[:, P:2 * P], zh[:, cols], ALU.subtract)\
                            .then_inc(zlo_ready, 1)

                    nc.vector.memset(sone[:, :, :], 1.0)
                    nc.vector.memset(pk[:, :, :, :, :], 0.0)
                    nc.vector.memset(vp[:, :, :, DH:DH + 1], VS).then_inc(ones_set, 1)
                    run(dve, VECTOR_ORDER, {"stats1": stats1, "mean_var1": mean_var1, "v_lo": v_lo,
                        "make_qk": make_qk, "qk_hi": qk_hi, "read_state": read_state,
                        "scores_lo": scores_lo, "denominator": denominator,
                        "invert": invert, "divide": divide, "residual": residual,
                        "stats2": stats2, "mean_var2": mean_var2, "normalise": normalise,
                        "z_lo": z_lo})

                @block.gpsimd
                def _(pool):
                    mhalf = kc[:, COL["mhalf"][0]:COL["mhalf"][0] + 1]

                    def eps1(b, t):
                        n = TILES * b + t
                        pool.wait_ge(mv1, n + 1)
                        nc.gpsimd.tensor_tensor(st[:, t % 4, 9:10], st[:, t % 4, 7:8], kcol("eps")[:, 0:1], ALU.add)\
                            .then_inc(ve1, 1)

                    def eps2(b, t):
                        n = TILES * b + t
                        pool.wait_ge(mv2, n + 1)
                        nc.gpsimd.tensor_tensor(st2[:, t % 4, 9:10], st2[:, t % 4, 7:8], kcol("eps")[:, 1:2], ALU.add)\
                            .then_inc(ve2, 1)

                    def rsqrt1(b, t):
                        n = TILES * b + t
                        s = st[:, t % 4, :]
                        pool.wait_ge(ve1, n + 1)
                        nc.gpsimd.tensor_tensor(s[:, 8:9], s[:, 9:10], mhalf, ALU.pow).then_inc(rstd1, 1)

                    def rsqrt2(b, t):
                        n = TILES * b + t
                        s = st2[:, t % 4, :]
                        pool.wait_ge(ve2, n + 1)
                        nc.gpsimd.tensor_tensor(s[:, 8:9], s[:, 9:10], mhalf, ALU.pow).then_inc(rstd2, 1)

                    def qk_lo(b, t):
                        n = TILES * b + t
                        pool.wait_ge(hi_ready, n + 1)
                        for w in range(2):
                            src = qk[:, t % 4, w * C:(w + 1) * C].rearrange("p (h i) -> p h i", i=DH)
                            lo = pk[:, t % 4, w, :, (1 + w) * DH:(2 + w) * DH]
                            last = nc.gpsimd.tensor_tensor(lo, src, pk[:, t % 4, w, :, 0:DH], ALU.subtract)
                        last.then_inc(lo_ready, 1)

                    def state_hi(b, t):
                        if t == TILES - 1:
                            return
                        m = (TILES - 1) * b + t
                        pool.wait_ge(sm_ready, m + 1)
                        at_least(pool, av_done, TILES * b + t - 2)
                        nc.gpsimd.tensor_tensor(sp2[:, t % 4, 0, :, :], sm[:, t % 2, :, :], sone[:, :, :], ALU.mult)\
                            .then_inc(sh_ready, 1)

                    def state_lo(b, t):
                        if t == TILES - 1:
                            return
                        pool.wait_ge(sh_ready, (TILES - 1) * b + t + 1)
                        nc.gpsimd.tensor_tensor(sp2[:, t % 4, 1, :, :], sm[:, t % 2, :, :], sp2[:, t % 4, 0, :, :],
                                                ALU.subtract).then_inc(sp_ready, 1)

                    def split_x(b, t):
                        if t % HALF:
                            return
                        hf = t // HALF
                        q = 2 * b + hf
                        pool.wait_ge(xh_ready, q + 1)
                        nc.gpsimd.tensor_tensor(xl[:, hf, :], xf[:, hf, :], xh[:, hf, :], ALU.subtract)\
                            .then_inc(xl_ready, 1)

                    run(pool, GPSIMD_ORDER, {"eps1": eps1, "rsqrt1": rsqrt1, "qk_lo": qk_lo,
                        "state_hi": state_hi, "state_lo": state_lo, "split_x": split_x,
                        "eps2": eps2, "rsqrt2": rsqrt2})

        with ExitStack() as pb:
            grep = sb(pb, "gate_by_row", [P, B])
            g9 = sb(pb, "gate_and_one", [E + 1, B])
            gsum = sb(pb, "gate_hidden_batch_sums", [P, B])
            gbf = sb(pb, "gate_blocks_f32", [P, GB, FI])
            gbh = sb(pb, "gate_blocks_hi", [P, GB, FI], F16)
            gbl = sb(pb, "gate_blocks_lo", [P, GB, FI], F16)
            b1m = sb(pb, "merged_b1", [P, FC, B + 1])
            b1s = sb(pb, "merged_b1_of_half", [P, 2, FC])
            b2s = sb(pb, "merged_b2_rows", [64, C], F16)
            b2f = sb(pb, "merged_b2_f32", [B, C])
            wm1 = [sb(pb, f"merged_W1_{s}", [P, GB * F], F16) for s in ("hi", "lo")]
            wm2 = [sb(pb, f"merged_W2_{s}", [P, FC, GB * C], F16) for s in ("hi", "lo")]
            hf_ = sb(pb, "h_f32", [P, 2, 512])
            hh = sb(pb, "h_hi", [P, 2, FC, 512], F16)
            hl = sb(pb, "h_lo", [P, 2, FC, 512], F16)
            t1b = sb(pb, "t1_back", [P, 2, HALF, C])
            rn = sb(pb, "normed", [P, 2, HALF, C])
            rs = sb(pb, "ffn_stats", [P, 2, HALF, 6])
            rmv = sb(pb, "ffn_mean_var", [P, 2, HALF, 2])
            rr = sb(pb, "ffn_rstd_shift", [P, 2, 3, HALF])
            ob = sb(pb, "out_tile", [P, 2, 512])
            ps = pb.enter_context(nc.psum_tensor("psb", [P, 8, 512], F32))

            (b1_ready, gs_ready, g_done, g8, g9r, b12_done, b_chain, gb_a, gb_ready, mg_done, mhi_ready, mlo_ready,
             f1_done, h_ready, hhi_ready, hlo_ready, f2_done, fbn, fmv, fve, frs, fsh, n_ready, gain_ready, v_ready,
             t_done, ob_ready) = [sem(s) for s in (
                "b1_ready gs_ready g_done g8_ready g9_ready b12_done b_chain gb_f32 gb_ready mg_done mhi_ready mlo_ready "
                "f1_done h_ready hhi_ready hlo_ready f2_done fbn fmv fve frs fsh n_ready gain_ready v_ready "
                "t_done ob_ready").split()]
            t1_loaded = [sem(f"t1_loaded_{i}") for i in range(2)]
            out_stored = [sem(f"out_stored_{i}") for i in range(2)]
            NB_ = 16
            NQ = 2 * GB

            def at_least(eng, s, value):
                if not isinstance(value, int) or value > 0:
                    eng.wait_ge(s, value)

            def run(eng, g, stages, depth):
                for slot in range(6):
                    for k, stage_ in stages:
                        if slot - k >= 0:
                            stage_(g, (slot - k) // 2, (slot - k) % 2)
                with eng.Fori(3, GB) as bl:
                    for slot in range(2):
                        for k, stage_ in stages:
                            r = slot - k
                            stage_(g, bl + r // 2, r % 2)
                for slot in range(NQ, NQ + depth):
                    for k, stage_ in stages:
                        if slot - k < NQ:
                            stage_(g, (slot - k) // 2, (slot - k) % 2)

            def merged_views(kind, i, part):
                src = ps[:, i, :].rearrange("p (j m) -> p m j", j=4)
                if kind == 0:
                    dst = wm1[part][:, :].rearrange("p (m o) -> p m o", o=FO)[:, :, 4 * i:4 * i + 4]
                else:
                    dst = wm2[part][:, i // 2, :].rearrange("p (m o) -> p m o", o=DO)
                    dst = dst[:, :, 4 * (i % 2):4 * (i % 2) + 4]
                return src, dst

            with nc.Block() as block:
                @block.sync
                def _(sp):
                    def load(g, bl, hf):
                        q = NQ * g + 2 * bl + hf
                        if not (isinstance(bl, int) and bl == 0):
                            sp.wait_ge(v_ready, q - 1)
                        sp.dma_start(t1b[:, hf, :, :].rearrange("p a c -> p (a c)"), d["t1"][bass.ds(q * P, P), :])\
                            .then_inc(t1_loaded[hf], 16)

                    def store(g, bl, hf):
                        b = GB * g + bl
                        sp.wait_ge(ob_ready, 2 * b + hf + 1)
                        sp.dma_start(d["out"][bass.ds(b * P, P), hf * 512:(hf + 1) * 512], ob[:, hf, :])\
                            .then_inc(out_stored[hf], 16)

                    for g in range(NG):
                        if g:
                            sp.wait_ge(v_ready, NQ * g)
                        load(g, 0, 0)
                        load(g, 0, 1)
                        with sp.Fori(1, GB) as bl:
                            for hf in range(2):
                                load(g, bl, hf)
                                store(g, bl - 1, hf)
                        store(g, GB - 1, 0)
                        store(g, GB - 1, 1)
                    sp.wait_ge(out_stored[0], 16 * B)
                    sp.wait_ge(out_stored[1], 16 * B)

                @block.tensor
                def _(pe):
                    mm = nc.tensor.matmul
                    pe.wait_ge(gs_ready, 1)
                    mm(ps[:, 0, 0:B], gf2rep[:, :, :].rearrange("p e i -> p (e i)"), gsum[:, :], start=True, stop=True)
                    mm(ps[0:E, 1, 0:B], gf2T[:, :], gsum[:, :], start=True, stop=True).then_inc(g_done, 1)
                    pe.wait_ge(g9r, 1)
                    for c in range(FC):
                        mm(ps[:, 2, c * B:(c + 1) * B], t9b1[:, c * P:(c + 1) * P], g9[:, :], start=(c == 0), stop=True,
                           skip_group_check=True)
                    mm(ps[0:B, 3, 0:C], g9[:, :], t9b2[:, :], start=True, stop=True).then_inc(b12_done, 1)

                    def merge(g):
                        pe.wait_ge(gb_ready, g + 1)
                        for kind in range(2):
                            for i in range(8):
                                k = 8 * kind + i
                                if k >= 8:
                                    pe.wait_ge(mlo_ready, NB_ * g + k - 7)
                                elif g:
                                    pe.wait_ge(ob_ready, NQ * g)
                                    pe.wait_ge(hhi_ready, FC * NQ * g)
                                    pe.wait_ge(n_ready, NQ * g)
                                for j in range(4):
                                    if kind == 0:
                                        c0 = (4 * i + j) * C
                                        th, tl, base = tv1[0], tv1[1], w1s
                                    else:
                                        c0 = (4 * (i % 2) + j) * F + (i // 2) * P
                                        th, tl, base = tv2[0], tv2[1], w2s
                                    o = ps[:, i, j * P:(j + 1) * P]
                                    gh, gl = (x[:, :, :].rearrange("p b i -> p (b i)") for x in (gbh, gbl))
                                    mm(o, th[:, c0:c0 + P], gh, start=True, stop=False)
                                    mm(o, th[:, c0:c0 + P], gl, start=False, stop=False)
                                    mm(o, tl[:, c0:c0 + P], gh, start=False, stop=False)
                                    last = mm(o, base[:, c0:c0 + P], delta2h[:, :, :].rearrange("p b i -> p (b i)"),
                                              start=False, stop=True)
                                last.then_inc(mg_done, 1)

                    def up(c):
                        def stage_(g, bl, hf):
                            q = NQ * g + 2 * bl + hf
                            n = HALF * q
                            if not (isinstance(bl, int) and bl == 0 and hf == 0):
                                pe.wait_ge(hhi_ready, FC * (q - 1) + c + 1)
                            w = [x[:, bass.ds(bl * F + c * P, P)] for x in wm1]
                            hi, lo = zh[:, bass.ds(n * P, 512)], zl[:, bass.ds(n * P, 512)]
                            mm(ps[:, c, :], w[0], hi, start=True, stop=False)
                            mm(ps[:, c, :], w[0], lo, start=False, stop=False)
                            mm(ps[:, c, :], w[1], hi, start=False, stop=True).then_inc(f1_done, 1)
                        return stage_

                    def down(j):
                        def stage_(g, bl, hf):
                            q = NQ * g + 2 * bl + hf
                            n = HALF * q + j
                            o = ps[:, 4 + hf, j * P:(j + 1) * P]
                            if j == 0 and not (isinstance(bl, int) and bl == 0):
                                pe.wait_ge(n_ready, q - 1)
                            zc = bass.ds(n * P, P)
                            mm(o, zh[:, zc], ident_ws[:, :], start=True, stop=False)
                            mm(o, zl[:, zc], ident_ws[:, :], start=False, stop=False)
                            mm(o, onehoth[:, bass.ds(GB * g + bl, 1)].broadcast_to([64, P]), b2s[:, :],
                               start=False, stop=False)
                            for c in range(FC):
                                if j == 0:
                                    pe.wait_ge(hlo_ready, FC * q + c + 1)
                                w = [x[:, c, bass.ds(bl * C, C)] for x in wm2]
                                hi, lo = (x[:, hf, c, j * P:(j + 1) * P] for x in (hh, hl))
                                mm(o, hi, w[0], start=False, stop=False)
                                mm(o, hi, w[1], start=False, stop=False)
                                last = mm(o, lo, w[0], start=False, stop=(c == FC - 1))
                            if j == HALF - 1:
                                last.then_inc(f2_done, 1)
                        return stage_

                    def turn(g, bl, hf):
                        q = NQ * g + 2 * bl + hf
                        pe.wait_ge(v_ready, q + 1)
                        if not (isinstance(bl, int) and bl == 0):
                            pe.wait_ge(ob_ready, q - 1)
                        for j in range(HALF):
                            last = nc.tensor.transpose(ps[:, 6 + hf, j * P:(j + 1) * P], rn[:, hf, j, :], ident)
                        last.then_inc(t_done, 1)

                    for g in range(NG):
                        merge(g)
                        pe.wait_ge(mlo_ready, NB_ * (g + 1))
                        stages = []
                        for i in range(4):
                            stages += [(0, up(i)), (1, down(i))]
                        run(pe, g, stages + [(3, turn)], 3)

                @block.scalar
                def _(act):
                    def merged_hi(g):
                        for k in range(NB_):
                            kind, i = k // 8, k % 8
                            act.wait_ge(mg_done, NB_ * g + k + 1)
                            if g and k == 0:
                                act.wait_ge(f2_done, NQ * g)
                            src, dst = merged_views(kind, i, 0)
                            nc.scalar.activation(dst, src, ACT.Copy).then_inc(mhi_ready, 1)

                    def hidden(c):
                        def stage_(g, bl, hf):
                            q = NQ * g + 2 * bl + hf
                            m = FC * q + c
                            act.wait_ge(f1_done, m + 1)
                            if c == 0:
                                act.wait_ge(b1_ready, q + 1)
                            bias = b1s[:, hf, c:c + 1]
                            if not (isinstance(bl, int) and bl == 0 and hf == 0 and c < 2):
                                act.wait_ge(hlo_ready, m - 1)
                            nc.scalar.activation(hf_[:, c % 2, :], ps[:, c, :], ACT.Relu, bias=bias, scale=1.0 / WS)\
                                .then_inc(h_ready, 1)
                            if c == 0 and not (isinstance(bl, int) and bl == 0):
                                act.wait_ge(f2_done, q - 1)
                            nc.scalar.activation(hh[:, hf, c, :], ps[:, c, :], ACT.Relu, bias=bias, scale=1.0 / WS)\
                                .then_inc(hhi_ready, 1)
                        return stage_

                    def normalise(g, bl, hf):
                        q = NQ * g + 2 * bl + hf
                        act.wait_ge(fsh, q + 1)
                        if not (isinstance(bl, int) and bl == 0):
                            act.wait_ge(t_done, q - 1)
                        for j in range(HALF):
                            last = nc.scalar.activation(rn[:, hf, j, :], ps[:, 4 + hf, j * P:(j + 1) * P], ACT.Identity,
                                                        bias=rr[:, hf, 1, j:j + 1], scale=rr[:, hf, 0, j:j + 1])
                        last.then_inc(n_ready, 1)

                    def finish(g, bl, hf):
                        q = NQ * g + 2 * bl + hf
                        act.wait_ge(t_done, q + 1)
                        at_least(act, out_stored[hf], 16 * (GB * g + bl))
                        nc.scalar.activation(ob[:, hf, :], ps[:, 6 + hf, :], ACT.Identity, bias=lnb[:, 0:1])\
                            .then_inc(ob_ready, 1)

                    for g in range(NG):
                        merged_hi(g)
                        run(act, g, [(0, hidden(0)), (0, hidden(1)), (2, normalise), (0, hidden(2)), (0, hidden(3)),
                                     (3, finish)], 3)

                @block.vector
                def _(dve):
                    n = [0]

                    def link(ins):
                        n[0] += 1
                        ins.then_inc(b_chain, 1)
                        dve.wait_ge(b_chain, n[0])

                    nc.vector.memset(b2s[:, :], 0.0)
                    nc.vector.memset(b1m[:, :, B:B + 1], 0.0)
                    link(nc.vector.memset(g9[:, :], 1.0))
                    nc.vector.tensor_reduce(gsum[:, :], ghs[:, :].rearrange("p (b t) -> p b t", t=TILES), AX.X, ALU.add)\
                        .then_inc(gs_ready, 1)
                    dve.wait_ge(g_done, 1)
                    nc.vector.tensor_scalar(g9[0:E, :], ps[0:E, 1, 0:B], 1.0 / T, gf2b[:, 0:1], ALU.mult, ALU.add)\
                        .then_inc(g9r, 1)
                    link(nc.vector.tensor_scalar(grep[:, :], ps[:, 0, 0:B], 1.0 / T, gf2brep[:, 0:1], ALU.mult, ALU.add))
                    dve.wait_ge(b12_done, 1)
                    link(nc.vector.tensor_copy(b1m[:, :, 0:B], ps[:, 2, 0:FC * B].rearrange("p (c b) -> p c b", c=FC)))
                    nc.vector.tensor_copy(b1s[:, 0, :], b1m[:, :, 0]).then_inc(b1_ready, 1)
                    link(nc.vector.tensor_scalar(b2f[:, :], ps[0:B, 3, 0:C], WS, None, ALU.mult))
                    link(nc.vector.tensor_copy(b2s[0:B, :], b2f[:, :]))
                    link(nc.vector.tensor_tensor(b2s[32:32 + B, :], b2f[:, :], b2s[0:B, :], ALU.subtract))

                    def merged_lo(g):
                        if g:
                            dve.wait_ge(mg_done, NB_ * g)
                        delta = kcol("delta").unsqueeze(1).broadcast_to([P, GB, FI])
                        link(nc.vector.tensor_tensor(gbf[:, :, :], delta,
                                                     grep[:, g * GB:(g + 1) * GB].unsqueeze(2).broadcast_to([P, GB, FI]),
                                                     ALU.mult))
                        link(nc.vector.tensor_copy(gbh[:, :, :], gbf[:, :, :]))
                        nc.vector.tensor_tensor(gbl[:, :, :], gbf[:, :, :], gbh[:, :, :], ALU.subtract)\
                            .then_inc(gb_ready, 1)
                        for k in range(NB_):
                            kind, i = k // 8, k % 8
                            dve.wait_ge(mhi_ready, NB_ * g + k + 1)
                            src, hi = merged_views(kind, i, 0)
                            _, lo = merged_views(kind, i, 1)
                            nc.vector.tensor_tensor(lo, src, hi, ALU.subtract).then_inc(mlo_ready, 1)

                    def hidden_lo(c):
                        def stage_(g, bl, hf):
                            q = NQ * g + 2 * bl + hf
                            dve.wait_ge(hhi_ready, FC * q + c + 1)
                            nc.vector.tensor_tensor(hl[:, hf, c, :], hf_[:, c % 2, :], hh[:, hf, c, :], ALU.subtract)\
                                .then_inc(hlo_ready, 1)
                        return stage_

                    def stats(g, bl, hf):
                        q = NQ * g + 2 * bl + hf
                        dve.wait_ge(f2_done, q + 1)
                        for j in range(HALF):
                            last = nc.vector.bn_stats(rs[:, hf, j, :], ps[:, 4 + hf, j * P:(j + 1) * P])
                        last.then_inc(fbn, 1)
                        dve.wait_ge(gs_ready, 1)
                        dve.wait_ge(fbn, q + 1)
                        for j in range(HALF):
                            last = nc.vector.bn_aggr(rmv[:, hf, j, :], rs[:, hf, j, :])
                        last.then_inc(fmv, 1)
                        dve.wait_ge(fmv, q + 1)
                        nc.vector.tensor_scalar(rr[:, hf, 2, :], rmv[:, hf, :, 1], EPS * WS * WS, None, ALU.add)\
                            .then_inc(fve, 1)

                    def shift(g, bl, hf):
                        q = NQ * g + 2 * bl + hf
                        dve.wait_ge(frs, q + 1)
                        nc.vector.scalar_tensor_tensor(rr[:, hf, 1, :], rmv[:, hf, :, 0], -1.0, rr[:, hf, 0, :],
                                                       ALU.mult, ALU.mult).then_inc(fsh, 1)

                    def add_up(g, bl, hf):
                        q = NQ * g + 2 * bl + hf
                        dve.wait_ge(gain_ready, q + 1)
                        dve.wait_ge(t1_loaded[hf], 16 * (GB * g + bl + 1))
                        nc.vector.tensor_tensor(rn[:, hf, :, :], rn[:, hf, :, :], t1b[:, hf, :, :], ALU.add)\
                            .then_inc(v_ready, 1)

                    def next_bias(g, bl, hf):
                        b = GB * g + bl + hf
                        nc.vector.tensor_copy(b1s[:, 1 - hf, :], b1m[:, :, bass.ds(b, 1)].squeeze(2))\
                            .then_inc(b1_ready, 1)

                    for g in range(NG):
                        merged_lo(g)
                        run(dve, g, [(0, hidden_lo(0)), (0, next_bias), (2, stats), (0, hidden_lo(1)), (2, shift), (0, hidden_lo(2)),
                                     (2, add_up), (0, hidden_lo(3))], 3)

                @block.gpsimd
                def _(pool):
                    def gain(g, bl, hf):
                        q = NQ * g + 2 * bl + hf
                        pool.wait_ge(n_ready, q + 1)
                        nc.gpsimd.tensor_tensor(rn[:, hf, :, :], rn[:, hf, :, :],
                                                lng[:, :].unsqueeze(1).broadcast_to([P, HALF, C]), ALU.mult)\
                            .then_inc(gain_ready, 1)

                    def rsqrt(g, bl, hf):
                        q = NQ * g + 2 * bl + hf
                        pool.wait_ge(fve, q + 1)
                        nc.gpsimd.tensor_tensor(rr[:, hf, 0, :], rr[:, hf, 2, :], kcol("mhalf"), ALU.pow).then_inc(frs, 1)

                    for g in range(NG):
                        run(pool, g, [(0, rsqrt), (0, gain)], 0)


_INS = ["x", "L0_conv_width", "L0_conv_damp", "L1_attn_W_q", "L1_attn_W_k", "L1_attn_W_v", "L1_attn_W_out",
        "L1_ffn_gfc1_w", "L1_ffn_gfc1_b", "L1_ffn_gfc2_w", "L1_ffn_gfc2_b", "L1_ffn_W1", "L1_ffn_b1", "L1_ffn_W2",
        "L1_ffn_b2", "L1_ffn_ln_g", "L1_ffn_ln_b", "L1_ffn_tv_W1", "L1_ffn_tv_b1", "L1_ffn_tv_W2", "L1_ffn_tv_b2",
        "L1_ffn_tv_ln_g", "L1_ffn_tv_ln_b"]


def kernel(**inputs):
    import concourse.bacc as bacc
    from concourse.bass_utils import run_bass_kernel_spmd

    nc = bacc.Bacc("TRN2", target_bir_lowering=False, num_devices=1)
    arrays, aps = {}, {}
    for name in _INS:
        a = np.ascontiguousarray(inputs[name])
        if name == "x":
            a = a.reshape(B * C, T)
        if a.ndim == 0:
            a = a.reshape(1)
        arrays["in_" + name] = a
    arrays["in_consts"] = shape_constants()
    for name, a in arrays.items():
        aps[name[3:]] = nc.dram_tensor(name, a.shape, mybir.dt.from_np(a.dtype), kind="ExternalInput").ap()
    aps["t1"] = nc.dram_tensor("t1_rows", (NHALF * P, HALF * C), F32, kind="Internal").ap()
    aps["out"] = nc.dram_tensor("out_0", (B * C, T), F32, kind="ExternalOutput").ap()
    build(nc, aps)
    r = run_bass_kernel_spmd(nc, [arrays], core_ids=[0])
    return r.results[0]["out_0"].reshape(B, C, 32, 32)
```

```python
from contextlib import ExitStack

import numpy as np

import concourse.bass as bass
from concourse import mybir

F32 = mybir.dt.float32
F16 = mybir.dt.float16
BF16 = mybir.dt.bfloat16
ALU = mybir.AluOpType
ACT = mybir.ActivationFunctionType
AX = mybir.AxisListType

B, C, T = 16, 128, 1024
P = 128
TILES = T // P
NT = B * TILES
HALF = 4
NHALF = NT // HALF
NH, DH = 8, 16
VW = DH + 1
NP = NH // 2
F, E = 512, 8
FC = F // P
SCOPE = 63
WS = 32.0
WSI = 256.0
VS = 0.125
GB = 8
NG = B // GB
FI = P // E
FO = F // FI
DO = C // FI
EPS = 1e-5
BIG = -1.0e30

TENSOR_ORDER = [("turn", 2), ("turn_out", 5), ("project", 0), ("gate", 8), ("values", 4), ("turn_z", 7),
                ("state", 1), ("out_project", 5), ("scores", 2)]
SCALAR_ORDER = [("split_x", 0), ("relu_qk", 1), ("v_hi", 1), ("exp_qk", 1), ("scores_hi", 3),
                ("copy_out", 5), ("copy_qk", 2), ("gate_relu", 8), ("read_conv", 0), ("z_hi", 7)]
VECTOR_ORDER = [("read_state", 2), ("residual", 6), ("divide", 5), ("v_lo", 1), ("stats2", 6),
                ("make_qk", 1), ("mean_var2", 6), ("qk_hi", 1), ("stats1", 0), ("mean_var1", 0),
                ("scores_lo", 3), ("denominator", 4), ("z_lo", 7), ("invert", 4)]
GPSIMD_ORDER = [("centre", 7), ("split_x", 0), ("state_lo", 3), ("state_hi", 2), ("normalise", 7),
                ("eps2", 6), ("qk_lo", 1), ("eps1", 0), ("rsqrt1", 0), ("rsqrt2", 6)]

FFN_TENSOR_ORDER = [("up_2", 1), ("up_1", 0), ("up_3", 0), ("up_0", 0), ("turn", 3), ("down_0", 1),
                    ("down_1", 1), ("down_2", 1), ("down_3", 1)]
FFN_SCALAR_ORDER = [("hidden_hi_2", 1), ("hidden_2", 1), ("hidden_1", 0), ("hidden_3", 0),
                    ("hidden_hi_0", 0), ("hidden_0", 0), ("finish", 3), ("normalise", 2)]
FFN_VECTOR_ORDER = [("copy_w2", 0), ("copy_z", 0), ("stats", 2), ("add_up", 3), ("hidden_lo_2", 1),
                    ("mean_var", 2), ("add_eps", 2), ("hidden_hi_3", 0), ("hidden_hi_1", 0),
                    ("hidden_lo_1", 0), ("shift", 2), ("hidden_lo_0", 0), ("hidden_lo_3", 0)]
FFN_GPSIMD_ORDER = [("gain", 3), ("rsqrt", 2)]


def before(stage, other):
    names = [name for name, _ in TENSOR_ORDER]
    skew = dict(TENSOR_ORDER)
    return skew[other] - skew[stage] + (0 if names.index(other) < names.index(stage) else 1)


_COLS = [("cas", P), ("ident", P), ("maskneg", P), ("blk", 2 * VW), ("delta", FI), ("delta2", FI),
         ("onehot", B), ("pos", 1), ("fmask", 1), ("nodc", 1), ("lncoef", P), ("mhalf", HALF), ("eps", 2)]
COL = {}
_at = 0
for _name, _n in _COLS:
    COL[_name] = (_at, _at + _n)
    _at += _n
NCONST = _at


def shape_constants():
    k = np.zeros((P, NCONST), np.float32)

    def put(name, a):
        k[:a.shape[0], COL[name][0]:COL[name][1]] = a

    j = np.arange(P)
    ang = 2 * np.pi * ((j[:, None] * j[None, :]) % P) / P
    put("cas", np.cos(ang) + np.sin(ang))
    put("ident", np.eye(P))
    put("maskneg", np.where(j[:, None] > j[None, :], BIG, 0.0))
    put("blk", (j[:, None] // 64 == np.arange(2 * VW)[None, :] // VW).astype(np.float32))
    put("delta", (j[:, None] % FI == np.arange(FI)[None, :]).astype(np.float32))
    d2 = np.zeros((P, FI), np.float32)
    d2[:FI] = np.eye(FI)
    d2[32:32 + FI] = np.eye(FI)
    put("delta2", d2)
    oh = np.zeros((P, B), np.float32)
    oh[:B] = np.eye(B)
    oh[32:32 + B] = np.eye(B)
    put("onehot", oh)
    pos = np.where(j <= P // 2, j, j - P).astype(np.float32)
    put("pos", pos[:, None])
    put("fmask", ((np.abs(pos) <= SCOPE // 2) & (pos != 0)).astype(np.float32)[:, None])
    put("nodc", (j != 0).astype(np.float32)[:, None])
    merge = 0.03
    co = np.zeros((P, P), np.float32)
    co[:E] = merge
    co[E] = 1 - E * merge
    put("lncoef", co)
    put("mhalf", np.full((P, HALF), -0.5))
    put("eps", np.full((P, 2), [EPS * WSI * WSI, EPS]))
    return k


def build(nc, d):
    top = ExitStack()
    with top:
        def sb(ctx, name, shape, dt=F32):
            return ctx.enter_context(nc.sbuf_tensor(name, shape, dt))

        def sem(name):
            return top.enter_context(nc.semaphore(name))

        kc = sb(top, "consts", [P, NCONST])
        identb = sb(top, "ident_bf16", [P, P], BF16)
        identh = sb(top, "ident_f16", [P, P], F16)
        ident_ws = sb(top, "ident_f16_scaled", [P, P], F16)
        maskb = sb(top, "mask_bf16", [P, P], BF16)
        onehoth = sb(top, "onehot_f16", [64, B], F16)
        delta2h = sb(top, "delta2_f16", [64, GB, FI], F16)
        wh = sb(top, "w_in_hi", [P, 4 * C], F16)
        wl = sb(top, "w_in_lo", [P, 4 * C], F16)
        woT = sb(top, "w_outT", [P, C])
        gfh = sb(top, "gate1_hi", [P, C], F16)
        gfl = sb(top, "gate1_lo", [P, C], F16)
        gf1b = sb(top, "gate1_b", [P, 1])
        gf2T = sb(top, "gate2T", [P, E])
        gf2rep = sb(top, "gate2T_rep", [P, E, FI])
        gf2b = sb(top, "gate2_b", [E, 1])
        gf2brep = sb(top, "gate2_b_rep", [P, 1])
        t9b1 = sb(top, "tv_b1_and_b1", [E + 1, F])
        t9b2 = sb(top, "tv_b2_and_b2", [E + 1, C])
        lng = sb(top, "ln_gain_rows", [P, C])
        lnb = sb(top, "ln_bias_col", [P, 1])
        tv1 = [sb(top, f"tv_W1_{s}", [P, FO * C], F16) for s in ("hi", "lo")]
        tv2 = [sb(top, f"tv_W2_{s}", [P, DO * F], F16) for s in ("hi", "lo")]
        w1s = sb(top, "W1_hi_lo_rows", [64, FO * C], F16)
        w2s = sb(top, "W2_hi_lo_rows", [64, DO * F], F16)
        zh = sb(top, "zT_hi", [P, NT * P], F16)
        zl = sb(top, "zT_lo", [P, NT * P], F16)
        ghs = sb(top, "gate_hidden_sums", [P, NT])

        cas = kc[:, COL["cas"][0]:COL["cas"][1]]
        ident = kc[:, COL["ident"][0]:COL["ident"][1]]

        def kcol(name, rows=P):
            return kc[0:rows, COL[name][0]:COL[name][1]]

        s_const = sem("const_loaded")
        s_scal = sem("scalars_loaded")
        s_wts = sem("square_weights_loaded")
        s_small = sem("small_weights_loaded")
        s_tvl = [sem(f"tv_staged_{i}") for i in range(4)]
        s_tvf = sem("tv_stage_freed")
        s_dch = sem("setup_vector_chain")
        s_ach = sem("setup_scalar_chain")
        s_pch = sem("setup_tensor_chain")
        s_gch = sem("setup_gpsimd_chain")
        with ExitStack() as su:
            wid = sb(su, "width", [P, 1])
            dmp = sb(su, "damp", [P, 1])
            wsq = sb(su, "square_weights", [P, 5, C])
            wsqT = sb(su, "square_weights_T", [P, 5, C])
            g2n = sb(su, "gate2_rows", [E, C])
            l9g = sb(su, "ln_g_rows", [E + 1, C])
            l9b = sb(su, "ln_b_rows", [E + 1, C])
            v = sb(su, "filter_steps", [P, 16])
            casd = sb(su, "cas_scaled", [P, 2, C])
            wbig = sb(su, "w_in", [P, 4 * C])
            cw = sb(su, "centred_inverse", [P, C])
            stage = sb(su, "tv_stage", [P, 2, 4096])
            pa = su.enter_context(nc.psum_tensor("setup_psum", [P, 8, 512], F32))

            SQ = ["L1_attn_W_q", "L1_attn_W_k", "L1_attn_W_v", "L1_attn_W_out", "L1_ffn_gfc1_w"]
            tvsrc = [d["L1_ffn_tv_W1"].rearrange("e (i o) d -> (e i) (o d)", i=FI),
                     d["L1_ffn_tv_W2"].rearrange("e (i o) f -> (e i) (o f)", i=FI),
                     d["L1_ffn_W1"].rearrange("(i o) d -> i (o d)", i=FI),
                     d["L1_ffn_W2"].rearrange("(i o) f -> i (o f)", i=FI)]
            tvrows = [P, P, FI, FI]
            with nc.Block() as block:
                @block.sync
                def _(sp):
                    sp.dma_start(kc[:, :], d["consts"]).then_inc(s_const, 16)
                    sp.dma_start(wid[:, :], d["L0_conv_width"].partition_broadcast(P)).then_inc(s_scal, 16)
                    sp.dma_start(dmp[:, :], d["L0_conv_damp"].partition_broadcast(P)).then_inc(s_scal, 16)
                    for i, name in enumerate(SQ):
                        sp.dma_start(wsq[:, i, :], d[name]).then_inc(s_wts, 16)
                    sp.dma_start(g2n[:, :], d["L1_ffn_gfc2_w"]).then_inc(s_small, 16)
                    for dst, tv, base in ((l9g, "tv_ln_g", "ln_g"), (l9b, "tv_ln_b", "ln_b"),
                                          (t9b1, "tv_b1", "b1"), (t9b2, "tv_b2", "b2")):
                        sp.dma_start(dst[0:E, :], d["L1_ffn_" + tv]).then_inc(s_small, 16)
                        sp.dma_start(dst[E:E + 1, :], d["L1_ffn_" + base].unsqueeze(0)).then_inc(s_small, 16)
                    sp.dma_start(gf1b[:, :], d["L1_ffn_gfc1_b"].unsqueeze(1)).then_inc(s_small, 16)
                    sp.dma_start(gf2b[:, :], d["L1_ffn_gfc2_b"].unsqueeze(1)).then_inc(s_small, 16)
                    for e in range(E):
                        sp.dma_start(gf2brep[e * FI:(e + 1) * FI, :],
                                     d["L1_ffn_gfc2_b"][e:e + 1].partition_broadcast(FI)).then_inc(s_small, 16)
                    for i in range(4):
                        if i >= 2:
                            sp.wait_ge(s_tvf, i - 1)
                        sp.dma_start(stage[0:tvrows[i], i % 2, :], tvsrc[i]).then_inc(s_tvl[i], 16)
                NSMALL = 16 * (1 + 8 + 2 + E)

                @block.vector
                def _(dve):
                    n = [0]

                    def link(ins):
                        n[0] += 1
                        ins.then_inc(s_dch, 1)
                        dve.wait_ge(s_dch, n[0])

                    dve.wait_ge(s_const, 16)
                    dve.wait_ge(s_scal, 32)
                    pos, fmask, nodc = kcol("pos"), kcol("fmask"), kcol("nodc")
                    link(nc.vector.reciprocal(v[:, 0:1], wid[:, :]))
                    link(nc.vector.tensor_tensor(v[:, 1:2], pos, v[:, 0:1], ALU.mult))
                    link(nc.vector.tensor_tensor(v[:, 2:3], v[:, 1:2], v[:, 1:2], ALU.mult))
                    link(nc.vector.tensor_scalar(v[:, 3:4], v[:, 2:3], -1.0, 1.0, ALU.mult, ALU.add))
                    link(nc.vector.tensor_scalar(v[:, 14:15], wid[:, :], 3.0, None, ALU.mult))
                    dve.wait_ge(s_gch, 2)
                    link(nc.vector.tensor_scalar(v[:, 5:6], v[:, 4:5], float(2.0 / np.pi ** 0.25), dmp[:, 0:1],
                                                 ALU.mult, ALU.mult))
                    link(nc.vector.tensor_tensor(v[:, 6:7], v[:, 5:6], v[:, 3:4], ALU.mult))
                    link(nc.vector.tensor_tensor(v[:, 7:8], v[:, 6:7], fmask, ALU.mult))
                    dve.wait_ge(s_ach, 1)
                    link(nc.vector.tensor_tensor(v[:, 8:9], v[:, 7:8], v[:, 9:10], ALU.mult))
                    nc.vector.tensor_copy(identb[:, :], ident)
                    nc.vector.tensor_copy(identh[:, :], ident)
                    nc.vector.tensor_scalar(ident_ws[:, :], ident, WS, None, ALU.mult)
                    nc.vector.tensor_copy(maskb[:, :], kcol("maskneg"))
                    nc.vector.tensor_copy(onehoth[:, :], kcol("onehot", 64))
                    nc.vector.tensor_copy(delta2h[:, :, :],
                                          kcol("delta2", 64).unsqueeze(1).broadcast_to([64, GB, FI]))
                    dve.wait_ge(s_pch, 1)
                    link(nc.vector.tensor_scalar(v[:, 10:11], pa[:, 0, 0:1], -1.0, 1.0, ALU.mult, ALU.add))
                    link(nc.vector.reciprocal(v[:, 11:12], v[:, 10:11]))
                    link(nc.vector.tensor_scalar(v[:, 12:13], v[:, 11:12], 1.0 / P, None, ALU.mult))
                    link(nc.vector.tensor_tensor(v[:, 13:14], v[:, 12:13], nodc, ALU.mult))
                    link(nc.vector.tensor_scalar(casd[:, 0, :], cas, v[:, 12:13], None, ALU.mult))
                    link(nc.vector.tensor_scalar(casd[:, 1, :], cas, v[:, 13:14], None, ALU.mult))
                    dve.wait_ge(s_pch, 2)
                    nc.vector.tensor_copy(cw[:, :], pa[:, 1, 128:256])
                    nc.vector.tensor_scalar(wbig[:, 0:C], pa[:, 1, 0:128], WSI, None, ALU.mult)
                    link(nc.vector.tensor_copy(wsqT[:, 0:4, :], pa[:, 2, :].rearrange("p (a c) -> p a c", a=4)))
                    link(nc.vector.tensor_scalar(wsqT[:, 4, :], pa[:, 3, 0:128], WS, None, ALU.mult))
                    link(nc.vector.tensor_copy(woT[:, :], wsqT[:, 3, :]))
                    link(nc.vector.tensor_copy(gf2T[:, :], pa[:, 3, 128:128 + E]))
                    link(nc.vector.tensor_copy(gf2rep[:, :, :],
                                               gf2T[:, :].unsqueeze(2).broadcast_to([P, E, FI])))
                    link(nc.vector.tensor_copy(gfh[:, :], wsqT[:, 4, :]))
                    link(nc.vector.tensor_tensor(gfl[:, :], wsqT[:, 4, :], gfh[:, :], ALU.subtract))
                    dve.wait_ge(s_pch, 3)
                    nc.vector.tensor_scalar(wbig[:, C:3 * C], pa[:, 4, 0:2 * C], WSI, None, ALU.mult)
                    link(nc.vector.tensor_scalar(wbig[:, 3 * C:4 * C], pa[:, 4, 2 * C:3 * C], WSI * VS, None, ALU.mult))
                    link(nc.vector.tensor_copy(wh[:, :], wbig[:, :]))
                    link(nc.vector.tensor_tensor(wl[:, :], wbig[:, :], wh[:, :], ALU.subtract))
                    dve.wait_ge(s_pch, 4)
                    nc.vector.tensor_copy(lng[:, :], pa[:, 5, 0:C])
                    nc.vector.tensor_copy(lnb[:, :], pa[:, 5, C:C + 1])
                    dve.wait_ge(s_gch, 1)
                    los = [tv1[1], tv2[1]]
                    his = [tv1[0], tv2[0]]
                    for i in range(4):
                        dve.wait_ge(s_ach, i + 2)
                        if i < 2:
                            lo, hi, src = los[i][:, :], his[i][:, :], stage[:, i % 2, :]
                        else:
                            w = (w1s, w2s)[i - 2]
                            lo, hi, src = w[32:32 + FI, :], w[0:FI, :], stage[0:FI, i % 2, :]
                        nc.vector.scalar_tensor_tensor(lo, src, WS, hi, ALU.mult, ALU.subtract).then_inc(s_tvf, 1)

                @block.gpsimd
                def _(pool):
                    nc.gpsimd.memset(w1s[:, :], 0.0)
                    nc.gpsimd.memset(w2s[:, :], 0.0).then_inc(s_gch, 1)
                    pool.wait_ge(s_dch, 5)
                    nc.gpsimd.tensor_tensor(v[:, 4:5], v[:, 14:15], kc[:, COL["mhalf"][0]:COL["mhalf"][0] + 1], ALU.pow)\
                        .then_inc(s_gch, 1)

                @block.scalar
                def _(act):
                    act.wait_ge(s_dch, 3)
                    nc.scalar.activation(v[:, 9:10], v[:, 2:3], ACT.Exp, scale=-0.5).then_inc(s_ach, 1)
                    act.wait_ge(s_gch, 1)
                    for i in range(4):
                        act.wait_ge(s_tvl[i], 16)
                        hi = (tv1[0][:, :], tv2[0][:, :], w1s[0:FI, :], w2s[0:FI, :])[i]
                        nc.scalar.activation(hi, stage[0:tvrows[i], i % 2, :], ACT.Copy, scale=WS).then_inc(s_ach, 1)

                @block.tensor
                def _(pe):
                    mm = nc.tensor.matmul
                    pe.wait_ge(s_dch, 9)
                    mm(pa[:, 0, 0:1], cas, v[:, 8:9], start=True, stop=True).then_inc(s_pch, 1)
                    pe.wait_ge(s_wts, 16 * 5)
                    pe.wait_ge(s_small, NSMALL)
                    for i in range(5):
                        nc.tensor.transpose(pa[:, 2 + i // 4, (i % 4) * 128:(i % 4) * 128 + 128], wsq[:, i, :], ident)
                    nc.tensor.transpose(pa[:, 3, 128:128 + E], g2n[:, :], kc[0:E, COL["ident"][0]:COL["ident"][0] + E])
                    pe.wait_ge(s_dch, 15)
                    mm(pa[:, 1, 0:128], casd[:, 0, :], cas, start=True, stop=True)
                    mm(pa[:, 1, 128:256], casd[:, 1, :], cas, start=True, stop=True).then_inc(s_pch, 1)
                    pe.wait_ge(s_dch, 16)
                    mm(pa[:, 4, 0:3 * C], cw[:, :], wsqT[:, 0:3, :].rearrange("p a c -> p (a c)"),
                       start=True, stop=True).then_inc(s_pch, 1)
                    mm(pa[:, 5, 0:C], kcol("lncoef", E + 1), l9g[:, :], start=True, stop=True)
                    mm(pa[:, 5, C:C + 1], l9b[:, :], kc[0:E + 1, COL["lncoef"][0]:COL["lncoef"][0] + 1],
                       start=True, stop=True).then_inc(s_pch, 1)

        with ExitStack() as pa_:
            xf = sb(pa_, "x_f32", [P, 2, HALF * P])
            xh = sb(pa_, "x_hi", [P, 2, HALF * P], F16)
            xl = sb(pa_, "x_lo", [P, 2, HALF * P], F16)
            yt = sb(pa_, "y_then_t1", [P, TILES, C])
            eq = sb(pa_, "exp_qk", [P, 4, 2 * C])
            rq = sb(pa_, "relu_qk", [P, 4, 2 * C])
            qk = sb(pa_, "qk_f32", [P, 4, 2 * C])
            pk = sb(pa_, "qk_parts", [P, 4, 2, NH, 4 * DH], F16)
            vp = sb(pa_, "v_parts", [P, 8, NH, 2 * DH + 1], F16)
            qkT = sb(pa_, "qkT_parts", [P, 4, 2, NP, P], F16)
            ah = sb(pa_, "scores_hi", [P, 2, NH * P], F16)
            al = sb(pa_, "scores_lo", [P, 2, NH * P], F16)
            sm = sb(pa_, "state_f32", [P, 2, NP, 2 * VW])
            sone = sb(pa_, "state_ones", [P, NP, 2 * VW])
            sp2 = sb(pa_, "state_parts", [P, 4, 2, NP, 2 * VW], F16)
            o_ = sb(pa_, "attn_out", [P, 2, C])
            oT = sb(pa_, "attn_outT", [P, 2, C])
            z_ = sb(pa_, "z", [P, 2, C])
            st = sb(pa_, "stats1", [P, 4, 16])
            st2 = sb(pa_, "stats2", [P, 4, 16])
            dn = sb(pa_, "denominators", [P, 2, 2, NH])
            gjunk = sb(pa_, "gate_hidden", [P, P])

            p_in = pa_.enter_context(nc.psum_tensor("p_in", [P, 512], F32))
            p_m1 = pa_.enter_context(nc.psum_tensor("p_m1", [P, 512], F32))
            p_tr = pa_.enter_context(nc.psum_tensor("p_tr", [P, 2, NP, P], F16))
            p_a = pa_.enter_context(nc.psum_tensor("p_a", [P, NH * P], F32))
            p_o = pa_.enter_context(nc.psum_tensor("p_o", [P, 512], F32))
            p_s = pa_.enter_context(nc.psum_tensor("p_s", [P, 512], F32))
            p_m2 = pa_.enter_context(nc.psum_tensor("p_m2", [P, 512], F32))
            num = p_o[:, 0:NH * VW].rearrange("p (h w) -> p h w", w=VW)
            sbank = p_s[:, 0:NP * 2 * VW].rearrange("p (a w) -> p a w", w=2 * VW)

            x_loaded = [sem(f"x_loaded_{i}") for i in range(2)]
            t1_stored = [sem(f"t1_stored_{i}") for i in range(TILES // 2)]
            (xh_ready, xl_ready, in_done, bn1, mv1, ve1, rstd1, y_ready, vhi_ready, exp_ready, relu_ready, vlo_ready,
             qk_ready, hi_ready, lo_ready, tr_done, qkT_ready, su_done, sm_ready, sh_ready, sp_ready,
             sc_done, ahi_ready, alo_ready, av_done, den1, den2, o_ready, ot_done, oT_ready, wo_done,
             t1_ready, bn2, mv2, ve2, rstd2, zc_ready, z_ready, zt_done, zhi_ready, zlo_ready, gt_done, gate_ready) = [
                sem(s) for s in (
                    "xh_ready xl_ready in_done bn1 mv1 ve1 rstd1 y_ready vhi_ready exp_ready relu_ready vlo_ready "
                    "qk_ready hi_ready lo_ready tr_done qkT_ready su_done sm_ready sh_ready sp_ready "
                    "sc_done ahi_ready alo_ready av_done den1 den2 o_ready ot_done oT_ready wo_done "
                    "t1_ready bn2 mv2 ve2 rstd2 zc_ready z_ready zt_done zhi_ready zlo_ready gt_done gate_ready").split()]
            ones_set = sem("ones_set")

            def at_least(eng, s, value):
                if not isinstance(value, int) or value > 0:
                    eng.wait_ge(s, value)

            def batch(stages, b, old=True, new=True):
                for slot in range(TILES):
                    for k, stage_ in stages:
                        t = slot - k
                        if t >= 0 and new:
                            stage_(b, t)
                        elif t < 0 and old:
                            stage_(b - 1, t + TILES)

            def run(eng, order, stages):
                stages = [(skew, stages[name]) for name, skew in order]
                batch(stages, 0, old=False)
                with eng.Fori(1, B) as b:
                    batch(stages, b)
                batch(stages, B, new=False)

            def cap(n):
                return min(n, NT) if isinstance(n, int) else n

            with nc.Block() as block:
                @block.sync
                def _(sp):
                    def load(b, hf):
                        q = 2 * b + hf
                        at_least(sp, xh_ready, q - 1)
                        at_least(sp, xl_ready, q - 1)
                        sp.dma_start(xf[:, hf, :], d["x"][bass.ds(b * P, P), hf * HALF * P:(hf + 1) * HALF * P])\
                            .then_inc(x_loaded[hf], 16)

                    def store(b, pair):
                        hf, i = pair // 2, pair % 2
                        sp.wait_ge(t1_ready, TILES * b + 2 * (pair + 1))
                        sp.dma_start(d["t1"][bass.ds((2 * b + hf) * P, P), 2 * C * i:2 * C * (i + 1)],
                                     yt[:, 2 * pair:2 * pair + 2, :].rearrange("p a c -> p (a c)"))\
                            .then_inc(t1_stored[pair], 16)

                    load(0, 0)
                    load(0, 1)
                    with sp.Fori(1, B) as b:
                        load(b, 0)
                        store(b - 1, 0)
                        store(b - 1, 1)
                        load(b, 1)
                        store(b - 1, 2)
                        store(b - 1, 3)
                    for pair in range(TILES // 2):
                        store(B - 1, pair)
                    for pair in range(TILES // 2):
                        sp.wait_ge(t1_stored[pair], 16 * B)

                @block.tensor
                def _(pe):
                    mm = nc.tensor.matmul

                    def project(b, t):
                        n = TILES * b + t
                        hf, j = t // HALF, t % HALF
                        if j == 0:
                            pe.wait_ge(xh_ready, 2 * b + hf + 1)
                            pe.wait_ge(xl_ready, 2 * b + hf + 1)
                        at_least(pe, exp_ready, n)
                        at_least(pe, relu_ready, n)
                        at_least(pe, vlo_ready, n)
                        cols = slice(j * P, (j + 1) * P)
                        mm(p_in[:, :], xh[:, hf, cols], wh[:, :], start=True, stop=False)
                        mm(p_in[:, :], xh[:, hf, cols], wl[:, :], start=False, stop=False)
                        mm(p_in[:, :], xl[:, hf, cols], wh[:, :], start=False, stop=True).then_inc(in_done, 1)

                    def state(b, t):
                        if t == TILES - 1:
                            return
                        n = TILES * b + t
                        pe.wait_ge(lo_ready, n + 1)
                        pe.wait_ge(hi_ready, n + 1)
                        pe.wait_ge(vlo_ready, n + 1)
                        pe.wait_ge(vhi_ready, n + 1)
                        if n == 0 if isinstance(n, int) else False:
                            pe.wait_ge(ones_set, 1)
                        at_least(pe, sm_ready, (TILES - 1) * b + t)
                        for a in range(NP):
                            kk = pk[:, t % 4, 1, 2 * a:2 * a + 2, :].rearrange("p h c -> p (h c)")
                            mm(sbank[:, a, :], kk, vp[:, t, 2 * a:2 * a + 2, 0:VW],
                               start=(t == 0 and a == 0), stop=False, skip_group_check=True)
                            last = mm(sbank[:, a, :].rearrange("p (h w) -> p h w", w=VW)[:, :, 0:DH], kk,
                                      vp[:, t, 2 * a:2 * a + 2, VW:VW + DH],
                                      start=False, stop=True, skip_group_check=True)
                        last.then_inc(su_done, 1)

                    def turn(b, t):
                        n = TILES * b + t
                        pe.wait_ge(lo_ready, n + 1)
                        pe.wait_ge(hi_ready, n + 1)
                        at_least(pe, qkT_ready, n)
                        for w in range(2):
                            for a in range(NP):
                                last = nc.tensor.transpose(
                                    p_tr[:, w, a, :], pk[:, t % 4, w, 2 * a:2 * a + 2, :].rearrange("p h c -> p (h c)"),
                                    identh[:, :])
                        last.then_inc(tr_done, 1)

                    def scores(b, t):
                        n = TILES * b + t
                        pe.wait_ge(qkT_ready, n + 1)
                        at_least(pe, ahi_ready, n)
                        at_least(pe, alo_ready, n)
                        for eo in range(2):
                            mm(p_a[:, eo * 512:(eo + 1) * 512], identb[:, :],
                               maskb[:, :].unsqueeze(1).broadcast_to([P, NP, P]),
                               start=True, stop=False, skip_group_check=True)
                        for h in range(NH):
                            a, eo = h // 2, h % 2
                            r = 64 * eo
                            last = mm(p_a[:, eo * 512 + a * P:eo * 512 + (a + 1) * P],
                                      qkT[r:r + 64, t % 4, 1, a, :], qkT[r:r + 64, t % 4, 0, a, :],
                                      start=False, stop=True, skip_group_check=True)
                        last.then_inc(sc_done, 1)

                    def values(b, t):
                        n = TILES * b + t
                        pe.wait_ge(ahi_ready, n + 1)
                        pe.wait_ge(alo_ready, n + 1)
                        at_least(pe, o_ready, n)
                        if t:
                            pe.wait_ge(sp_ready, (TILES - 1) * b + t)
                        for h in range(NH):
                            c0 = (h % 2) * 512 + (h // 2) * P
                            hi, lo = ah[:, t % 2, c0:c0 + P], al[:, t % 2, c0:c0 + P]
                            mm(num[:, h, :], hi, vp[:, t, h, 0:VW], start=(h == 0), stop=False,
                               skip_group_check=True)
                            mm(num[:, h, 0:DH], hi, vp[:, t, h, VW:VW + DH], start=False, stop=False,
                               skip_group_check=True)
                            last = mm(num[:, h, :], lo, vp[:, t, h, 0:VW], start=False, stop=True,
                                      skip_group_check=True)
                        if t:
                            for a in range(NP):
                                for part in range(2):
                                    last = mm(p_o[:, 2 * VW * a:2 * VW * (a + 1)], qkT[:, t % 4, 0, a, :],
                                              sp2[:, (t - 1) % 4, part, a, :], start=False, stop=True,
                                              skip_group_check=True)
                        last.then_inc(av_done, 1)

                    def other_read(n, own, other, lag):
                        for s_ in other:
                            at_least(pe, s_, cap(n - lag + 1))
                        if isinstance(n, int) and (n - lag < 0 or n - lag >= NT):
                            for s_ in own:
                                at_least(pe, s_, n)

                    def turn_out(b, t):
                        n = TILES * b + t
                        pe.wait_ge(o_ready, n + 1)
                        other_read(n, (oT_ready,), (zhi_ready, zlo_ready), before("turn_out", "turn_z"))
                        nc.tensor.transpose(p_m2[:, 0:P], o_[:, t % 2, :], ident).then_inc(ot_done, 1)

                    def out_project(b, t):
                        n = TILES * b + t
                        pe.wait_ge(oT_ready, n + 1)
                        other_read(n, (t1_ready,), (gate_ready,), before("out_project", "gate"))
                        mm(p_m1[:, 0:P], oT[:, t % 2, :], woT[:, :], start=True, stop=True).then_inc(wo_done, 1)

                    def turn_z(b, t):
                        n = TILES * b + t
                        pe.wait_ge(z_ready, n + 1)
                        other_read(n, (zhi_ready, zlo_ready), (oT_ready,), before("turn_z", "turn_out"))
                        nc.tensor.transpose(p_m2[:, P:2 * P], z_[:, t % 2, :], ident).then_inc(zt_done, 1)

                    def gate(b, t):
                        n = TILES * b + t
                        pe.wait_ge(zhi_ready, n + 1)
                        pe.wait_ge(zlo_ready, n + 1)
                        other_read(n, (gate_ready,), (t1_ready,), before("gate", "out_project"))
                        g = p_m1[:, P:2 * P]
                        hi, lo = zh[:, bass.ds(n * P, P)], zl[:, bass.ds(n * P, P)]
                        mm(g, gfh[:, :], hi, start=True, stop=False)
                        mm(g, gfl[:, :], hi, start=False, stop=False)
                        mm(g, gfh[:, :], lo, start=False, stop=True).then_inc(gt_done, 1)

                    pe.wait_ge(ones_set, 1)
                    run(pe, TENSOR_ORDER, {"project": project, "state": state, "turn": turn, "scores": scores,
                        "values": values, "turn_out": turn_out, "out_project": out_project, "turn_z": turn_z,
                        "gate": gate})

                @block.scalar
                def _(act):
                    def split_x(b, t):
                        if t % HALF:
                            return
                        hf = t // HALF
                        q = 2 * b + hf
                        act.wait_ge(x_loaded[hf], 16 * (b + 1))
                        at_least(act, in_done, HALF * (q - 1))
                        nc.scalar.activation(xh[:, hf, :], xf[:, hf, :], ACT.Copy).then_inc(xh_ready, 1)

                    def read_conv(b, t):
                        n = TILES * b + t
                        act.wait_ge(bn1, n + 1)
                        if t % 2 == 0:
                            at_least(act, t1_stored[t // 2], 16 * b)
                        at_least(act, z_ready, n - TILES + 1)
                        nc.scalar.activation(yt[:, t, :], p_in[:, 0:C], ACT.Copy, scale=1.0 / WSI).then_inc(y_ready, 1)

                    def v_hi(b, t):
                        n = TILES * b + t
                        act.wait_ge(rstd1, n + 1)
                        at_least(act, av_done, n - TILES + 2)
                        nc.scalar.activation(vp[:, t, :, 0:DH],
                                             p_in[:, 3 * C:4 * C].rearrange("p (h i) -> p h i", i=DH),
                                             ACT.Copy, scale=st[:, t % 4, 8:9]).then_inc(vhi_ready, 1)

                    def exp_qk(b, t):
                        n = TILES * b + t
                        act.wait_ge(rstd1, n + 1)
                        at_least(act, qk_ready, n - 3)
                        nc.scalar.activation(eq[:, t % 4, :], p_in[:, C:3 * C], ACT.Exp, scale=st[:, t % 4, 8:9])\
                            .then_inc(exp_ready, 1)

                    def relu_qk(b, t):
                        n = TILES * b + t
                        act.wait_ge(rstd1, n + 1)
                        at_least(act, qk_ready, n - 3)
                        nc.scalar.activation(rq[:, t % 4, :], p_in[:, C:3 * C], ACT.Relu, scale=st[:, t % 4, 8:9])\
                            .then_inc(relu_ready, 1)

                    def copy_out(b, t):
                        n = TILES * b + t
                        act.wait_ge(ot_done, n + 1)
                        at_least(act, wo_done, n - 1)
                        nc.scalar.activation(oT[:, t % 2, :], p_m2[:, 0:P], ACT.Copy).then_inc(oT_ready, 1)

                    def copy_qk(b, t):
                        n = TILES * b + t
                        act.wait_ge(tr_done, n + 1)
                        at_least(act, av_done, n - 3)
                        nc.scalar.activation(qkT[:, t % 4, :, :, :].rearrange("p w a c -> p (w a c)"),
                                             p_tr[:, :, :, :].rearrange("p w a c -> p (w a c)"), ACT.Copy)\
                            .then_inc(qkT_ready, 1)

                    def scores_hi(b, t):
                        n = TILES * b + t
                        act.wait_ge(sc_done, n + 1)
                        at_least(act, av_done, n - 1)
                        nc.scalar.activation(ah[:, t % 2, :], p_a[:, :], ACT.Relu).then_inc(ahi_ready, 1)

                    def z_hi(b, t):
                        n = TILES * b + t
                        act.wait_ge(ones_set, 1)
                        act.wait_ge(zt_done, n + 1)
                        nc.scalar.activation(zh[:, bass.ds(n * P, P)], p_m2[:, P:2 * P], ACT.Copy).then_inc(zhi_ready, 1)

                    def gate_relu(b, t):
                        n = TILES * b + t
                        act.wait_ge(ones_set, 1)
                        act.wait_ge(gt_done, n + 1)
                        nc.scalar.activation(gjunk[:, :], p_m1[:, P:2 * P], ACT.Relu, bias=gf1b[:, 0:1], scale=1.0 / WS,
                                             accum_out=ghs[:, bass.ds(n, 1)]).then_inc(gate_ready, 1)

                    run(act, SCALAR_ORDER, {"split_x": split_x, "read_conv": read_conv, "v_hi": v_hi,
                        "exp_qk": exp_qk, "relu_qk": relu_qk, "copy_qk": copy_qk, "scores_hi": scores_hi,
                        "copy_out": copy_out, "z_hi": z_hi, "gate_relu": gate_relu})

                @block.vector
                def _(dve):
                    def stats1(b, t):
                        n = TILES * b + t
                        dve.wait_ge(in_done, n + 1)
                        nc.vector.bn_stats(st[:, t % 4, 0:6], p_in[:, 0:C]).then_inc(bn1, 1)

                    def mean_var1(b, t):
                        n = TILES * b + t
                        dve.wait_ge(ones_set, 1)
                        dve.wait_ge(bn1, n + 1)
                        nc.vector.bn_aggr(st[:, t % 4, 6:8], st[:, t % 4, 0:6]).then_inc(mv1, 1)

                    def v_lo(b, t):
                        n = TILES * b + t
                        dve.wait_ge(vhi_ready, n + 1)
                        dve.wait_ge(exp_ready, n + 1)
                        dve.wait_ge(relu_ready, n + 1)
                        nc.vector.scalar_tensor_tensor(
                            vp[:, t, :, VW:VW + DH], p_in[:, 3 * C:4 * C].rearrange("p (h i) -> p h i", i=DH),
                            st[:, t % 4, 8:9], vp[:, t, :, 0:DH], ALU.mult, ALU.subtract).then_inc(vlo_ready, 1)

                    def make_qk(b, t):
                        n = TILES * b + t
                        dve.wait_ge(exp_ready, n + 1)
                        dve.wait_ge(relu_ready, n + 1)
                        at_least(dve, lo_ready, n - 3)
                        nc.vector.scalar_tensor_tensor(qk[:, t % 4, :], eq[:, t % 4, :], 1.0, rq[:, t % 4, :],
                                                       ALU.min, ALU.add).then_inc(qk_ready, 1)

                    def qk_hi(b, t):
                        n = TILES * b + t
                        dve.wait_ge(qk_ready, n + 1)
                        at_least(dve, tr_done, n - 3)
                        for w in range(2):
                            src = qk[:, t % 4, w * C:(w + 1) * C].rearrange("p (h i) -> p h i", i=DH)
                            dst = pk[:, t % 4, w, :, :].rearrange("p h (a b i) -> p h a b i", a=2, b=2)
                            dst = dst[:, :, :, 0, :] if w == 0 else dst[:, :, 0, :, :]
                            last = nc.vector.tensor_copy(dst, src.unsqueeze(2).broadcast_to([P, NH, 2, DH]))
                        last.then_inc(hi_ready, 1)

                    def read_state(b, t):
                        if t == TILES - 1:
                            return
                        m = (TILES - 1) * b + t
                        dve.wait_ge(su_done, m + 1)
                        at_least(dve, sp_ready, m if t == 0 else m - 1)
                        nc.vector.tensor_tensor(sm[:, t % 2, :, :], sbank,
                                                kcol("blk").unsqueeze(1).broadcast_to([P, NP, 2 * VW]), ALU.mult)\
                            .then_inc(sm_ready, 1)

                    def scores_lo(b, t):
                        n = TILES * b + t
                        dve.wait_ge(ahi_ready, n + 1)
                        at_least(dve, av_done, n - 1)
                        nc.vector.scalar_tensor_tensor(al[:, t % 2, :], p_a[:, :], 0.0, ah[:, t % 2, :],
                                                       ALU.max, ALU.subtract).then_inc(alo_ready, 1)

                    def denominator(b, t):
                        n = TILES * b + t
                        dve.wait_ge(av_done, n + 1)
                        nc.vector.tensor_scalar(dn[:, t % 2, 0, :], num[:, :, DH], 1e-6 * VS, None, ALU.max)\
                            .then_inc(den1, 1)

                    def invert(b, t):
                        n = TILES * b + t
                        dve.wait_ge(den1, n + 1)
                        nc.vector.reciprocal(dn[:, t % 2, 1, :], dn[:, t % 2, 0, :]).then_inc(den2, 1)

                    def divide(b, t):
                        n = TILES * b + t
                        dve.wait_ge(den2, n + 1)
                        at_least(dve, ot_done, n - 1)
                        nc.vector.tensor_tensor(o_[:, t % 2, :].rearrange("p (h i) -> p h i", i=DH), num[:, :, 0:DH],
                                                dn[:, t % 2, 1, :].unsqueeze(2).broadcast_to([P, NH, DH]), ALU.mult)\
                            .then_inc(o_ready, 1)

                    def residual(b, t):
                        n = TILES * b + t
                        dve.wait_ge(wo_done, n + 1)
                        dve.wait_ge(y_ready, n + 1)
                        nc.vector.tensor_tensor(yt[:, t, :], p_m1[:, 0:P], yt[:, t, :], ALU.add).then_inc(t1_ready, 1)

                    def stats2(b, t):
                        n = TILES * b + t
                        dve.wait_ge(t1_ready, n + 1)
                        nc.vector.bn_stats(st2[:, t % 4, 0:6], yt[:, t, :]).then_inc(bn2, 1)

                    def mean_var2(b, t):
                        n = TILES * b + t
                        dve.wait_ge(ones_set, 1)
                        dve.wait_ge(bn2, n + 1)
                        nc.vector.bn_aggr(st2[:, t % 4, 6:8], st2[:, t % 4, 0:6]).then_inc(mv2, 1)

                    def z_lo(b, t):
                        n = TILES * b + t
                        dve.wait_ge(zhi_ready, n + 1)
                        cols = bass.ds(n * P, P)
                        nc.vector.tensor_tensor(zl[:, cols], p_m2[:, P:2 * P], zh[:, cols], ALU.subtract)\
                            .then_inc(zlo_ready, 1)

                    nc.vector.memset(sone[:, :, :], 1.0)
                    nc.vector.memset(pk[:, :, :, :, :], 0.0)
                    nc.vector.memset(vp[:, :, :, DH:DH + 1], VS).then_inc(ones_set, 1)
                    run(dve, VECTOR_ORDER, {"stats1": stats1, "mean_var1": mean_var1, "v_lo": v_lo,
                        "make_qk": make_qk, "qk_hi": qk_hi, "read_state": read_state,
                        "scores_lo": scores_lo, "denominator": denominator,
                        "invert": invert, "divide": divide, "residual": residual,
                        "stats2": stats2, "mean_var2": mean_var2, 
                        "z_lo": z_lo})

                @block.gpsimd
                def _(pool):
                    mhalf = kc[:, COL["mhalf"][0]:COL["mhalf"][0] + 1]

                    def eps1(b, t):
                        n = TILES * b + t
                        pool.wait_ge(mv1, n + 1)
                        nc.gpsimd.tensor_tensor(st[:, t % 4, 9:10], st[:, t % 4, 7:8], kcol("eps")[:, 0:1], ALU.add)\
                            .then_inc(ve1, 1)

                    def eps2(b, t):
                        n = TILES * b + t
                        pool.wait_ge(mv2, n + 1)
                        nc.gpsimd.tensor_tensor(st2[:, t % 4, 9:10], st2[:, t % 4, 7:8], kcol("eps")[:, 1:2], ALU.add)\
                            .then_inc(ve2, 1)

                    def rsqrt1(b, t):
                        n = TILES * b + t
                        s = st[:, t % 4, :]
                        pool.wait_ge(ve1, n + 1)
                        nc.gpsimd.tensor_tensor(s[:, 8:9], s[:, 9:10], mhalf, ALU.pow).then_inc(rstd1, 1)

                    def rsqrt2(b, t):
                        n = TILES * b + t
                        s = st2[:, t % 4, :]
                        pool.wait_ge(ve2, n + 1)
                        nc.gpsimd.tensor_tensor(s[:, 8:9], s[:, 9:10], mhalf, ALU.pow).then_inc(rstd2, 1)

                    def qk_lo(b, t):
                        n = TILES * b + t
                        pool.wait_ge(hi_ready, n + 1)
                        for w in range(2):
                            src = qk[:, t % 4, w * C:(w + 1) * C].rearrange("p (h i) -> p h i", i=DH)
                            lo = pk[:, t % 4, w, :, (1 + w) * DH:(2 + w) * DH]
                            last = nc.gpsimd.tensor_tensor(lo, src, pk[:, t % 4, w, :, 0:DH], ALU.subtract)
                        last.then_inc(lo_ready, 1)

                    def state_hi(b, t):
                        if t == TILES - 1:
                            return
                        m = (TILES - 1) * b + t
                        pool.wait_ge(sm_ready, m + 1)
                        at_least(pool, av_done, TILES * b + t - 2)
                        nc.gpsimd.tensor_tensor(sp2[:, t % 4, 0, :, :], sm[:, t % 2, :, :], sone[:, :, :], ALU.mult)\
                            .then_inc(sh_ready, 1)

                    def state_lo(b, t):
                        if t == TILES - 1:
                            return
                        pool.wait_ge(sh_ready, (TILES - 1) * b + t + 1)
                        nc.gpsimd.tensor_tensor(sp2[:, t % 4, 1, :, :], sm[:, t % 2, :, :], sp2[:, t % 4, 0, :, :],
                                                ALU.subtract).then_inc(sp_ready, 1)

                    def split_x(b, t):
                        if t % HALF:
                            return
                        hf = t // HALF
                        q = 2 * b + hf
                        pool.wait_ge(xh_ready, q + 1)
                        nc.gpsimd.tensor_tensor(xl[:, hf, :], xf[:, hf, :], xh[:, hf, :], ALU.subtract)\
                            .then_inc(xl_ready, 1)

                    def centre(b, t):
                        n = TILES * b + t
                        pool.wait_ge(mv2, n + 1)
                        at_least(pool, zt_done, n)
                        nc.gpsimd.tensor_tensor(z_[:, t % 2, :], yt[:, t, :],
                                                st2[:, t % 4, 6:7].broadcast_to([P, C]), ALU.subtract)\
                            .then_inc(zc_ready, 1)

                    def normalise(b, t):
                        n = TILES * b + t
                        pool.wait_ge(zc_ready, n + 1)
                        pool.wait_ge(rstd2, n + 1)
                        nc.gpsimd.tensor_tensor(z_[:, t % 2, :], z_[:, t % 2, :],
                                                st2[:, t % 4, 8:9].broadcast_to([P, C]), ALU.mult)\
                            .then_inc(z_ready, 1)

                    run(pool, GPSIMD_ORDER, {"eps1": eps1, "rsqrt1": rsqrt1, "qk_lo": qk_lo,
                        "state_hi": state_hi, "state_lo": state_lo, "split_x": split_x,
                        "eps2": eps2, "rsqrt2": rsqrt2,
                        "centre": centre, "normalise": normalise})

        with ExitStack() as pb:
            grep = sb(pb, "gate_by_row", [P, B])
            g9 = sb(pb, "gate_and_one", [E + 1, B])
            gsum = sb(pb, "gate_hidden_batch_sums", [P, B])
            gbf = sb(pb, "gate_blocks_f32", [P, GB, FI])
            gbh = sb(pb, "gate_blocks_hi", [P, GB, FI], F16)
            gbl = sb(pb, "gate_blocks_lo", [P, GB, FI], F16)
            b1m = sb(pb, "merged_b1", [P, FC, B])
            b1s = sb(pb, "merged_b1_of_batch", [P, 2, FC])
            b2s = sb(pb, "merged_b2_rows", [64, C], F16)
            b2f = sb(pb, "merged_b2_f32", [B, C])
            wm1 = [sb(pb, f"merged_W1_{s}", [P, GB * F], F16) for s in ("hi", "lo")]
            wm2 = [sb(pb, f"merged_W2_{s}", [P, FC, GB * C], F16) for s in ("hi", "lo")]
            zs = sb(pb, "zT_of_half", [P, 2, 2, 512], F16)
            w2b = sb(pb, "merged_W2_of_batch", [P, 2, 2, FC, C], F16)
            ohb = sb(pb, "onehot_of_batch", [64, 2, P], F16)
            hf_ = sb(pb, "h_f32", [P, FC, 512])
            hh = sb(pb, "h_hi", [P, 2, FC, 512], F16)
            hl = sb(pb, "h_lo", [P, 2, FC, 512], F16)
            t1b = sb(pb, "t1_back", [P, 2, HALF, C])
            rn = sb(pb, "normed", [P, 2, HALF, C])
            rs = sb(pb, "ffn_stats", [P, 2, HALF, 6])
            rmv = sb(pb, "ffn_mean_var", [P, 2, HALF, 2])
            rr = sb(pb, "ffn_rstd_shift", [P, 2, 3, HALF])
            ob = sb(pb, "out_tile", [P, 2, 512])
            ps = pb.enter_context(nc.psum_tensor("psb", [P, 8, 512], F32))

            (b1_ready, gs_ready, g_done, g8, g9r, b12_done, b_chain, gb_a, gb_ready, mg_done, mhi_ready, mlo_ready,
             z_copied, w2_copied, f2_done, fbn, fmv, fve, frs, fsh, n_ready, gain_ready, v_ready,
             t_done, ob_ready) = [sem(s) for s in (
                "b1_ready gs_ready g_done g8_ready g9_ready b12_done b_chain gb_f32 gb_ready mg_done mhi_ready mlo_ready "
                "z_copied w2_copied f2_done fbn fmv fve frs fsh n_ready gain_ready v_ready "
                "t_done ob_ready").split()]
            up_done, h_ready, hhi_ready, hlo_ready = [[sem(f"{s}_{c}") for c in range(FC)] for s in
                                                      ("up_done", "h_ready", "hhi_ready", "hlo_ready")]
            t1_loaded = [sem(f"t1_loaded_{i}") for i in range(2)]
            out_stored = [sem(f"out_stored_{i}") for i in range(2)]
            NB_ = 16
            NQ = 2 * GB

            def at_least(eng, s, value):
                if not isinstance(value, int) or value > 0:
                    eng.wait_ge(s, value)

            HB = 4

            def run(eng, g, order, stages):
                stages = [(skew, stages[name]) for name, skew in order]
                for slot in range(HB):
                    for k, stage_ in stages:
                        if slot >= k:
                            stage_(g, 0, slot - k)
                with eng.Fori(1, NQ // HB) as pair:
                    for slot in range(HB):
                        for k, stage_ in stages:
                            stage_(g, pair + (slot - k) // HB, (slot - k) % HB)
                for slot in range(NQ, NQ + HB - 1):
                    for k, stage_ in stages:
                        if slot - k < NQ:
                            stage_(g, (slot - k) // HB, (slot - k) % HB)

            def merged_views(kind, i, part):
                src = ps[:, i, :].rearrange("p (j m) -> p m j", j=4)
                if kind == 0:
                    dst = wm1[part][:, :].rearrange("p (m o) -> p m o", o=FO)[:, :, 4 * i:4 * i + 4]
                else:
                    dst = wm2[part][:, i // 2, :].rearrange("p (m o) -> p m o", o=DO)
                    dst = dst[:, :, 4 * (i % 2):4 * (i % 2) + 4]
                return src, dst

            with nc.Block() as block:
                @block.sync
                def _(sp):
                    def load(g, bl, hf):
                        q = NQ * g + 2 * bl + hf
                        if not (isinstance(bl, int) and bl == 0):
                            sp.wait_ge(v_ready, q - 1)
                        sp.dma_start(t1b[:, hf, :, :].rearrange("p a c -> p (a c)"), d["t1"][bass.ds(q * P, P), :])\
                            .then_inc(t1_loaded[hf], 16)

                    def store(g, bl, hf):
                        b = GB * g + bl
                        sp.wait_ge(ob_ready, 2 * b + hf + 1)
                        sp.dma_start(d["out"][bass.ds(b * P, P), hf * 512:(hf + 1) * 512], ob[:, hf, :])\
                            .then_inc(out_stored[hf], 16)

                    for g in range(NG):
                        if g:
                            sp.wait_ge(v_ready, NQ * g)
                        load(g, 0, 0)
                        load(g, 0, 1)
                        with sp.Fori(1, GB) as bl:
                            for hf in range(2):
                                load(g, bl, hf)
                                store(g, bl - 1, hf)
                        store(g, GB - 1, 0)
                        store(g, GB - 1, 1)
                    sp.wait_ge(out_stored[0], 16 * (B + 1))
                    sp.wait_ge(out_stored[1], 16 * (B + 1))

                @block.tensor
                def _(pe):
                    mm = nc.tensor.matmul
                    pe.wait_ge(gs_ready, 1)
                    mm(ps[:, 0, 0:B], gf2rep[:, :, :].rearrange("p e i -> p (e i)"), gsum[:, :], start=True, stop=True)
                    mm(ps[0:E, 1, 0:B], gf2T[:, :], gsum[:, :], start=True, stop=True).then_inc(g_done, 1)
                    pe.wait_ge(g9r, 1)
                    for c in range(FC):
                        mm(ps[:, 2, c * B:(c + 1) * B], t9b1[:, c * P:(c + 1) * P], g9[:, :], start=(c == 0), stop=True,
                           skip_group_check=True)
                    mm(ps[0:B, 3, 0:C], g9[:, :], t9b2[:, :], start=True, stop=True).then_inc(b12_done, 1)

                    def merge(g):
                        pe.wait_ge(gb_ready, g + 1)
                        for kind in range(2):
                            for i in range(8):
                                k = 8 * kind + i
                                if k >= 8:
                                    pe.wait_ge(mlo_ready, NB_ * g + k - 7)
                                elif g and k == 0:
                                    pe.wait_ge(ob_ready, NQ * g)
                                    pe.wait_ge(n_ready, NQ * g)
                                    for c in range(FC):
                                        pe.wait_ge(h_ready[c], NQ * g)
                                        pe.wait_ge(hhi_ready[c], NQ * g)
                                for j in range(4):
                                    if kind == 0:
                                        c0 = (4 * i + j) * C
                                        th, tl, base = tv1[0], tv1[1], w1s
                                    else:
                                        c0 = (4 * (i % 2) + j) * F + (i // 2) * P
                                        th, tl, base = tv2[0], tv2[1], w2s
                                    o = ps[:, i, j * P:(j + 1) * P]
                                    gh, gl = (x[:, :, :].rearrange("p b i -> p (b i)") for x in (gbh, gbl))
                                    mm(o, th[:, c0:c0 + P], gh, start=True, stop=False)
                                    mm(o, th[:, c0:c0 + P], gl, start=False, stop=False)
                                    mm(o, tl[:, c0:c0 + P], gh, start=False, stop=False)
                                    last = mm(o, base[:, c0:c0 + P], delta2h[:, :, :].rearrange("p b i -> p (b i)"),
                                              start=False, stop=True)
                                last.then_inc(mg_done, 1)

                    def up(c):
                        def stage_(g, pair, h):
                            q, hf, bl = NQ * g + HB * pair + h, h % 2, 2 * pair + h // 2
                            pe.wait_ge(z_copied, q + 1)
                            at_least(pe, h_ready[c], q)
                            at_least(pe, hhi_ready[c], q)
                            w = [x[:, bass.ds(bl * F + c * P, P)] for x in wm1]
                            mm(ps[:, c, :], w[0], zs[:, hf, 0, :], start=True, stop=False)
                            mm(ps[:, c, :], w[0], zs[:, hf, 1, :], start=False, stop=False)
                            mm(ps[:, c, :], w[1], zs[:, hf, 0, :], start=False, stop=True).then_inc(up_done[c], 1)
                        return stage_

                    def down(j):
                        def stage_(g, pair, h):
                            q, hf, bb = NQ * g + HB * pair + h, h % 2, h // 2
                            o = ps[:, 4 + hf, j * P:(j + 1) * P]
                            cols = slice(j * P, (j + 1) * P)
                            if j == 0:
                                if hf == 0:
                                    pe.wait_ge(w2_copied, GB * g + 2 * pair + bb + 1)
                                at_least(pe, n_ready, q - 1)
                            mm(o, zs[:, hf, 0, cols], ident_ws[:, :], start=True, stop=False)
                            mm(o, zs[:, hf, 1, cols], ident_ws[:, :], start=False, stop=False)
                            mm(o, ohb[:, bb, :], b2s[:, :], start=False, stop=False)
                            for c in range(FC):
                                if j == 0:
                                    pe.wait_ge(hlo_ready[c], q + 1)
                                hi, lo = hh[:, hf, c, cols], hl[:, hf, c, cols]
                                mm(o, hi, w2b[:, bb, 0, c, :], start=False, stop=False)
                                mm(o, hi, w2b[:, bb, 1, c, :], start=False, stop=False)
                                last = mm(o, lo, w2b[:, bb, 0, c, :], start=False, stop=(c == FC - 1))
                            if j == HALF - 1:
                                last.then_inc(f2_done, 1)
                        return stage_

                    def turn(g, pair, h):
                        q, hf = NQ * g + HB * pair + h, h % 2
                        pe.wait_ge(v_ready, q + 1)
                        at_least(pe, ob_ready, q)
                        for j in range(HALF):
                            last = nc.tensor.transpose(ps[:, 6 + hf, j * P:(j + 1) * P], rn[:, hf, j, :], ident)
                        last.then_inc(t_done, 1)

                    for g in range(NG):
                        merge(g)
                        pe.wait_ge(mlo_ready, NB_ * (g + 1))
                        run(pe, g, FFN_TENSOR_ORDER, {
                            **{f"up_{c}": up(c) for c in range(FC)}, **{f"down_{j}": down(j) for j in range(HALF)},
                            "turn": turn})

                @block.scalar
                def _(act):
                    def merged_hi(g):
                        for k in range(NB_):
                            kind, i = k // 8, k % 8
                            act.wait_ge(mg_done, NB_ * g + k + 1)
                            if g and k == 0:
                                act.wait_ge(f2_done, NQ * g)
                            src, dst = merged_views(kind, i, 0)
                            nc.scalar.activation(dst, src, ACT.Copy).then_inc(mhi_ready, 1)

                    def hidden(c):
                        def stage_(g, pair, h):
                            q = NQ * g + HB * pair + h
                            if h % 2 == 0:
                                act.wait_ge(b1_ready, GB * g + 2 * pair + h // 2 + 1)
                            at_least(act, hlo_ready[c], q)
                            act.wait_ge(up_done[c], q + 1)
                            nc.scalar.activation(hf_[:, c, :], ps[:, c, :], ACT.Relu, bias=b1s[:, h // 2, c:c + 1],
                                                 scale=1.0 / WS).then_inc(h_ready[c], 1)
                        return stage_

                    def hidden_hi(c):
                        def stage_(g, pair, h):
                            q = NQ * g + HB * pair + h
                            if h % 2 == 0:
                                act.wait_ge(b1_ready, GB * g + 2 * pair + h // 2 + 1)
                            at_least(act, f2_done, q - 1)
                            act.wait_ge(up_done[c], q + 1)
                            nc.scalar.activation(hh[:, h % 2, c, :], ps[:, c, :], ACT.Relu,
                                                 bias=b1s[:, h // 2, c:c + 1], scale=1.0 / WS).then_inc(hhi_ready[c], 1)
                        return stage_

                    def normalise(g, pair, h):
                        q, hf = NQ * g + HB * pair + h, h % 2
                        act.wait_ge(fsh, q + 1)
                        at_least(act, t_done, q - 1)
                        for j in range(HALF):
                            last = nc.scalar.activation(rn[:, hf, j, :], ps[:, 4 + hf, j * P:(j + 1) * P], ACT.Identity,
                                                        bias=rr[:, hf, 1, j:j + 1], scale=rr[:, hf, 0, j:j + 1])
                        last.then_inc(n_ready, 1)

                    def finish(g, pair, h):
                        q, hf = NQ * g + HB * pair + h, h % 2
                        act.wait_ge(t_done, q + 1)
                        act.wait_ge(out_stored[hf], 16 * (GB * g + 2 * pair + h // 2 + 1))
                        nc.scalar.activation(ob[:, hf, :], ps[:, 6 + hf, :], ACT.Identity, bias=lnb[:, 0:1])\
                            .then_inc(ob_ready, 1)

                    for g in range(NG):
                        merged_hi(g)
                        run(act, g, FFN_SCALAR_ORDER, {
                            **{f"hidden_{c}": hidden(c) for c in range(FC)},
                            **{f"hidden_hi_{c}": hidden_hi(c) for c in range(FC)},
                            "normalise": normalise, "finish": finish})

                @block.vector
                def _(dve):
                    n = [0]

                    def link(ins):
                        n[0] += 1
                        ins.then_inc(b_chain, 1)
                        dve.wait_ge(b_chain, n[0])

                    nc.vector.memset(ob[:, 0, :], 0.0).then_inc(out_stored[0], 16)
                    nc.vector.memset(ob[:, 1, :], 0.0).then_inc(out_stored[1], 16)
                    nc.vector.memset(b2s[:, :], 0.0)
                    link(nc.vector.memset(g9[:, :], 1.0))
                    nc.vector.tensor_reduce(gsum[:, :], ghs[:, :].rearrange("p (b t) -> p b t", t=TILES), AX.X, ALU.add)\
                        .then_inc(gs_ready, 1)
                    dve.wait_ge(g_done, 1)
                    nc.vector.tensor_scalar(g9[0:E, :], ps[0:E, 1, 0:B], 1.0 / T, gf2b[:, 0:1], ALU.mult, ALU.add)\
                        .then_inc(g9r, 1)
                    link(nc.vector.tensor_scalar(grep[:, :], ps[:, 0, 0:B], 1.0 / T, gf2brep[:, 0:1], ALU.mult, ALU.add))
                    dve.wait_ge(b12_done, 1)
                    link(nc.vector.tensor_copy(b1m[:, :, :], ps[:, 2, 0:FC * B].rearrange("p (c b) -> p c b", c=FC)))
                    link(nc.vector.tensor_scalar(b2f[:, :], ps[0:B, 3, 0:C], WS, None, ALU.mult))
                    link(nc.vector.tensor_copy(b2s[0:B, :], b2f[:, :]))
                    link(nc.vector.tensor_tensor(b2s[32:32 + B, :], b2f[:, :], b2s[0:B, :], ALU.subtract))

                    def merged_lo(g):
                        if g:
                            dve.wait_ge(mg_done, NB_ * g)
                        delta = kcol("delta").unsqueeze(1).broadcast_to([P, GB, FI])
                        link(nc.vector.tensor_tensor(gbf[:, :, :], delta,
                                                     grep[:, g * GB:(g + 1) * GB].unsqueeze(2).broadcast_to([P, GB, FI]),
                                                     ALU.mult))
                        link(nc.vector.tensor_copy(gbh[:, :, :], gbf[:, :, :]))
                        nc.vector.tensor_tensor(gbl[:, :, :], gbf[:, :, :], gbh[:, :, :], ALU.subtract)\
                            .then_inc(gb_ready, 1)
                        for k in range(NB_):
                            kind, i = k // 8, k % 8
                            dve.wait_ge(mhi_ready, NB_ * g + k + 1)
                            src, hi = merged_views(kind, i, 0)
                            _, lo = merged_views(kind, i, 1)
                            nc.vector.tensor_tensor(lo, src, hi, ALU.subtract).then_inc(mlo_ready, 1)

                    def copy_z(g, pair, h):
                        q, hf, bb = NQ * g + HB * pair + h, h % 2, h // 2
                        b = GB * g + 2 * pair + bb
                        at_least(dve, f2_done, q - 1)
                        if hf == 0:
                            nc.vector.tensor_copy(b1s[:, bb, :], b1m[:, :, bass.ds(b, 1)].squeeze(2))\
                                .then_inc(b1_ready, 1)
                        for part, src in enumerate((zh, zl)):
                            last = nc.vector.tensor_copy(zs[:, hf, part, :], src[:, bass.ds(q * HALF * P, HALF * P)])
                        last.then_inc(z_copied, 1)

                    def copy_w2(g, pair, h):
                        if h % 2:
                            return
                        q, bb, bl = NQ * g + HB * pair + h, h // 2, 2 * pair + h // 2
                        at_least(dve, f2_done, q - 2)
                        nc.vector.tensor_copy(ohb[:, bb, :],
                                              onehoth[:, bass.ds(GB * g + bl, 1)].broadcast_to([64, P]))
                        for part in range(2):
                            last = nc.vector.tensor_copy(w2b[:, bb, part, :, :], wm2[part][:, :, bass.ds(bl * C, C)])
                        last.then_inc(w2_copied, 1)

                    def hidden_hi(c):
                        def stage_(g, pair, h):
                            q = NQ * g + HB * pair + h
                            at_least(dve, f2_done, q - 1)
                            dve.wait_ge(h_ready[c], q + 1)
                            nc.vector.tensor_copy(hh[:, h % 2, c, :], hf_[:, c, :]).then_inc(hhi_ready[c], 1)
                        return stage_

                    def hidden_lo(c):
                        def stage_(g, pair, h):
                            q = NQ * g + HB * pair + h
                            dve.wait_ge(h_ready[c], q + 1)
                            dve.wait_ge(hhi_ready[c], q + 1)
                            nc.vector.tensor_tensor(hl[:, h % 2, c, :], hf_[:, c, :], hh[:, h % 2, c, :], ALU.subtract)\
                                .then_inc(hlo_ready[c], 1)
                        return stage_

                    def stats(g, pair, h):
                        q, hf = NQ * g + HB * pair + h, h % 2
                        dve.wait_ge(f2_done, q + 1)
                        for j in range(HALF):
                            last = nc.vector.bn_stats(rs[:, hf, j, :], ps[:, 4 + hf, j * P:(j + 1) * P])
                        last.then_inc(fbn, 1)

                    def mean_var(g, pair, h):
                        q, hf = NQ * g + HB * pair + h, h % 2
                        dve.wait_ge(gs_ready, 1)
                        dve.wait_ge(fbn, q + 1)
                        for j in range(HALF):
                            last = nc.vector.bn_aggr(rmv[:, hf, j, :], rs[:, hf, j, :])
                        last.then_inc(fmv, 1)

                    def add_eps(g, pair, h):
                        q, hf = NQ * g + HB * pair + h, h % 2
                        dve.wait_ge(fmv, q + 1)
                        nc.vector.tensor_scalar(rr[:, hf, 2, :], rmv[:, hf, :, 1], EPS * WS * WS, None, ALU.add)\
                            .then_inc(fve, 1)

                    def shift(g, pair, h):
                        q, hf = NQ * g + HB * pair + h, h % 2
                        dve.wait_ge(frs, q + 1)
                        nc.vector.scalar_tensor_tensor(rr[:, hf, 1, :], rmv[:, hf, :, 0], -1.0, rr[:, hf, 0, :],
                                                       ALU.mult, ALU.mult).then_inc(fsh, 1)

                    def add_up(g, pair, h):
                        q, hf = NQ * g + HB * pair + h, h % 2
                        dve.wait_ge(gain_ready, q + 1)
                        dve.wait_ge(t1_loaded[hf], 16 * (GB * g + 2 * pair + h // 2 + 1))
                        nc.vector.tensor_tensor(rn[:, hf, :, :], rn[:, hf, :, :], t1b[:, hf, :, :], ALU.add)\
                            .then_inc(v_ready, 1)

                    for g in range(NG):
                        merged_lo(g)
                        dve.wait_ge(mlo_ready, NB_ * (g + 1))
                        run(dve, g, FFN_VECTOR_ORDER, {
                            "copy_z": copy_z, "copy_w2": copy_w2, "stats": stats, "mean_var": mean_var,
                            "add_eps": add_eps, "shift": shift, "add_up": add_up,
                            **{f"hidden_hi_{c}": hidden_hi(c) for c in range(FC)},
                            **{f"hidden_lo_{c}": hidden_lo(c) for c in range(FC)}})

                @block.gpsimd
                def _(pool):
                    def gain(g, pair, h):
                        q, hf = NQ * g + HB * pair + h, h % 2
                        pool.wait_ge(n_ready, q + 1)
                        nc.gpsimd.tensor_tensor(rn[:, hf, :, :], rn[:, hf, :, :],
                                                lng[:, :].unsqueeze(1).broadcast_to([P, HALF, C]), ALU.mult)\
                            .then_inc(gain_ready, 1)

                    def rsqrt(g, pair, h):
                        q, hf = NQ * g + HB * pair + h, h % 2
                        pool.wait_ge(fve, q + 1)
                        nc.gpsimd.tensor_tensor(rr[:, hf, 0, :], rr[:, hf, 2, :], kcol("mhalf"), ALU.pow).then_inc(frs, 1)

                    for g in range(NG):
                        run(pool, g, FFN_GPSIMD_ORDER, {"rsqrt": rsqrt, "gain": gain})


_INS = ["x", "L0_conv_width", "L0_conv_damp", "L1_attn_W_q", "L1_attn_W_k", "L1_attn_W_v", "L1_attn_W_out",
        "L1_ffn_gfc1_w", "L1_ffn_gfc1_b", "L1_ffn_gfc2_w", "L1_ffn_gfc2_b", "L1_ffn_W1", "L1_ffn_b1", "L1_ffn_W2",
        "L1_ffn_b2", "L1_ffn_ln_g", "L1_ffn_ln_b", "L1_ffn_tv_W1", "L1_ffn_tv_b1", "L1_ffn_tv_W2", "L1_ffn_tv_b2",
        "L1_ffn_tv_ln_g", "L1_ffn_tv_ln_b"]


def kernel(**inputs):
    import concourse.bacc as bacc
    from concourse.bass_utils import run_bass_kernel_spmd

    nc = bacc.Bacc("TRN2", target_bir_lowering=False, num_devices=1)
    arrays, aps = {}, {}
    for name in _INS:
        a = np.ascontiguousarray(inputs[name])
        if name == "x":
            a = a.reshape(B * C, T)
        if a.ndim == 0:
            a = a.reshape(1)
        arrays["in_" + name] = a
    arrays["in_consts"] = shape_constants()
    for name, a in arrays.items():
        aps[name[3:]] = nc.dram_tensor(name, a.shape, mybir.dt.from_np(a.dtype), kind="ExternalInput").ap()
    aps["t1"] = nc.dram_tensor("t1_rows", (NHALF * P, HALF * C), F32, kind="Internal").ap()
    aps["out"] = nc.dram_tensor("out_0", (B * C, T), F32, kind="ExternalOutput").ap()
    build(nc, aps)
    r = run_bass_kernel_spmd(nc, [arrays], core_ids=[0])
    return r.results[0]["out_0"].reshape(B, C, 32, 32)
```

```python
from contextlib import ExitStack

import numpy as np

import concourse.bass as bass
from concourse import mybir

F32 = mybir.dt.float32
F16 = mybir.dt.float16
BF16 = mybir.dt.bfloat16
ALU = mybir.AluOpType
ACT = mybir.ActivationFunctionType
AX = mybir.AxisListType

B, C, T = 16, 128, 1024
P = 128
TILES = T // P
NT = B * TILES
HALF = 4
NHALF = NT // HALF
NH, DH = 8, 16
VW = DH + 1
NP = NH // 2
F, E = 512, 8
FC = F // P
SCOPE = 63
WS = 32.0
WSI = 256.0
VS = 0.125
GB = 8
NG = B // GB
FI = P // E
FO = F // FI
DO = C // FI
BW = F * C // P
TVW = FO * C // B
EPS = 1e-5
BIG = -1.0e30

TENSOR_ORDER = [("scores_0", 3), ("scores_1", 3), ("turn", 2), ("turn_out", 5), ("conv", 0), ("values", 4),
                ("gate", 8), ("turn_z", 7), ("project", 0), ("state", 1), ("out_project", 5)]
SCALAR_ORDER = [("split_x", 0), ("z_hi", 8), ("exp_qk", 1), ("relu_qk", 1), ("read_t1", 6), ("tv_hi", 0),
                ("v_hi", 1), ("scores_hi_0", 3), ("scores_hi_1", 3), ("copy_out", 5), ("copy_qk", 2),
                ("gate_relu", 8)]
VECTOR_ORDER = [("denominator", 5), ("read_state", 2), ("invert", 5), ("z_lo", 8), ("divide", 5),
                ("make_qk", 1), ("stats2", 6), ("qk_hi", 1), ("stats1", 0), ("mean_var2", 6), ("tv_lo", 0),
                ("v_lo", 1), ("mean_var1", 0), ("eps1", 0), ("eps2", 6), ("scores_lo_0", 3),
                ("scores_lo_1", 3)]
GPSIMD_ORDER = [("rsqrt2", 7), ("split_x", 0), ("state_hi", 2), ("normalise", 7), ("state_lo", 2),
                ("qk_lo", 1), ("rsqrt1", 0), ("centre", 6)]

FFN_TENSOR_ORDER = [("up_0", 0), ("up_3", 0), ("up_1", 0), ("down_0", 1), ("down_1", 1), ("down_2", 1),
                    ("down_3", 1), ("up_2", 0), ("turn", 3)]
FFN_SCALAR_ORDER = [("hidden_3", 0), ("hidden_1", 0), ("hidden_hi_0", 0), ("hidden_0", 0), ("normalise", 2),
                    ("hidden_2", 0), ("hidden_hi_2", 0), ("finish", 3)]
FFN_VECTOR_ORDER = [("copy_z", 0), ("stats", 2), ("hidden_lo_0", 1), ("hidden_lo_2", 1), ("add_up", 3),
                    ("mean_var", 2), ("add_eps", 2), ("hidden_hi_1", 0), ("copy_w2", 0), ("shift", 2),
                    ("hidden_hi_3", 0), ("hidden_lo_1", 0), ("hidden_lo_3", 0)]
FFN_GPSIMD_ORDER = [("rsqrt", 2), ("gain", 2)]


def before(stage, other):
    names = [name for name, _ in TENSOR_ORDER]
    skew = dict(TENSOR_ORDER)
    return skew[other] - skew[stage] + (0 if names.index(other) < names.index(stage) else 1)


_COLS = [("cas", P), ("ident", P), ("maskneg", P), ("blk", 2 * VW), ("delta", FI), ("delta2", FI),
         ("onehot", B), ("pos", 1), ("fmask", 1), ("nodc", 1), ("lncoef", P), ("mhalf", HALF)]
COL = {}
_at = 0
for _name, _n in _COLS:
    COL[_name] = (_at, _at + _n)
    _at += _n
NCONST = _at


def shape_constants():
    k = np.zeros((P, NCONST), np.float32)

    def put(name, a):
        k[:a.shape[0], COL[name][0]:COL[name][1]] = a

    j = np.arange(P)
    ang = 2 * np.pi * ((j[:, None] * j[None, :]) % P) / P
    put("cas", np.cos(ang) + np.sin(ang))
    put("ident", np.eye(P))
    put("maskneg", np.where(j[:, None] > j[None, :], BIG, 0.0))
    put("blk", (j[:, None] // 64 == np.arange(2 * VW)[None, :] // VW).astype(np.float32))
    put("delta", (j[:, None] % FI == np.arange(FI)[None, :]).astype(np.float32))
    put("delta2", np.vstack([np.eye(FI), np.eye(FI)]))
    oh = np.zeros((P, B), np.float32)
    oh[:B] = np.eye(B)
    oh[32:32 + B] = np.eye(B)
    put("onehot", oh)
    pos = np.where(j <= P // 2, j, j - P).astype(np.float32)
    put("pos", pos[:, None])
    put("fmask", ((np.abs(pos) <= SCOPE // 2) & (pos != 0)).astype(np.float32)[:, None])
    put("nodc", (j != 0).astype(np.float32)[:, None])
    merge = 0.03
    co = np.zeros((P, P), np.float32)
    co[:E] = merge
    co[E] = 1 - E * merge
    put("lncoef", co)
    put("mhalf", np.full((P, HALF), -0.5))
    return k


def build(nc, d):
    top = ExitStack()
    with top:
        def sb(ctx, name, shape, dt=F32):
            return ctx.enter_context(nc.sbuf_tensor(name, shape, dt))

        def sem(name):
            return top.enter_context(nc.semaphore(name))

        kc = sb(top, "consts", [P, NCONST])
        identb = sb(top, "ident_bf16", [P, P], BF16)
        identh = sb(top, "ident_f16", [P, P], F16)
        ident_ws = sb(top, "ident_f16_scaled", [P, P], F16)
        maskb = sb(top, "mask_bf16", [P, P], BF16)
        onehoth = sb(top, "onehot_f16", [64, B], F16)
        delta2h = sb(top, "delta2_f16", [2 * FI, GB, FI], F16)
        wh = sb(top, "w_in_hi", [P, 4 * C], F16)
        wl = sb(top, "w_in_lo", [P, 4 * C], F16)
        woT = sb(top, "w_outT", [P, C])
        gfh = sb(top, "gate1_hi", [P, C], F16)
        gfl = sb(top, "gate1_lo", [P, C], F16)
        gf1b = sb(top, "gate1_b", [P, 1])
        gf2T = sb(top, "gate2T", [P, E])
        gf2rep = sb(top, "gate2T_rep", [P, E, FI])
        gf2b = sb(top, "gate2_b", [E, 1])
        gf2brep = sb(top, "gate2_b_rep", [P, 1])
        t9b1 = sb(top, "tv_b1_and_b1", [E + 1, F])
        t9b2 = sb(top, "tv_b2_and_b2", [E + 1, C])
        lng = sb(top, "ln_gain_rows", [P, C])
        lnb = sb(top, "ln_bias_col", [P, 1])
        tv = [sb(top, f"tv_{s}", [P, 2, FO * C], F16) for s in ("hi", "lo")]
        w1s = sb(top, "W1_hi_lo_rows", [2 * FI, FO * C], F16)
        w2s = sb(top, "W2_hi_lo_rows", [2 * FI, DO * F], F16)
        zh = sb(top, "zT_hi", [P, NT * P], F16)
        zl = sb(top, "zT_lo", [P, NT * P], F16)
        ghs = sb(top, "gate_hidden_sums", [P, NT])

        cas = kc[:, COL["cas"][0]:COL["cas"][1]]
        ident = kc[:, COL["ident"][0]:COL["ident"][1]]

        def kcol(name, rows=P):
            return kc[0:rows, COL[name][0]:COL[name][1]]

        s_const = sem("const_loaded")
        s_scal = sem("scalars_loaded")
        s_wts = sem("square_weights_loaded")
        s_small = sem("small_weights_loaded")
        NSMALL = 16 * (1 + 8 + 2 + E)
        s_inv = sem("inverse_ready")
        s_wtr = sem("weights_turned")
        s_wtc = sem("turned_weights_copied")
        x_loaded = [sem(f"x_loaded_{i}") for i in range(2)]
        ones_set = sem("ones_set")
        t1_stored = [sem(f"t1_stored_{i}") for i in range(TILES // 2)]
        ln_done, g2_ready = sem("merged_ln_done"), sem("gate2_ready")
        s_base = sem("base_weights_loaded")
        s_bhi = sem("base_hi_ready")
        s_blo = sem("base_lo_ready")
        base_stored = sem("base_parts_stored")
        base_placed = sem("base_rows_placed")
        s_dch = sem("setup_vector_chain")
        s_ach = sem("setup_scalar_chain")
        s_pch = sem("setup_tensor_chain")
        s_gch = sem("setup_gpsimd_chain")
        early = ExitStack()
        with ExitStack() as su:
            xf = sb(early, "x_f32", [P, 2, HALF * P])
            pk = sb(early, "qk_parts", [P, 4, 2, NH, 4 * DH], F16)
            vp = sb(early, "v_parts", [P, 8, NH, 2 * DH + 1], F16)
            sone = sb(early, "state_ones", [P, NP, 2 * VW])
            yt = sb(early, "t1", [P, TILES, C])
            g2n = sb(early, "gate2_rows", [E, C])
            l9g = sb(early, "ln_g_rows", [E + 1, C])
            l9b = sb(early, "ln_b_rows", [E + 1, C])
            bw = sb(early, "base_ffn_weights", [P, 2, BW])
            bwh = sb(early, "base_ffn_hi", [P, 2, BW], F16)
            bwl = sb(early, "base_ffn_lo", [P, 2, BW], F16)
            wid = sb(su, "width", [P, 1])
            dmp = sb(su, "damp", [P, 1])
            wsq = sb(su, "square_weights", [P, 5, C])
            wsqT = sb(su, "square_weights_T", [P, 5, C])
            v = sb(su, "filter_steps", [P, 16])
            casd = sb(su, "cas_scaled", [P, 2, C])
            wbig = sb(su, "w_in", [P, 4 * C])
            cw = sb(su, "centred_inverse", [P, C])
            pa = su.enter_context(nc.psum_tensor("setup_psum", [P, 8, 512], F32))

            SQ = ["L1_attn_W_q", "L1_attn_W_k", "L1_attn_W_v", "L1_attn_W_out", "L1_ffn_gfc1_w"]
            with nc.Block() as block:
                @block.sync
                def _(sp):
                    sp.dma_start(kc[:, :], d["consts"]).then_inc(s_const, 16)
                    sp.dma_start(wid[:, :], d["L0_conv_width"].partition_broadcast(P)).then_inc(s_scal, 16)
                    sp.dma_start(dmp[:, :], d["L0_conv_damp"].partition_broadcast(P)).then_inc(s_scal, 16)
                    for i, name in enumerate(SQ):
                        sp.dma_start(wsq[:, i, :], d[name]).then_inc(s_wts, 16)
                    for hf in range(2):
                        sp.dma_start(xf[:, hf, :], d["x"][0:P, hf * HALF * P:(hf + 1) * HALF * P])\
                            .then_inc(x_loaded[hf], 16)
                    for i, name in enumerate(("W1", "W2")):
                        flat = d["L1_ffn_" + name].rearrange("a b -> (a b)").rearrange("(p w) -> p w", p=P)
                        sp.dma_start(bw[:, i, :], flat).then_inc(s_base, 16)

                @block.vector
                def _(dve):
                    n = [0]

                    def link(ins):
                        n[0] += 1
                        ins.then_inc(s_dch, 1)
                        dve.wait_ge(s_dch, n[0])

                    dve.wait_ge(s_const, 16)
                    dve.wait_ge(s_scal, 32)
                    pos, fmask, nodc = kcol("pos"), kcol("fmask"), kcol("nodc")
                    link(nc.vector.reciprocal(v[:, 0:1], wid[:, :]))
                    link(nc.vector.tensor_tensor(v[:, 1:2], pos, v[:, 0:1], ALU.mult))
                    link(nc.vector.tensor_tensor(v[:, 2:3], v[:, 1:2], v[:, 1:2], ALU.mult))
                    link(nc.vector.tensor_scalar(v[:, 3:4], v[:, 2:3], -1.0, 1.0, ALU.mult, ALU.add))
                    link(nc.vector.tensor_scalar(v[:, 14:15], wid[:, :], 3.0, None, ALU.mult))
                    dve.wait_ge(s_gch, 1)
                    link(nc.vector.tensor_scalar(v[:, 5:6], v[:, 4:5], float(2.0 / np.pi ** 0.25), dmp[:, 0:1],
                                                 ALU.mult, ALU.mult))
                    link(nc.vector.tensor_tensor(v[:, 6:7], v[:, 5:6], v[:, 3:4], ALU.mult))
                    link(nc.vector.tensor_tensor(v[:, 7:8], v[:, 6:7], fmask, ALU.mult))
                    dve.wait_ge(s_ach, 1)
                    link(nc.vector.tensor_tensor(v[:, 8:9], v[:, 7:8], v[:, 9:10], ALU.mult))
                    nc.vector.tensor_copy(identb[:, :], ident)
                    nc.vector.tensor_copy(identh[:, :], ident)
                    nc.vector.tensor_scalar(ident_ws[:, :], ident, WS, None, ALU.mult)
                    nc.vector.tensor_copy(maskb[:, :], kcol("maskneg"))
                    nc.vector.tensor_copy(onehoth[:, :], kcol("onehot", 64))
                    nc.vector.tensor_copy(delta2h[:, :, :],
                                          kcol("delta2", 2 * FI).unsqueeze(1).broadcast_to([2 * FI, GB, FI]))
                    dve.wait_ge(s_pch, 1)
                    link(nc.vector.tensor_scalar(v[:, 10:11], pa[:, 0, 0:1], -1.0, 1.0, ALU.mult, ALU.add))
                    link(nc.vector.reciprocal(v[:, 11:12], v[:, 10:11]))
                    link(nc.vector.tensor_scalar(v[:, 12:13], v[:, 11:12], 1.0 / P, None, ALU.mult))
                    link(nc.vector.tensor_tensor(v[:, 13:14], v[:, 12:13], nodc, ALU.mult))
                    link(nc.vector.tensor_scalar(casd[:, 0, :], cas, v[:, 12:13], None, ALU.mult))
                    link(nc.vector.tensor_scalar(casd[:, 1, :], cas, v[:, 13:14], None, ALU.mult))
                    dve.wait_ge(s_wtr, 1)
                    nc.vector.tensor_copy(wsqT[:, 0:4, :], pa[:, 2, :].rearrange("p (a c) -> p a c", a=4))\
                        .then_inc(s_wtc, 1)
                    link(nc.vector.tensor_scalar(wsqT[:, 4, :], pa[:, 3, 0:128], WS, None, ALU.mult))
                    dve.wait_ge(s_pch, 2)
                    nc.vector.tensor_copy(cw[:, :], pa[:, 1, 128:256]).then_inc(s_inv, 1)
                    nc.vector.tensor_scalar(wbig[:, 0:C], pa[:, 1, 0:128], WSI, None, ALU.mult)
                    link(nc.vector.tensor_copy(gfh[:, :], wsqT[:, 4, :]))
                    dve.wait_ge(s_wtc, 1)
                    nc.vector.tensor_scalar(woT[:, :], wsqT[:, 3, :], WSI, None, ALU.mult)
                    link(nc.vector.tensor_tensor(gfl[:, :], wsqT[:, 4, :], gfh[:, :], ALU.subtract))
                    dve.wait_ge(s_pch, 3)
                    nc.vector.tensor_scalar(wbig[:, C:3 * C], pa[:, 4, 0:2 * C], WSI, None, ALU.mult)
                    link(nc.vector.tensor_scalar(wbig[:, 3 * C:4 * C], pa[:, 4, 2 * C:3 * C], WSI * VS, None, ALU.mult))
                    link(nc.vector.tensor_copy(wh[:, :], wbig[:, :]))
                    link(nc.vector.tensor_tensor(wl[:, :], wbig[:, :], wh[:, :], ALU.subtract))

                @block.gpsimd
                def _(pool):
                    pool.wait_ge(s_dch, 5)
                    nc.gpsimd.tensor_tensor(v[:, 4:5], v[:, 14:15], kc[:, COL["mhalf"][0]:COL["mhalf"][0] + 1], ALU.pow)\
                        .then_inc(s_gch, 1)
                    for pair in range(TILES // 2):
                        nc.gpsimd.memset(yt[:, 2 * pair, 0:1], 0.0).then_inc(t1_stored[pair], 16)
                    nc.gpsimd.memset(sone[:, :, :], 1.0)
                    nc.gpsimd.memset(pk[:, :, :, :, :], 0.0)
                    nc.gpsimd.memset(vp[:, :, :, DH:DH + 1], VS).then_inc(ones_set, 1)

                @block.scalar
                def _(act):
                    act.wait_ge(s_dch, 3)
                    nc.scalar.activation(v[:, 9:10], v[:, 2:3], ACT.Exp, scale=-0.5).then_inc(s_ach, 1)
                    act.wait_ge(s_base, 32)
                    nc.scalar.activation(bwh[:, :, :], bw[:, :, :], ACT.Copy, scale=WS).then_inc(s_bhi, 1)

                @block.tensor
                def _(pe):
                    mm = nc.tensor.matmul
                    pe.wait_ge(s_dch, 9)
                    mm(pa[:, 0, 0:1], cas, v[:, 8:9], start=True, stop=True).then_inc(s_pch, 1)
                    pe.wait_ge(s_wts, 16 * 5)
                    for i in range(5):
                        last = nc.tensor.transpose(pa[:, 2 + i // 4, (i % 4) * 128:(i % 4) * 128 + 128], wsq[:, i, :],
                                                   ident)
                    last.then_inc(s_wtr, 1)
                    pe.wait_ge(s_dch, 15)
                    mm(pa[:, 1, 0:128], casd[:, 0, :], cas, start=True, stop=True)
                    mm(pa[:, 1, 128:256], casd[:, 1, :], cas, start=True, stop=True).then_inc(s_pch, 1)
                    pe.wait_ge(s_inv, 1)
                    pe.wait_ge(s_wtc, 1)
                    mm(pa[:, 4, 0:3 * C], cw[:, :], wsqT[:, 0:3, :].rearrange("p a c -> p (a c)"),
                       start=True, stop=True).then_inc(s_pch, 1)

        with early, ExitStack() as pa_:
            xh = sb(pa_, "x_hi", [P, 2, HALF * P], F16)
            xl = sb(pa_, "x_lo", [P, 2, HALF * P], F16)
            eq = sb(pa_, "exp_qk", [P, 4, 2 * C])
            rq = sb(pa_, "relu_qk", [P, 4, 2 * C])
            qk = sb(pa_, "qk_f32", [P, 4, 2 * C])
            qkT = sb(pa_, "qkT_parts", [P, 4, 2, NP, P], F16)
            ah = sb(pa_, "scores_hi", [P, 2, NH * P], F16)
            al = sb(pa_, "scores_lo", [P, 2, NH * P], F16)
            sm = sb(pa_, "state_f32", [P, 2, NP, 2 * VW])
            sp2 = sb(pa_, "state_parts", [P, 4, 2, NP, 2 * VW], F16)
            o_ = sb(pa_, "attn_out", [P, 2, C])
            oT = sb(pa_, "attn_outT", [P, 2, C])
            z_ = sb(pa_, "z", [P, 2, C])
            st = sb(pa_, "stats1", [P, 4, 16])
            st2 = sb(pa_, "stats2", [P, 4, 16])
            dn = sb(pa_, "denominators", [P, 2, 2, NH])
            gjunk = sb(pa_, "gate_hidden", [P, P])
            tvs = sb(pa_, "tv_share", [P, 2, TVW])

            p_in = pa_.enter_context(nc.psum_tensor("p_in", [P, 3 * C], F32))
            p_m1 = pa_.enter_context(nc.psum_tensor("p_m1", [P, 512], F32))
            p_tr = pa_.enter_context(nc.psum_tensor("p_tr", [P, 2, NP, P], F16))
            p_a = pa_.enter_context(nc.psum_tensor("p_a", [P, NH * P], F32))
            p_o = pa_.enter_context(nc.psum_tensor("p_o", [P, 512], F32))
            p_s = pa_.enter_context(nc.psum_tensor("p_s", [P, 512], F32))
            p_m2 = pa_.enter_context(nc.psum_tensor("p_m2", [P, 512], F32))
            num = p_o[:, 0:NH * VW].rearrange("p (h w) -> p h w", w=VW)
            sbank = p_s[:, 0:NP * 2 * VW].rearrange("p (a w) -> p a w", w=2 * VW)

            (xh_ready, xl_ready, conv_done, in_done, bn1, mv1, ve1, rstd1, vhi_ready, exp_ready, relu_ready, vlo_ready,
             qk_ready, hi_ready, lo_ready, tr_done, qkT_ready, su_done, sm_ready, sh_ready, sp_ready,
             av_done, den1, den2, o_ready, ot_done, oT_ready, wo_done,
             t1_ready, bn2, mv2, ve2, rstd2, zc_ready, z_ready, zt_done, zhi_ready, zlo_ready, gt_done, gate_ready) = [
                sem(s) for s in (
                    "xh_ready xl_ready conv_done in_done bn1 mv1 ve1 rstd1 vhi_ready exp_ready relu_ready vlo_ready "
                    "qk_ready hi_ready lo_ready tr_done qkT_ready su_done sm_ready sh_ready sp_ready "
                    "av_done den1 den2 o_ready ot_done oT_ready wo_done "
                    "t1_ready bn2 mv2 ve2 rstd2 zc_ready z_ready zt_done zhi_ready zlo_ready gt_done gate_ready").split()]

            sc_done, ahi_ready, alo_ready = [[sem(f"{name}_{eo}") for eo in range(2)] for name in
                                             ("sc_done", "ahi_ready", "alo_ready")]
            tv_loaded, tv_hi_ready, tv_split = sem("tv_loaded"), sem("tv_hi_ready"), sem("tv_split")

            def at_least(eng, s, value):
                if not isinstance(value, int) or value > 0:
                    eng.wait_ge(s, value)

            def batch(stages, b, old=True, new=True):
                for slot in range(TILES):
                    for k, stage_ in stages:
                        t = slot - k
                        if t >= 0 and new:
                            stage_(b, t)
                        elif t < 0 and old:
                            stage_(b - 1, t + TILES)

            def run(eng, order, stages):
                stages = [(skew, stages[name]) for name, skew in order]
                batch(stages, 0, old=False)
                with eng.Fori(1, B) as b:
                    batch(stages, b)
                batch(stages, B, new=False)

            def cap(n):
                return min(n, NT) if isinstance(n, int) else n

            with nc.Block() as block:
                @block.sync
                def _(sp):
                    def load(b, hf):
                        q = 2 * b + hf
                        at_least(sp, xh_ready, 2 * (q - 1))
                        at_least(sp, xl_ready, 2 * (q - 1))
                        sp.dma_start(xf[:, hf, :], d["x"][bass.ds(b * P, P), hf * HALF * P:(hf + 1) * HALF * P])\
                            .then_inc(x_loaded[hf], 16)

                    def load_tv(b):
                        if not isinstance(b, int):
                            sp.wait_ge(tv_split, b)
                        for i, src in enumerate((d["L1_ffn_tv_W1"].rearrange("e (i o) d -> (e i) (o d)", i=FI),
                                                 d["L1_ffn_tv_W2"].rearrange("e (i o) f -> (e i) (o f)", i=FI))):
                            sp.dma_start(tvs[:, i, :], src[:, bass.ds(b * TVW, TVW)]).then_inc(tv_loaded, 16)

                    def store(b, pair):
                        hf, i = pair // 2, pair % 2
                        sp.wait_ge(t1_ready, TILES * b + 2 * (pair + 1))
                        sp.dma_start(d["t1"][bass.ds((2 * b + hf) * P, P), 2 * C * i:2 * C * (i + 1)],
                                     yt[:, 2 * pair:2 * pair + 2, :].rearrange("p a c -> p (a c)"))\
                            .then_inc(t1_stored[pair], 16)

                    load_tv(0)
                    for part, (done, src) in enumerate(((s_bhi, bwh), (s_blo, bwl))):
                        sp.wait_ge(done, 1)
                        sp.dma_start(d["base_parts"][part].rearrange("i p w -> p i w"), src[:, :, :])\
                            .then_inc(base_stored, 16)
                    sp.dma_start(g2n[:, :], d["L1_ffn_gfc2_w"]).then_inc(s_small, 16)
                    for dst, tvn, base in ((l9g, "tv_ln_g", "ln_g"), (l9b, "tv_ln_b", "ln_b"),
                                           (t9b1, "tv_b1", "b1"), (t9b2, "tv_b2", "b2")):
                        sp.dma_start(dst[0:E, :], d["L1_ffn_" + tvn]).then_inc(s_small, 16)
                        sp.dma_start(dst[E:E + 1, :], d["L1_ffn_" + base].unsqueeze(0)).then_inc(s_small, 16)
                    sp.dma_start(gf1b[:, :], d["L1_ffn_gfc1_b"].unsqueeze(1)).then_inc(s_small, 16)
                    sp.dma_start(gf2b[:, :], d["L1_ffn_gfc2_b"].unsqueeze(1)).then_inc(s_small, 16)
                    for e in range(E):
                        sp.dma_start(gf2brep[e * FI:(e + 1) * FI, :],
                                     d["L1_ffn_gfc2_b"][e:e + 1].partition_broadcast(FI)).then_inc(s_small, 16)
                    sp.wait_ge(base_stored, 32)
                    for i, rows in enumerate((w1s, w2s)):
                        for part in range(2):
                            sp.dma_start(rows[part * FI:(part + 1) * FI, :],
                                         d["base_parts"][part, i].rearrange("(a r) w -> a (r w)", a=FI))\
                                .then_inc(base_placed, 16)
                    with sp.Fori(1, B) as b:
                        load(b, 0)
                        load_tv(b)
                        store(b - 1, 0)
                        store(b - 1, 1)
                        load(b, 1)
                        store(b - 1, 2)
                        store(b - 1, 3)
                    for pair in range(TILES // 2):
                        store(B - 1, pair)
                    for pair in range(TILES // 2):
                        sp.wait_ge(t1_stored[pair], 16 * (B + 1))

                @block.tensor
                def _(pe):
                    mm = nc.tensor.matmul

                    banks = [{"conv": (bn1,), "out_project": (t1_ready,), "gate": (gate_ready,)},
                             {"turn_out": (oT_ready,), "turn_z": (zhi_ready, zlo_ready)}]

                    def bank_read(stage, n):
                        uses = [u for u in banks if stage in u][0]
                        order = [name for name, _ in TENSOR_ORDER if name in uses]
                        previous = order[order.index(stage) - 1]
                        assert TILES - dict(TENSOR_ORDER)[stage] - before(stage, previous) + 1 > 0
                        if isinstance(n, int):
                            for other, read in uses.items():
                                for s_ in read:
                                    at_least(pe, s_, cap(n - before(stage, other) + 1))
                        else:
                            for s_ in uses[previous]:
                                pe.wait_ge(s_, n - before(stage, previous) + 1)

                    def conv(b, t):
                        n = TILES * b + t
                        hf, j = t // HALF, t % HALF
                        if j % 2 == 0:
                            pe.wait_ge(xh_ready, TILES // 2 * b + t // 2 + 1)
                            pe.wait_ge(xl_ready, TILES // 2 * b + t // 2 + 1)
                        bank_read("conv", n)
                        o, cols = p_m1[:, 2 * P:3 * P], slice(j * P, (j + 1) * P)
                        mm(o, xh[:, hf, cols], wh[:, 0:C], start=True, stop=False)
                        mm(o, xh[:, hf, cols], wl[:, 0:C], start=False, stop=False)
                        mm(o, xl[:, hf, cols], wh[:, 0:C], start=False, stop=True).then_inc(conv_done, 1)

                    def project(b, t):
                        n = TILES * b + t
                        hf, j = t // HALF, t % HALF
                        if j % 2 == 0:
                            pe.wait_ge(xh_ready, TILES // 2 * b + t // 2 + 1)
                            pe.wait_ge(xl_ready, TILES // 2 * b + t // 2 + 1)
                        at_least(pe, exp_ready, n)
                        at_least(pe, relu_ready, n)
                        at_least(pe, vlo_ready, n)
                        cols = slice(j * P, (j + 1) * P)
                        mm(p_in[:, :], xh[:, hf, cols], wh[:, C:4 * C], start=True, stop=False)
                        mm(p_in[:, :], xh[:, hf, cols], wl[:, C:4 * C], start=False, stop=False)
                        mm(p_in[:, :], xl[:, hf, cols], wh[:, C:4 * C], start=False, stop=True).then_inc(in_done, 1)

                    def state(b, t):
                        if t == TILES - 1:
                            return
                        n = TILES * b + t
                        pe.wait_ge(lo_ready, n + 1)
                        pe.wait_ge(hi_ready, n + 1)
                        pe.wait_ge(vlo_ready, n + 1)
                        pe.wait_ge(vhi_ready, n + 1)
                        if n == 0 if isinstance(n, int) else False:
                            pe.wait_ge(ones_set, 1)
                        at_least(pe, sm_ready, (TILES - 1) * b + t)
                        for a in range(NP):
                            kk = pk[:, t % 4, 1, 2 * a:2 * a + 2, :].rearrange("p h c -> p (h c)")
                            mm(sbank[:, a, :], kk, vp[:, t, 2 * a:2 * a + 2, 0:VW],
                               start=(t == 0 and a == 0), stop=False, skip_group_check=True)
                            last = mm(sbank[:, a, :].rearrange("p (h w) -> p h w", w=VW)[:, :, 0:DH], kk,
                                      vp[:, t, 2 * a:2 * a + 2, VW:VW + DH],
                                      start=False, stop=True, skip_group_check=True)
                        last.then_inc(su_done, 1)

                    def turn(b, t):
                        n = TILES * b + t
                        pe.wait_ge(lo_ready, n + 1)
                        pe.wait_ge(hi_ready, n + 1)
                        at_least(pe, qkT_ready, n)
                        for w in range(2):
                            for a in range(NP):
                                last = nc.tensor.transpose(
                                    p_tr[:, w, a, :], pk[:, t % 4, w, 2 * a:2 * a + 2, :].rearrange("p h c -> p (h c)"),
                                    identh[:, :])
                        last.then_inc(tr_done, 1)

                    def scores(eo):
                        def stage_(b, t):
                            n = TILES * b + t
                            pe.wait_ge(qkT_ready, n + 1)
                            at_least(pe, ahi_ready[eo], n)
                            at_least(pe, alo_ready[eo], n)
                            bank, r = p_a[:, eo * 512:(eo + 1) * 512], 64 * eo
                            mm(bank, identb[:, :], maskb[:, :].unsqueeze(1).broadcast_to([P, NP, P]),
                               start=True, stop=False, skip_group_check=True)
                            for a in range(NP):
                                last = mm(bank[:, a * P:(a + 1) * P],
                                          qkT[r:r + 64, t % 4, 1, a, :], qkT[r:r + 64, t % 4, 0, a, :],
                                          start=False, stop=True, skip_group_check=True)
                            last.then_inc(sc_done[eo], 1)
                        return stage_

                    def values(b, t):
                        n = TILES * b + t
                        for eo in range(2):
                            pe.wait_ge(ahi_ready[eo], n + 1)
                            pe.wait_ge(alo_ready[eo], n + 1)
                        at_least(pe, o_ready, n)
                        if t:
                            pe.wait_ge(sp_ready, (TILES - 1) * b + t)
                        for h in range(NH):
                            c0 = (h % 2) * 512 + (h // 2) * P
                            hi, lo = ah[:, t % 2, c0:c0 + P], al[:, t % 2, c0:c0 + P]
                            mm(num[:, h, :], hi, vp[:, t, h, 0:VW], start=(h == 0), stop=False,
                               skip_group_check=True)
                            mm(num[:, h, 0:DH], hi, vp[:, t, h, VW:VW + DH], start=False, stop=False,
                               skip_group_check=True)
                            last = mm(num[:, h, :], lo, vp[:, t, h, 0:VW], start=False, stop=True,
                                      skip_group_check=True)
                        if t:
                            for a in range(NP):
                                for part in range(2):
                                    last = mm(p_o[:, 2 * VW * a:2 * VW * (a + 1)], qkT[:, t % 4, 0, a, :],
                                              sp2[:, (t - 1) % 4, part, a, :], start=False, stop=True,
                                              skip_group_check=True)
                        last.then_inc(av_done, 1)

                    def turn_out(b, t):
                        n = TILES * b + t
                        pe.wait_ge(o_ready, n + 1)
                        bank_read("turn_out", n)
                        nc.tensor.transpose(p_m2[:, 0:P], o_[:, t % 2, :], ident).then_inc(ot_done, 1)

                    def out_project(b, t):
                        n = TILES * b + t
                        hf, j = t // HALF, t % HALF
                        bank_read("out_project", n)
                        o, cols = p_m1[:, 0:P], slice(j * P, (j + 1) * P)
                        mm(o, xh[:, hf, cols], wh[:, 0:C], start=True, stop=False)
                        mm(o, xh[:, hf, cols], wl[:, 0:C], start=False, stop=False)
                        mm(o, xl[:, hf, cols], wh[:, 0:C], start=False, stop=False)
                        pe.wait_ge(oT_ready, n + 1)
                        mm(o, oT[:, t % 2, :], woT[:, :], start=False, stop=True).then_inc(wo_done, 1)

                    def turn_z(b, t):
                        n = TILES * b + t
                        pe.wait_ge(z_ready, n + 1)
                        bank_read("turn_z", n)
                        nc.tensor.transpose(p_m2[:, P:2 * P], z_[:, t % 2, :], ident).then_inc(zt_done, 1)

                    def gate(b, t):
                        n = TILES * b + t
                        pe.wait_ge(zhi_ready, n + 1)
                        pe.wait_ge(zlo_ready, n + 1)
                        bank_read("gate", n)
                        g = p_m1[:, P:2 * P]
                        hi, lo = zh[:, bass.ds(n * P, P)], zl[:, bass.ds(n * P, P)]
                        mm(g, gfh[:, :], hi, start=True, stop=False)
                        mm(g, gfl[:, :], hi, start=False, stop=False)
                        mm(g, gfh[:, :], lo, start=False, stop=True).then_inc(gt_done, 1)

                    pe.wait_ge(ones_set, 1)
                    run(pe, TENSOR_ORDER, {"conv": conv, "project": project, "state": state, "turn": turn,
                        "scores_0": scores(0), "scores_1": scores(1),
                        "values": values, "turn_out": turn_out, "out_project": out_project, "turn_z": turn_z,
                        "gate": gate})

                    pe.wait_ge(exp_ready, NT)
                    pe.wait_ge(relu_ready, NT)
                    pe.wait_ge(vlo_ready, NT)
                    pe.wait_ge(s_small, NSMALL)
                    nc.tensor.transpose(p_in[:, 0:E], g2n[:, :], kc[0:E, COL["ident"][0]:COL["ident"][0] + E])
                    mm(p_in[:, C:2 * C], kcol("lncoef", E + 1), l9g[:, :], start=True, stop=True)
                    mm(p_in[:, 2 * C:2 * C + 1], l9b[:, :], kc[0:E + 1, COL["lncoef"][0]:COL["lncoef"][0] + 1],
                       start=True, stop=True).then_inc(ln_done, 1)

                @block.scalar
                def _(act):
                    def split_x(b, t):
                        if t % 2:
                            return
                        n = TILES * b + t
                        hf, j = t // HALF, t % HALF
                        if j == 0:
                            act.wait_ge(x_loaded[hf], 16 * (b + 1))
                        at_least(act, wo_done, n - TILES + 2)
                        cols = slice(j * P, (j + 2) * P)
                        nc.scalar.activation(xh[:, hf, cols], xf[:, hf, cols], ACT.Copy).then_inc(xh_ready, 1)

                    def tv_hi(b, t):
                        if t:
                            return
                        act.wait_ge(ones_set, 1)
                        act.wait_ge(tv_loaded, 32 * (b + 1))
                        nc.scalar.activation(tv[0][:, :, bass.ds(b * TVW, TVW)], tvs[:, :, :], ACT.Copy, scale=WS)\
                            .then_inc(tv_hi_ready, 1)

                    def read_t1(b, t):
                        n = TILES * b + t
                        if t % 2 == 0:
                            act.wait_ge(t1_stored[t // 2], 16 * (b + 1))
                        at_least(act, z_ready, n - 1)
                        act.wait_ge(wo_done, n + 1)
                        nc.scalar.activation(yt[:, t, :], p_m1[:, 0:P], ACT.Copy, scale=1.0 / WSI).then_inc(t1_ready, 1)

                    def v_hi(b, t):
                        n = TILES * b + t
                        act.wait_ge(rstd1, n + 1)
                        act.wait_ge(in_done, n + 1)
                        at_least(act, av_done, n - TILES + 2)
                        nc.scalar.activation(vp[:, t, :, 0:DH],
                                             p_in[:, 2 * C:3 * C].rearrange("p (h i) -> p h i", i=DH),
                                             ACT.Copy, scale=st[:, t % 4, 8:9]).then_inc(vhi_ready, 1)

                    def exp_qk(b, t):
                        n = TILES * b + t
                        act.wait_ge(rstd1, n + 1)
                        act.wait_ge(in_done, n + 1)
                        at_least(act, qk_ready, n - 3)
                        nc.scalar.activation(eq[:, t % 4, :], p_in[:, 0:2 * C], ACT.Exp, scale=st[:, t % 4, 8:9])\
                            .then_inc(exp_ready, 1)

                    def relu_qk(b, t):
                        n = TILES * b + t
                        act.wait_ge(rstd1, n + 1)
                        act.wait_ge(in_done, n + 1)
                        at_least(act, qk_ready, n - 3)
                        nc.scalar.activation(rq[:, t % 4, :], p_in[:, 0:2 * C], ACT.Relu, scale=st[:, t % 4, 8:9])\
                            .then_inc(relu_ready, 1)

                    def copy_out(b, t):
                        n = TILES * b + t
                        act.wait_ge(ot_done, n + 1)
                        at_least(act, wo_done, n - 1)
                        nc.scalar.activation(oT[:, t % 2, :], p_m2[:, 0:P], ACT.Copy).then_inc(oT_ready, 1)

                    def copy_qk(b, t):
                        n = TILES * b + t
                        act.wait_ge(tr_done, n + 1)
                        at_least(act, av_done, n - 3)
                        nc.scalar.activation(qkT[:, t % 4, :, :, :].rearrange("p w a c -> p (w a c)"),
                                             p_tr[:, :, :, :].rearrange("p w a c -> p (w a c)"), ACT.Copy)\
                            .then_inc(qkT_ready, 1)

                    def scores_hi(eo):
                        def stage_(b, t):
                            n = TILES * b + t
                            at_least(act, av_done, n - 1)
                            act.wait_ge(sc_done[eo], n + 1)
                            cols = slice(eo * 512, (eo + 1) * 512)
                            nc.scalar.activation(ah[:, t % 2, cols], p_a[:, cols], ACT.Relu).then_inc(ahi_ready[eo], 1)
                        return stage_

                    def z_hi(b, t):
                        n = TILES * b + t
                        act.wait_ge(ones_set, 1)
                        act.wait_ge(zt_done, n + 1)
                        nc.scalar.activation(zh[:, bass.ds(n * P, P)], p_m2[:, P:2 * P], ACT.Copy).then_inc(zhi_ready, 1)

                    def gate_relu(b, t):
                        n = TILES * b + t
                        if isinstance(n, int) and n == 0:
                            act.wait_ge(s_small, NSMALL)
                        act.wait_ge(ones_set, 1)
                        act.wait_ge(gt_done, n + 1)
                        nc.scalar.activation(gjunk[:, :], p_m1[:, P:2 * P], ACT.Relu, bias=gf1b[:, 0:1], scale=1.0 / WS,
                                             accum_out=ghs[:, bass.ds(n, 1)]).then_inc(gate_ready, 1)

                    run(act, SCALAR_ORDER, {"tv_hi": tv_hi, "split_x": split_x, "read_t1": read_t1, "v_hi": v_hi,
                        "exp_qk": exp_qk, "relu_qk": relu_qk, "copy_qk": copy_qk,
                        "scores_hi_0": scores_hi(0), "scores_hi_1": scores_hi(1),
                        "copy_out": copy_out, "z_hi": z_hi, "gate_relu": gate_relu})

                @block.vector
                def _(dve):
                    def stats1(b, t):
                        n = TILES * b + t
                        dve.wait_ge(conv_done, n + 1)
                        nc.vector.bn_stats(st[:, t % 4, 0:6], p_m1[:, 2 * P:3 * P]).then_inc(bn1, 1)

                    def mean_var1(b, t):
                        n = TILES * b + t
                        dve.wait_ge(ones_set, 1)
                        dve.wait_ge(bn1, n + 1)
                        nc.vector.bn_aggr(st[:, t % 4, 6:8], st[:, t % 4, 0:6]).then_inc(mv1, 1)

                    def tv_lo(b, t):
                        if t:
                            return
                        dve.wait_ge(tv_hi_ready, b + 1)
                        cols = bass.ds(b * TVW, TVW)
                        nc.vector.scalar_tensor_tensor(tv[1][:, :, cols], tvs[:, :, :], WS, tv[0][:, :, cols],
                                                       ALU.mult, ALU.subtract).then_inc(tv_split, 1)

                    def eps1(b, t):
                        n = TILES * b + t
                        dve.wait_ge(mv1, n + 1)
                        nc.vector.tensor_scalar(st[:, t % 4, 9:10], st[:, t % 4, 7:8], EPS * WSI * WSI, None, ALU.add)\
                            .then_inc(ve1, 1)

                    def eps2(b, t):
                        n = TILES * b + t
                        dve.wait_ge(mv2, n + 1)
                        nc.vector.tensor_scalar(st2[:, t % 4, 9:10], st2[:, t % 4, 7:8], EPS, None, ALU.add)\
                            .then_inc(ve2, 1)

                    def v_lo(b, t):
                        n = TILES * b + t
                        dve.wait_ge(vhi_ready, n + 1)
                        dve.wait_ge(exp_ready, n + 1)
                        dve.wait_ge(relu_ready, n + 1)
                        nc.vector.scalar_tensor_tensor(
                            vp[:, t, :, VW:VW + DH], p_in[:, 2 * C:3 * C].rearrange("p (h i) -> p h i", i=DH),
                            st[:, t % 4, 8:9], vp[:, t, :, 0:DH], ALU.mult, ALU.subtract).then_inc(vlo_ready, 1)

                    def make_qk(b, t):
                        n = TILES * b + t
                        dve.wait_ge(exp_ready, n + 1)
                        dve.wait_ge(relu_ready, n + 1)
                        at_least(dve, lo_ready, n - 3)
                        nc.vector.scalar_tensor_tensor(qk[:, t % 4, :], eq[:, t % 4, :], 1.0, rq[:, t % 4, :],
                                                       ALU.min, ALU.add).then_inc(qk_ready, 1)

                    def qk_hi(b, t):
                        n = TILES * b + t
                        dve.wait_ge(qk_ready, n + 1)
                        at_least(dve, tr_done, n - 3)
                        for w in range(2):
                            src = qk[:, t % 4, w * C:(w + 1) * C].rearrange("p (h i) -> p h i", i=DH)
                            dst = pk[:, t % 4, w, :, :].rearrange("p h (a b i) -> p h a b i", a=2, b=2)
                            dst = dst[:, :, :, 0, :] if w == 0 else dst[:, :, 0, :, :]
                            last = nc.vector.tensor_copy(dst, src.unsqueeze(2).broadcast_to([P, NH, 2, DH]))
                        last.then_inc(hi_ready, 1)

                    def read_state(b, t):
                        if t == TILES - 1:
                            return
                        m = (TILES - 1) * b + t
                        dve.wait_ge(su_done, m + 1)
                        at_least(dve, sp_ready, m if t == 0 else m - 1)
                        nc.vector.tensor_tensor(sm[:, t % 2, :, :], sbank,
                                                kcol("blk").unsqueeze(1).broadcast_to([P, NP, 2 * VW]), ALU.mult)\
                            .then_inc(sm_ready, 1)

                    def scores_lo(eo):
                        def stage_(b, t):
                            n = TILES * b + t
                            at_least(dve, av_done, n - 1)
                            dve.wait_ge(ahi_ready[eo], n + 1)
                            cols = slice(eo * 512, (eo + 1) * 512)
                            nc.vector.scalar_tensor_tensor(al[:, t % 2, cols], p_a[:, cols], 0.0, ah[:, t % 2, cols],
                                                           ALU.max, ALU.subtract).then_inc(alo_ready[eo], 1)
                        return stage_

                    def denominator(b, t):
                        n = TILES * b + t
                        dve.wait_ge(av_done, n + 1)
                        nc.vector.tensor_scalar(dn[:, t % 2, 0, :], num[:, :, DH], 1e-6 * VS, None, ALU.max)\
                            .then_inc(den1, 1)

                    def invert(b, t):
                        n = TILES * b + t
                        dve.wait_ge(den1, n + 1)
                        nc.vector.reciprocal(dn[:, t % 2, 1, :], dn[:, t % 2, 0, :]).then_inc(den2, 1)

                    def divide(b, t):
                        n = TILES * b + t
                        dve.wait_ge(den2, n + 1)
                        at_least(dve, ot_done, n - 1)
                        nc.vector.tensor_tensor(o_[:, t % 2, :].rearrange("p (h i) -> p h i", i=DH), num[:, :, 0:DH],
                                                dn[:, t % 2, 1, :].unsqueeze(2).broadcast_to([P, NH, DH]), ALU.mult)\
                            .then_inc(o_ready, 1)

                    def stats2(b, t):
                        n = TILES * b + t
                        dve.wait_ge(t1_ready, n + 1)
                        nc.vector.bn_stats(st2[:, t % 4, 0:6], yt[:, t, :]).then_inc(bn2, 1)

                    def mean_var2(b, t):
                        n = TILES * b + t
                        dve.wait_ge(ones_set, 1)
                        dve.wait_ge(bn2, n + 1)
                        nc.vector.bn_aggr(st2[:, t % 4, 6:8], st2[:, t % 4, 0:6]).then_inc(mv2, 1)

                    def z_lo(b, t):
                        n = TILES * b + t
                        dve.wait_ge(zhi_ready, n + 1)
                        cols = bass.ds(n * P, P)
                        nc.vector.tensor_tensor(zl[:, cols], p_m2[:, P:2 * P], zh[:, cols], ALU.subtract)\
                            .then_inc(zlo_ready, 1)

                    dve.wait_ge(s_bhi, 1)
                    nc.vector.scalar_tensor_tensor(bwl[:, :, :], bw[:, :, :], WS, bwh[:, :, :], ALU.mult, ALU.subtract)\
                        .then_inc(s_blo, 1)
                    run(dve, VECTOR_ORDER, {"tv_lo": tv_lo, "stats1": stats1, "mean_var1": mean_var1, "v_lo": v_lo,
                        "make_qk": make_qk, "qk_hi": qk_hi, "read_state": read_state,
                        "scores_lo_0": scores_lo(0), "scores_lo_1": scores_lo(1), "denominator": denominator,
                        "invert": invert, "divide": divide,
                        "stats2": stats2, "mean_var2": mean_var2, "eps1": eps1, "eps2": eps2,
                        "z_lo": z_lo})

                    dve.wait_ge(ln_done, 1)
                    nc.vector.tensor_copy(gf2T[:, :], p_in[:, 0:E]).then_inc(g2_ready, 1)
                    nc.vector.tensor_copy(lng[:, :], p_in[:, C:2 * C])
                    nc.vector.tensor_copy(lnb[:, :], p_in[:, 2 * C:2 * C + 1])
                    dve.wait_ge(g2_ready, 1)
                    nc.vector.tensor_copy(gf2rep[:, :, :], gf2T[:, :].unsqueeze(2).broadcast_to([P, E, FI]))

                @block.gpsimd
                def _(pool):
                    mhalf = kc[:, COL["mhalf"][0]:COL["mhalf"][0] + 1]

                    def rsqrt1(b, t):
                        n = TILES * b + t
                        s = st[:, t % 4, :]
                        pool.wait_ge(ve1, n + 1)
                        nc.gpsimd.tensor_tensor(s[:, 8:9], s[:, 9:10], mhalf, ALU.pow).then_inc(rstd1, 1)

                    def rsqrt2(b, t):
                        n = TILES * b + t
                        s = st2[:, t % 4, :]
                        pool.wait_ge(ve2, n + 1)
                        nc.gpsimd.tensor_tensor(s[:, 8:9], s[:, 9:10], mhalf, ALU.pow).then_inc(rstd2, 1)

                    def qk_lo(b, t):
                        n = TILES * b + t
                        pool.wait_ge(hi_ready, n + 1)
                        for w in range(2):
                            src = qk[:, t % 4, w * C:(w + 1) * C].rearrange("p (h i) -> p h i", i=DH)
                            lo = pk[:, t % 4, w, :, (1 + w) * DH:(2 + w) * DH]
                            last = nc.gpsimd.tensor_tensor(lo, src, pk[:, t % 4, w, :, 0:DH], ALU.subtract)
                        last.then_inc(lo_ready, 1)

                    def state_hi(b, t):
                        if t == TILES - 1:
                            return
                        m = (TILES - 1) * b + t
                        pool.wait_ge(sm_ready, m + 1)
                        at_least(pool, av_done, TILES * b + t - 2)
                        nc.gpsimd.tensor_tensor(sp2[:, t % 4, 0, :, :], sm[:, t % 2, :, :], sone[:, :, :], ALU.mult)\
                            .then_inc(sh_ready, 1)

                    def state_lo(b, t):
                        if t == TILES - 1:
                            return
                        pool.wait_ge(sh_ready, (TILES - 1) * b + t + 1)
                        nc.gpsimd.tensor_tensor(sp2[:, t % 4, 1, :, :], sm[:, t % 2, :, :], sp2[:, t % 4, 0, :, :],
                                                ALU.subtract).then_inc(sp_ready, 1)

                    def split_x(b, t):
                        if t % 2:
                            return
                        hf, j = t // HALF, t % HALF
                        cols = slice(j * P, (j + 2) * P)
                        pool.wait_ge(xh_ready, TILES // 2 * b + t // 2 + 1)
                        nc.gpsimd.tensor_tensor(xl[:, hf, cols], xf[:, hf, cols], xh[:, hf, cols], ALU.subtract)\
                            .then_inc(xl_ready, 1)

                    def centre(b, t):
                        n = TILES * b + t
                        pool.wait_ge(mv2, n + 1)
                        at_least(pool, zt_done, n)
                        nc.gpsimd.tensor_tensor(z_[:, t % 2, :], yt[:, t, :],
                                                st2[:, t % 4, 6:7].broadcast_to([P, C]), ALU.subtract)\
                            .then_inc(zc_ready, 1)

                    def normalise(b, t):
                        n = TILES * b + t
                        pool.wait_ge(zc_ready, n + 1)
                        pool.wait_ge(rstd2, n + 1)
                        nc.gpsimd.tensor_tensor(z_[:, t % 2, :], z_[:, t % 2, :],
                                                st2[:, t % 4, 8:9].broadcast_to([P, C]), ALU.mult)\
                            .then_inc(z_ready, 1)

                    run(pool, GPSIMD_ORDER, {"rsqrt1": rsqrt1, "qk_lo": qk_lo,
                        "state_hi": state_hi, "state_lo": state_lo, "split_x": split_x,
                        "rsqrt2": rsqrt2,
                        "centre": centre, "normalise": normalise})

        with ExitStack() as pb:
            grep = sb(pb, "gate_by_row", [P, B])
            g9 = sb(pb, "gate_and_one", [E + 1, B])
            gsum = sb(pb, "gate_hidden_batch_sums", [P, B])
            gbf = sb(pb, "gate_blocks_f32", [P, B, FI])
            gbh = sb(pb, "gate_blocks_hi", [P, B, FI], F16)
            gbl = sb(pb, "gate_blocks_lo", [P, B, FI], F16)
            b1m = sb(pb, "merged_b1", [P, FC, B])
            b1s = sb(pb, "merged_b1_of_batch", [P, 2, FC])
            b2s = sb(pb, "merged_b2_rows", [64, C], F16)
            b2f = sb(pb, "merged_b2_f32", [B, C])
            wm1 = [sb(pb, f"merged_W1_{s}", [P, GB * F], F16) for s in ("hi", "lo")]
            wm2 = [sb(pb, f"merged_W2_{s}", [P, FC, GB * C], F16) for s in ("hi", "lo")]
            zs = sb(pb, "zT_of_half", [P, 2, 2, 512], F16)
            w2b = sb(pb, "merged_W2_of_batch", [P, 2, 2, FC, C], F16)
            ohb = sb(pb, "onehot_of_batch", [64, 2, P], F16)
            hf_ = sb(pb, "h_f32", [P, FC, 512])
            hh = sb(pb, "h_hi", [P, 2, FC, 512], F16)
            hl = sb(pb, "h_lo", [P, 2, FC, 512], F16)
            t1b = sb(pb, "t1_back", [P, 2, HALF, C])
            rn = sb(pb, "normed", [P, 2, HALF, C])
            rs = sb(pb, "ffn_stats", [P, 2, HALF, 6])
            rmv = sb(pb, "ffn_mean_var", [P, 2, HALF, 2])
            rr = sb(pb, "ffn_rstd_shift", [P, 2, 3, HALF])
            ob = sb(pb, "out_tile", [P, 2, 512])
            ps = pb.enter_context(nc.psum_tensor("psb", [P, 8, 512], F32))

            (b1_ready, gs_ready, g_done, g9r, b12_done, b_chain, gb_ready, mg_done, mhi_ready, mlo_ready,
             z_copied, w2_copied, f2_done, fbn, fmv, fve, frs, fsh, n_ready, gain_ready, v_ready,
             t_done, ob_ready) = [sem(s) for s in (
                "b1_ready gs_ready g_done g9_ready b12_done b_chain gb_ready mg_done mhi_ready mlo_ready "
                "z_copied w2_copied f2_done fbn fmv fve frs fsh n_ready gain_ready v_ready "
                "t_done ob_ready").split()]
            up_done, h_ready, hhi_ready, hlo_ready = [[sem(f"{s}_{c}") for c in range(FC)] for s in
                                                      ("up_done", "h_ready", "hhi_ready", "hlo_ready")]
            b2_cleared = sem("b2_rows_cleared")
            t1_loaded = [sem(f"t1_loaded_{i}") for i in range(2)]
            out_stored = [sem(f"out_stored_{i}") for i in range(2)]
            NB_ = 16
            NQ = 2 * GB

            def at_least(eng, s, value):
                if not isinstance(value, int) or value > 0:
                    eng.wait_ge(s, value)

            HB = 4

            MERGE_PARTS = [range(0, 7), range(7, 12), range(12, NB_)]

            def run(eng, g, order, stages, merge_next=None):
                stages = [(skew, stages[name]) for name, skew in order]
                for slot in range(HB):
                    for k, stage_ in stages:
                        if slot >= k:
                            stage_(g, 0, slot - k)
                with eng.Fori(1, NQ // HB) as pair:
                    for slot in range(HB):
                        for k, stage_ in stages:
                            stage_(g, pair + (slot - k) // HB, (slot - k) % HB)
                for slot in range(NQ, NQ + HB - 1):
                    for k, stage_ in stages:
                        if slot - k < NQ:
                            stage_(g, (slot - k) // HB, (slot - k) % HB)
                    if merge_next and g + 1 < NG:
                        merge_next(g + 1, MERGE_PARTS[slot - NQ])

            def merged_views(kind, i, part):
                src = ps[:, i % 4, :].rearrange("p (j m) -> p m j", j=4)
                if kind == 0:
                    dst = wm1[part][:, :].rearrange("p (m o) -> p m o", o=FO)[:, :, 4 * i:4 * i + 4]
                else:
                    dst = wm2[part][:, i // 2, :].rearrange("p (m o) -> p m o", o=DO)
                    dst = dst[:, :, 4 * (i % 2):4 * (i % 2) + 4]
                return src, dst

            with nc.Block() as block:
                @block.sync
                def _(sp):
                    def load(g, bl, hf):
                        q = NQ * g + 2 * bl + hf
                        if not (isinstance(bl, int) and bl == 0):
                            sp.wait_ge(v_ready, q - 1)
                        sp.dma_start(t1b[:, hf, :, :].rearrange("p a c -> p (a c)"), d["t1"][bass.ds(q * P, P), :])\
                            .then_inc(t1_loaded[hf], 16)

                    def store(g, bl, hf):
                        b = GB * g + bl
                        sp.wait_ge(ob_ready, 2 * b + hf + 1)
                        sp.dma_start(d["out"][bass.ds(b * P, P), hf * 512:(hf + 1) * 512], ob[:, hf, :])\
                            .then_inc(out_stored[hf], 16)

                    for g in range(NG):
                        if g:
                            sp.wait_ge(v_ready, NQ * g)
                        load(g, 0, 0)
                        load(g, 0, 1)
                        with sp.Fori(1, GB) as bl:
                            for hf in range(2):
                                load(g, bl, hf)
                                store(g, bl - 1, hf)
                        store(g, GB - 1, 0)
                        store(g, GB - 1, 1)
                    sp.wait_ge(out_stored[0], 16 * (B + 1))
                    sp.wait_ge(out_stored[1], 16 * (B + 1))

                @block.tensor
                def _(pe):
                    mm = nc.tensor.matmul
                    pe.wait_ge(gs_ready, 1)
                    mm(ps[:, 4, 0:B], gf2rep[:, :, :].rearrange("p e i -> p (e i)"), gsum[:, :], start=True, stop=True)
                    mm(ps[0:E, 5, 0:B], gf2T[:, :], gsum[:, :], start=True, stop=True).then_inc(g_done, 1)

                    def merge_biases():
                        pe.wait_ge(g9r, 1)
                        for c in range(FC):
                            mm(ps[:, 6, c * B:(c + 1) * B], t9b1[:, c * P:(c + 1) * P], g9[:, :], start=(c == 0),
                               stop=True, skip_group_check=True)
                        mm(ps[0:B, 7, 0:C], g9[:, :], t9b2[:, :], start=True, stop=True).then_inc(b12_done, 1)

                    def merge(g, banks_):
                        for k in banks_:
                            kind, i = k // 8, k % 8
                            if k >= 4:
                                pe.wait_ge(mlo_ready, NB_ * g + k - 3)
                            elif g:
                                pe.wait_ge(h_ready[k], NQ * g)
                                pe.wait_ge(hhi_ready[k], NQ * g)
                            for j in range(4):
                                if kind == 0:
                                    c0 = (4 * i + j) * C
                                    th, tl, base = tv[0][:, 0, :], tv[1][:, 0, :], w1s
                                else:
                                    c0 = (4 * (i % 2) + j) * F + (i // 2) * P
                                    th, tl, base = tv[0][:, 1, :], tv[1][:, 1, :], w2s
                                o = ps[:, k % 4, j * P:(j + 1) * P]
                                gh, gl = (x[:, g * GB:(g + 1) * GB, :].rearrange("p b i -> p (b i)")
                                          for x in (gbh, gbl))
                                mm(o, th[:, c0:c0 + P], gh, start=True, stop=False)
                                mm(o, th[:, c0:c0 + P], gl, start=False, stop=False)
                                mm(o, tl[:, c0:c0 + P], gh, start=False, stop=False)
                                last = mm(o, base[:, c0:c0 + P], delta2h[:, :, :].rearrange("p b i -> p (b i)"),
                                          start=False, stop=True)
                            last.then_inc(mg_done, 1)

                    def up(c):
                        def stage_(g, pair, h):
                            q, hf, bl = NQ * g + HB * pair + h, h % 2, 2 * pair + h // 2
                            pe.wait_ge(z_copied, q + 1)
                            at_least(pe, h_ready[c], q)
                            at_least(pe, hhi_ready[c], q)
                            w = [x[:, bass.ds(bl * F + c * P, P)] for x in wm1]
                            mm(ps[:, c, :], w[0], zs[:, hf, 0, :], start=True, stop=False)
                            mm(ps[:, c, :], w[0], zs[:, hf, 1, :], start=False, stop=False)
                            mm(ps[:, c, :], w[1], zs[:, hf, 0, :], start=False, stop=True).then_inc(up_done[c], 1)
                        return stage_

                    def down(j):
                        def stage_(g, pair, h):
                            q, hf, bb = NQ * g + HB * pair + h, h % 2, h // 2
                            o = ps[:, 4 + hf, j * P:(j + 1) * P]
                            cols = slice(j * P, (j + 1) * P)
                            if j == 0:
                                if hf == 0:
                                    pe.wait_ge(w2_copied, GB * g + 2 * pair + bb + 1)
                                at_least(pe, n_ready, q - 1)
                            mm(o, zs[:, hf, 0, cols], ident_ws[:, :], start=True, stop=False)
                            mm(o, zs[:, hf, 1, cols], ident_ws[:, :], start=False, stop=False)
                            mm(o, ohb[:, bb, :], b2s[:, :], start=False, stop=False)
                            for c in range(FC):
                                if j == 0:
                                    pe.wait_ge(hlo_ready[c], q + 1)
                                hi, lo = hh[:, hf, c, cols], hl[:, hf, c, cols]
                                mm(o, hi, w2b[:, bb, 0, c, :], start=False, stop=False)
                                mm(o, hi, w2b[:, bb, 1, c, :], start=False, stop=False)
                                last = mm(o, lo, w2b[:, bb, 0, c, :], start=False, stop=(c == FC - 1))
                            if j == HALF - 1:
                                last.then_inc(f2_done, 1)
                        return stage_

                    def turn(g, pair, h):
                        q, hf = NQ * g + HB * pair + h, h % 2
                        pe.wait_ge(v_ready, q + 1)
                        at_least(pe, ob_ready, q)
                        for j in range(HALF):
                            last = nc.tensor.transpose(ps[:, 6 + hf, j * P:(j + 1) * P], rn[:, hf, j, :], ident)
                        last.then_inc(t_done, 1)

                    pe.wait_ge(base_placed, 16 * 4)
                    pe.wait_ge(gb_ready, 1)
                    merge(0, range(4))
                    merge_biases()
                    merge(0, range(4, NB_))
                    for g in range(NG):
                        pe.wait_ge(mlo_ready, NB_ * (g + 1))
                        run(pe, g, FFN_TENSOR_ORDER, {
                            **{f"up_{c}": up(c) for c in range(FC)}, **{f"down_{j}": down(j) for j in range(HALF)},
                            "turn": turn}, merge)

                @block.scalar
                def _(act):
                    def merged_hi(g, banks_):
                        for k in banks_:
                            kind, i = k // 8, k % 8
                            act.wait_ge(mg_done, NB_ * g + k + 1)
                            if g and k == 0:
                                for c in range(FC):
                                    act.wait_ge(up_done[c], NQ * g)
                                act.wait_ge(w2_copied, GB * g)
                            src, dst = merged_views(kind, i, 0)
                            nc.scalar.activation(dst, src, ACT.Copy).then_inc(mhi_ready, 1)

                    def hidden(c):
                        def stage_(g, pair, h):
                            q = NQ * g + HB * pair + h
                            if h % 2 == 0:
                                act.wait_ge(b1_ready, GB * g + 2 * pair + h // 2 + 1)
                            at_least(act, hlo_ready[c], q)
                            act.wait_ge(up_done[c], q + 1)
                            nc.scalar.activation(hf_[:, c, :], ps[:, c, :], ACT.Relu, bias=b1s[:, h // 2, c:c + 1],
                                                 scale=1.0 / WS).then_inc(h_ready[c], 1)
                        return stage_

                    def hidden_hi(c):
                        def stage_(g, pair, h):
                            q = NQ * g + HB * pair + h
                            if h % 2 == 0:
                                act.wait_ge(b1_ready, GB * g + 2 * pair + h // 2 + 1)
                            at_least(act, f2_done, q - 1)
                            act.wait_ge(up_done[c], q + 1)
                            nc.scalar.activation(hh[:, h % 2, c, :], ps[:, c, :], ACT.Relu,
                                                 bias=b1s[:, h // 2, c:c + 1], scale=1.0 / WS).then_inc(hhi_ready[c], 1)
                        return stage_

                    def normalise(g, pair, h):
                        q, hf = NQ * g + HB * pair + h, h % 2
                        act.wait_ge(fsh, q + 1)
                        at_least(act, t_done, q - 1)
                        for j in range(HALF):
                            last = nc.scalar.activation(rn[:, hf, j, :], ps[:, 4 + hf, j * P:(j + 1) * P], ACT.Identity,
                                                        bias=rr[:, hf, 1, j:j + 1], scale=rr[:, hf, 0, j:j + 1])
                        last.then_inc(n_ready, 1)

                    def finish(g, pair, h):
                        q, hf = NQ * g + HB * pair + h, h % 2
                        act.wait_ge(t_done, q + 1)
                        act.wait_ge(out_stored[hf], 16 * (GB * g + 2 * pair + h // 2 + 1))
                        nc.scalar.activation(ob[:, hf, :], ps[:, 6 + hf, :], ACT.Identity, bias=lnb[:, 0:1])\
                            .then_inc(ob_ready, 1)

                    merged_hi(0, range(NB_))
                    for g in range(NG):
                        run(act, g, FFN_SCALAR_ORDER, {
                            **{f"hidden_{c}": hidden(c) for c in range(FC)},
                            **{f"hidden_hi_{c}": hidden_hi(c) for c in range(FC)},
                            "normalise": normalise, "finish": finish}, merged_hi)

                @block.vector
                def _(dve):
                    n = [0]

                    def link(ins):
                        n[0] += 1
                        ins.then_inc(b_chain, 1)
                        dve.wait_ge(b_chain, n[0])

                    nc.vector.tensor_reduce(gsum[:, :], ghs[:, :].rearrange("p (b t) -> p b t", t=TILES), AX.X, ALU.add)\
                        .then_inc(gs_ready, 1)
                    link(nc.vector.memset(g9[:, :], 1.0))
                    dve.wait_ge(g_done, 1)
                    link(nc.vector.tensor_scalar(grep[:, :], ps[:, 4, 0:B], 1.0 / T, gf2brep[:, 0:1], ALU.mult, ALU.add))
                    nc.vector.tensor_scalar(g9[0:E, :], ps[0:E, 5, 0:B], 1.0 / T, gf2b[:, 0:1], ALU.mult, ALU.add)\
                        .then_inc(g9r, 1)
                    link(nc.vector.tensor_tensor(gbf[:, :, :], kcol("delta").unsqueeze(1).broadcast_to([P, B, FI]),
                                                 grep[:, :].unsqueeze(2).broadcast_to([P, B, FI]), ALU.mult))
                    link(nc.vector.tensor_copy(gbh[:, :, :], gbf[:, :, :]))
                    nc.vector.tensor_tensor(gbl[:, :, :], gbf[:, :, :], gbh[:, :, :], ALU.subtract).then_inc(gb_ready, 1)

                    def merged_biases():
                        dve.wait_ge(b12_done, 1)
                        dve.wait_ge(b2_cleared, 1)
                        nc.vector.tensor_copy(b1m[:, :, :], ps[:, 6, 0:FC * B].rearrange("p (c b) -> p c b", c=FC))
                        link(nc.vector.tensor_scalar(b2f[:, :], ps[0:B, 7, 0:C], WS, None, ALU.mult))
                        link(nc.vector.tensor_copy(b2s[0:B, :], b2f[:, :]))
                        link(nc.vector.tensor_tensor(b2s[32:32 + B, :], b2f[:, :], b2s[0:B, :], ALU.subtract))

                    def merged_lo(g, banks_):
                        for k in banks_:
                            kind, i = k // 8, k % 8
                            dve.wait_ge(mhi_ready, NB_ * g + k + 1)
                            src, hi = merged_views(kind, i, 0)
                            _, lo = merged_views(kind, i, 1)
                            nc.vector.tensor_tensor(lo, src, hi, ALU.subtract).then_inc(mlo_ready, 1)

                    def copy_z(g, pair, h):
                        q, hf, bb = NQ * g + HB * pair + h, h % 2, h // 2
                        b = GB * g + 2 * pair + bb
                        at_least(dve, f2_done, q - 1)
                        if hf == 0:
                            nc.vector.tensor_copy(b1s[:, bb, :], b1m[:, :, bass.ds(b, 1)].squeeze(2))\
                                .then_inc(b1_ready, 1)
                        for part, src in enumerate((zh, zl)):
                            last = nc.vector.tensor_copy(zs[:, hf, part, :], src[:, bass.ds(q * HALF * P, HALF * P)])
                        last.then_inc(z_copied, 1)

                    def copy_w2(g, pair, h):
                        if h % 2:
                            return
                        q, bb, bl = NQ * g + HB * pair + h, h // 2, 2 * pair + h // 2
                        at_least(dve, f2_done, q - 2)
                        nc.vector.tensor_copy(ohb[:, bb, :],
                                              onehoth[:, bass.ds(GB * g + bl, 1)].broadcast_to([64, P]))
                        for part in range(2):
                            last = nc.vector.tensor_copy(w2b[:, bb, part, :, :], wm2[part][:, :, bass.ds(bl * C, C)])
                        last.then_inc(w2_copied, 1)

                    def hidden_hi(c):
                        def stage_(g, pair, h):
                            q = NQ * g + HB * pair + h
                            at_least(dve, f2_done, q - 1)
                            dve.wait_ge(h_ready[c], q + 1)
                            nc.vector.tensor_copy(hh[:, h % 2, c, :], hf_[:, c, :]).then_inc(hhi_ready[c], 1)
                        return stage_

                    def hidden_lo(c):
                        def stage_(g, pair, h):
                            q = NQ * g + HB * pair + h
                            dve.wait_ge(h_ready[c], q + 1)
                            dve.wait_ge(hhi_ready[c], q + 1)
                            nc.vector.tensor_tensor(hl[:, h % 2, c, :], hf_[:, c, :], hh[:, h % 2, c, :], ALU.subtract)\
                                .then_inc(hlo_ready[c], 1)
                        return stage_

                    def stats(g, pair, h):
                        q, hf = NQ * g + HB * pair + h, h % 2
                        dve.wait_ge(f2_done, q + 1)
                        for j in range(HALF):
                            last = nc.vector.bn_stats(rs[:, hf, j, :], ps[:, 4 + hf, j * P:(j + 1) * P])
                        last.then_inc(fbn, 1)

                    def mean_var(g, pair, h):
                        q, hf = NQ * g + HB * pair + h, h % 2
                        dve.wait_ge(gs_ready, 1)
                        dve.wait_ge(fbn, q + 1)
                        for j in range(HALF):
                            last = nc.vector.bn_aggr(rmv[:, hf, j, :], rs[:, hf, j, :])
                        last.then_inc(fmv, 1)

                    def add_eps(g, pair, h):
                        q, hf = NQ * g + HB * pair + h, h % 2
                        dve.wait_ge(fmv, q + 1)
                        nc.vector.tensor_scalar(rr[:, hf, 2, :], rmv[:, hf, :, 1], EPS * WS * WS, None, ALU.add)\
                            .then_inc(fve, 1)

                    def shift(g, pair, h):
                        q, hf = NQ * g + HB * pair + h, h % 2
                        dve.wait_ge(frs, q + 1)
                        nc.vector.scalar_tensor_tensor(rr[:, hf, 1, :], rmv[:, hf, :, 0], -1.0, rr[:, hf, 0, :],
                                                       ALU.mult, ALU.mult).then_inc(fsh, 1)

                    def add_up(g, pair, h):
                        q, hf = NQ * g + HB * pair + h, h % 2
                        dve.wait_ge(gain_ready, q + 1)
                        dve.wait_ge(t1_loaded[hf], 16 * (GB * g + 2 * pair + h // 2 + 1))
                        nc.vector.tensor_tensor(rn[:, hf, :, :], rn[:, hf, :, :], t1b[:, hf, :, :], ALU.add)\
                            .then_inc(v_ready, 1)

                    merged_lo(0, range(4))
                    merged_biases()
                    merged_lo(0, range(4, NB_))
                    for g in range(NG):
                        dve.wait_ge(mlo_ready, NB_ * (g + 1))
                        run(dve, g, FFN_VECTOR_ORDER, {
                            "copy_z": copy_z, "copy_w2": copy_w2, "stats": stats, "mean_var": mean_var,
                            "add_eps": add_eps, "shift": shift, "add_up": add_up,
                            **{f"hidden_hi_{c}": hidden_hi(c) for c in range(FC)},
                            **{f"hidden_lo_{c}": hidden_lo(c) for c in range(FC)}}, merged_lo)

                @block.gpsimd
                def _(pool):
                    nc.gpsimd.memset(b2s[:, :], 0.0).then_inc(b2_cleared, 1)

                    def gain(g, pair, h):
                        q, hf = NQ * g + HB * pair + h, h % 2
                        pool.wait_ge(n_ready, q + 1)
                        nc.gpsimd.tensor_tensor(rn[:, hf, :, :], rn[:, hf, :, :],
                                                lng[:, :].unsqueeze(1).broadcast_to([P, HALF, C]), ALU.mult)\
                            .then_inc(gain_ready, 1)

                    def rsqrt(g, pair, h):
                        q, hf = NQ * g + HB * pair + h, h % 2
                        pool.wait_ge(fve, q + 1)
                        nc.gpsimd.tensor_tensor(rr[:, hf, 0, :], rr[:, hf, 2, :], kcol("mhalf"), ALU.pow).then_inc(frs, 1)

                    nc.gpsimd.memset(ob[:, 0, :], 0.0).then_inc(out_stored[0], 16)
                    nc.gpsimd.memset(ob[:, 1, :], 0.0).then_inc(out_stored[1], 16)
                    for g in range(NG):
                        run(pool, g, FFN_GPSIMD_ORDER, {"rsqrt": rsqrt, "gain": gain})


_INS = ["x", "L0_conv_width", "L0_conv_damp", "L1_attn_W_q", "L1_attn_W_k", "L1_attn_W_v", "L1_attn_W_out",
        "L1_ffn_gfc1_w", "L1_ffn_gfc1_b", "L1_ffn_gfc2_w", "L1_ffn_gfc2_b", "L1_ffn_W1", "L1_ffn_b1", "L1_ffn_W2",
        "L1_ffn_b2", "L1_ffn_ln_g", "L1_ffn_ln_b", "L1_ffn_tv_W1", "L1_ffn_tv_b1", "L1_ffn_tv_W2", "L1_ffn_tv_b2",
        "L1_ffn_tv_ln_g", "L1_ffn_tv_ln_b"]


def kernel(**inputs):
    import concourse.bacc as bacc
    from concourse.bass_utils import run_bass_kernel_spmd

    nc = bacc.Bacc("TRN2", target_bir_lowering=False, num_devices=1)
    arrays, aps = {}, {}
    for name in _INS:
        a = np.ascontiguousarray(inputs[name])
        if name == "x":
            a = a.reshape(B * C, T)
        if a.ndim == 0:
            a = a.reshape(1)
        arrays["in_" + name] = a
    arrays["in_consts"] = shape_constants()
    for name, a in arrays.items():
        aps[name[3:]] = nc.dram_tensor(name, a.shape, mybir.dt.from_np(a.dtype), kind="ExternalInput").ap()
    aps["t1"] = nc.dram_tensor("t1_rows", (NHALF * P, HALF * C), F32, kind="Internal").ap()
    aps["base_parts"] = nc.dram_tensor("base_parts", (2, 2, P, BW), F16, kind="Internal").ap()
    aps["out"] = nc.dram_tensor("out_0", (B * C, T), F32, kind="ExternalOutput").ap()
    build(nc, aps)
    r = run_bass_kernel_spmd(nc, [arrays], core_ids=[0])
    return r.results[0]["out_0"].reshape(B, C, 32, 32)
```
